# Optimizing a Trainium2 kernel written in Bass

```python
import numpy as np
import jax
import jax.numpy as jnp

def _softmax(x, axis=-1):
    return jax.nn.softmax(x, axis=axis)

def _gelu(x):
    return jax.nn.gelu(x, approximate=True)

def _silu(x):
    return jax.nn.silu(x)

def _sigmoid(x):
    return jax.nn.sigmoid(x)

def _layernorm(x, axis=-1, eps=1e-05):
    m = jnp.mean(x, axis=axis, keepdims=True)
    v = jnp.var(x, axis=axis, keepdims=True)
    return (x - m) / jnp.sqrt(v + eps)

def _scatter_add(tgt, idx, src, axis=0):
    return tgt.at[idx].add(src)

def _segment_sum(src, seg, n):
    return jax.ops.segment_sum(src, seg, n)
kernel_name = 'mk_audio_tower_d1_tok_audfeat512_r4_c4c472'

def setup_inputs(seed: int=0):
    np.random.seed(seed)
    _w = jnp.asarray

    def _rec_inputs():
        import jax
        import jax.numpy as jnp
        _rk = jax.random.key(seed)
        x = -3.53888e-05 + 1.00021 * jax.random.normal(jax.random.fold_in(_rk, 1), (32, 125, 23), jnp.float32)
        return x
    x = _rec_inputs()

    def _L0_tok_setup():
        import jax, jax.numpy as jnp
        import numpy as np
        CONTEXT = 5
        DILATION = 1
        BN_EPS = 1e-05

        def _tdnn_forward(x, W, b, gamma, beta):
            B, T, D = x.shape
            L = T - (CONTEXT - 1) * DILATION
            frames = jnp.stack([jax.lax.dynamic_slice_in_dim(x, k * DILATION, L, axis=1) for k in range(CONTEXT)], axis=2)
            patches = frames.reshape(B, L, CONTEXT * D)
            y = jnp.einsum('blf,of->blo', patches, W) + b
            y = jax.nn.relu(y)
            mean = jnp.mean(y, axis=(0, 1))
            var = jnp.var(y, axis=(0, 1))
            y = (y - mean) * jax.lax.rsqrt(var + BN_EPS) * gamma + beta
            return y
        key = jax.random.key(seed)
        k1, k2, k3 = jax.random.split(key, 3)
        B, T, D, O = (64, 1024, 23, 128)
        x = jax.random.normal(k1, (B, T, D), dtype=jnp.float32)
        fan_in = D * CONTEXT
        bound = 1.0 / np.sqrt(fan_in)
        W = jax.random.uniform(k2, (O, fan_in), dtype=jnp.float32, minval=-bound, maxval=bound)
        b = jax.random.uniform(k3, (O,), dtype=jnp.float32, minval=-bound, maxval=bound)
        gamma = jnp.ones((O,), dtype=jnp.float32)
        beta = jnp.zeros((O,), dtype=jnp.float32)
        return {'x': x, 'W': W, 'b': b, 'gamma': gamma, 'beta': beta}
    _L0_tok_all = _L0_tok_setup()
    _L0_tok_in = {k: v for k, v in _L0_tok_all.items() if k in ('W', 'b', 'gamma', 'beta')}
    del _L0_tok_all

    def _L0_attn_setup():
        import jax, jax.numpy as jnp
        import numpy as np
        B, N, D, H, E = (4, 512, 128, 8, 8192)
        HD = D // H

        def _edge_col_bias(edge_index, edge_attr, eb_w, eb_b, n):
            eb = edge_attr @ eb_w.T + eb_b
            src, tgt = (edge_index[0], edge_index[1])
            valid = (src >= 0) & (src < n) & (tgt >= 0) & (tgt < n)
            order = jnp.where(valid, jnp.arange(edge_index.shape[1]), -1)
            tgt_safe = jnp.where(valid, tgt, 0)
            last = jnp.full((n,), -1, dtype=order.dtype).at[tgt_safe].max(order)
            hit = last >= 0
            gathered = eb[jnp.maximum(last, 0)]
            col_bias = jnp.where(hit[:, None], gathered, 0.0)
            return col_bias
        key = jax.random.key(seed)
        ks = jax.random.split(key, 12)
        s = 0.02
        inp = {'x': jax.random.normal(ks[0], (B, N, D), dtype=jnp.float32), 'edge_index': jax.random.randint(ks[1], (2, E), 0, N, dtype=jnp.int64), 'edge_attr': jax.random.normal(ks[2], (E, 3), dtype=jnp.float32), 'q_w': jax.random.normal(ks[3], (D, D), dtype=jnp.float32) * s, 'q_b': jnp.zeros((D,), jnp.float32), 'k_w': jax.random.normal(ks[4], (D, D), dtype=jnp.float32) * s, 'k_b': jnp.zeros((D,), jnp.float32), 'v_w': jax.random.normal(ks[5], (D, D), dtype=jnp.float32) * s, 'v_b': jnp.zeros((D,), jnp.float32), 'o_w': jax.random.normal(ks[6], (D, D), dtype=jnp.float32) * s, 'o_b': jnp.zeros((D,), jnp.float32), 'eb_w': jax.random.normal(ks[7], (H, 3), dtype=jnp.float32) * s, 'eb_b': jnp.zeros((H,), jnp.float32)}
        return inp
    _L0_attn_all = _L0_attn_setup()
    _L0_attn_in = {k: v for k, v in _L0_attn_all.items() if k in ('edge_index', 'edge_attr', 'q_w', 'q_b', 'k_w', 'k_b', 'v_w', 'v_b', 'o_w', 'o_b', 'eb_w', 'eb_b')}
    del _L0_attn_all

    def _L0_ffn_setup():
        import jax, jax.numpy as jnp
        import numpy as np
        B, S, D = (8, 1024, 128)
        H = 512
        O = 128
        E = 8
        TOP_K = 1
        key = jax.random.key(seed)
        ks = jax.random.split(key, 8)
        sc = 0.02
        return {'x': jax.random.normal(ks[0], (B, S, D), dtype=jnp.float32), 'Wr': jax.random.normal(ks[1], (D, E), dtype=jnp.float32) * sc, 'br': jnp.zeros((E,), dtype=jnp.float32), 'W1': jax.random.normal(ks[2], (E, D, H), dtype=jnp.float32) * sc, 'b1': jnp.zeros((E, H), dtype=jnp.float32), 'W2': jax.random.normal(ks[3], (E, H, O), dtype=jnp.float32) * sc, 'b2': jnp.zeros((E, O), dtype=jnp.float32)}
    _L0_ffn_all = _L0_ffn_setup()
    _L0_ffn_in = {k: v for k, v in _L0_ffn_all.items() if k in ('Wr', 'br', 'W1', 'b1', 'W2', 'b2')}
    del _L0_ffn_all
    return {'x': x, 'L0_tok_W': _L0_tok_in['W'], 'L0_tok_b': _L0_tok_in['b'], 'L0_tok_gamma': _L0_tok_in['gamma'], 'L0_tok_beta': _L0_tok_in['beta'], 'L0_attn_edge_index': _L0_attn_in['edge_index'], 'L0_attn_edge_attr': _L0_attn_in['edge_attr'], 'L0_attn_q_w': _L0_attn_in['q_w'], 'L0_attn_q_b': _L0_attn_in['q_b'], 'L0_attn_k_w': _L0_attn_in['k_w'], 'L0_attn_k_b': _L0_attn_in['k_b'], 'L0_attn_v_w': _L0_attn_in['v_w'], 'L0_attn_v_b': _L0_attn_in['v_b'], 'L0_attn_o_w': _L0_attn_in['o_w'], 'L0_attn_o_b': _L0_attn_in['o_b'], 'L0_attn_eb_w': _L0_attn_in['eb_w'], 'L0_attn_eb_b': _L0_attn_in['eb_b'], 'L0_ffn_Wr': _L0_ffn_in['Wr'], 'L0_ffn_br': _L0_ffn_in['br'], 'L0_ffn_W1': _L0_ffn_in['W1'], 'L0_ffn_b1': _L0_ffn_in['b1'], 'L0_ffn_W2': _L0_ffn_in['W2'], 'L0_ffn_b2': _L0_ffn_in['b2']}

def reference(x, L0_tok_W, L0_tok_b, L0_tok_gamma, L0_tok_beta, L0_attn_edge_index, L0_attn_edge_attr, L0_attn_q_w, L0_attn_q_b, L0_attn_k_w, L0_attn_k_b, L0_attn_v_w, L0_attn_v_b, L0_attn_o_w, L0_attn_o_b, L0_attn_eb_w, L0_attn_eb_b, L0_ffn_Wr, L0_ffn_br, L0_ffn_W1, L0_ffn_b1, L0_ffn_W2, L0_ffn_b2):
    import jax
    import jax.numpy as jnp

    def _L0_tok_ref(x, W, b, gamma, beta):
        import jax, jax.numpy as jnp
        import numpy as np
        CONTEXT = 5
        DILATION = 1
        BN_EPS = 1e-05

        def _tdnn_forward(x, W, b, gamma, beta):
            B, T, D = x.shape
            L = T - (CONTEXT - 1) * DILATION
            frames = jnp.stack([jax.lax.dynamic_slice_in_dim(x, k * DILATION, L, axis=1) for k in range(CONTEXT)], axis=2)
            patches = frames.reshape(B, L, CONTEXT * D)
            y = jnp.einsum('blf,of->blo', patches, W) + b
            y = jax.nn.relu(y)
            mean = jnp.mean(y, axis=(0, 1))
            var = jnp.var(y, axis=(0, 1))
            y = (y - mean) * jax.lax.rsqrt(var + BN_EPS) * gamma + beta
            return y
        return _tdnn_forward(x, W, b, gamma, beta)

    def _L0_attn_ref(x, edge_index, edge_attr, q_w, q_b, k_w, k_b, v_w, v_b, o_w, o_b, eb_w, eb_b):
        import jax, jax.numpy as jnp
        import numpy as np
        B, N, D, H, E = (4, 512, 128, 8, 8192)
        HD = D // H

        def _edge_col_bias(edge_index, edge_attr, eb_w, eb_b, n):
            eb = edge_attr @ eb_w.T + eb_b
            src, tgt = (edge_index[0], edge_index[1])
            valid = (src >= 0) & (src < n) & (tgt >= 0) & (tgt < n)
            order = jnp.where(valid, jnp.arange(edge_index.shape[1]), -1)
            tgt_safe = jnp.where(valid, tgt, 0)
            last = jnp.full((n,), -1, dtype=order.dtype).at[tgt_safe].max(order)
            hit = last >= 0
            gathered = eb[jnp.maximum(last, 0)]
            col_bias = jnp.where(hit[:, None], gathered, 0.0)
            return col_bias
        b, n, d = x.shape
        q = (x @ q_w.T + q_b).reshape(b, n, H, HD)
        k = (x @ k_w.T + k_b).reshape(b, n, H, HD)
        v = (x @ v_w.T + v_b).reshape(b, n, H, HD)
        scores = jnp.einsum('bnhd,bmhd->bhnm', q, k) / jnp.sqrt(jnp.float32(HD))
        col_bias = _edge_col_bias(edge_index, edge_attr, eb_w, eb_b, n)
        scores = scores + col_bias.T[None, :, None, :]
        attn = jax.nn.softmax(scores, axis=-1)
        out = jnp.einsum('bhnm,bmhd->bnhd', attn, v).reshape(b, n, d)
        return out @ o_w.T + o_b

    def _L0_ffn_ref(x, Wr, br, W1, b1, W2, b2):
        import jax, jax.numpy as jnp
        import numpy as np
        B, S, D = (8, 1024, 128)
        H = 512
        O = 128
        E = 8
        TOP_K = 1
        b, s, d = x.shape
        xf = x.reshape(-1, d)
        router_logits = xf @ Wr + br
        topk_logits, topk_idx = jax.lax.top_k(router_logits, TOP_K)
        topk_gates = jax.nn.softmax(topk_logits, axis=1)
        out = jnp.zeros((xf.shape[0], O), dtype=x.dtype)
        for k in range(TOP_K):
            idx_k = topk_idx[:, k]
            gate_k = topk_gates[:, k:k + 1]
            for e in range(E):
                h = jax.nn.relu(xf @ W1[e] + b1[e])
                oe = h @ W2[e] + b2[e]
                mask = (idx_k == e)[:, None]
                out = out + jnp.where(mask, gate_k * oe, 0.0)
        return out.reshape(b, s, O)
    h = _L0_tok_ref(x, L0_tok_W, L0_tok_b, L0_tok_gamma, L0_tok_beta)
    h = h + _L0_attn_ref(_layernorm(h, axis=-1), L0_attn_edge_index, L0_attn_edge_attr, L0_attn_q_w, L0_attn_q_b, L0_attn_k_w, L0_attn_k_b, L0_attn_v_w, L0_attn_v_b, L0_attn_o_w, L0_attn_o_b, L0_attn_eb_w, L0_attn_eb_b)
    h = h + _L0_ffn_ref(_layernorm(h, axis=-1), L0_ffn_Wr, L0_ffn_br, L0_ffn_W1, L0_ffn_b1, L0_ffn_W2, L0_ffn_b2)
    return h

_drawn_inputs = setup_inputs


def setup_inputs(seed=0):
    import zlib

    import numpy as np

    out = dict(_drawn_inputs(seed))
    spreads = {'L0_tok_gamma': (1.0, 0.2),
     'L0_tok_beta': (0.0, 0.1),
     'L0_attn_q_b': (0.0, 0.8),
     'L0_attn_k_b': (0.0, 2.0),
     'L0_attn_v_b': (0.0, 0.316),
     'L0_attn_o_b': (0.0, 0.1),
     'L0_attn_eb_b': (0.0, 2.0),
     'L0_ffn_br': (0.0, 0.1),
     'L0_ffn_b1': (0.0, 0.285),
     'L0_ffn_b2': (0.0, 0.1)}
    factors = {'L0_attn_edge_attr': 8.0,
     'L0_attn_q_w': 8.0,
     'L0_attn_k_w': 8.0,
     'L0_attn_v_w': 6.192,
     'L0_attn_eb_w': 8.0}
    for name, (base, spread) in spreads.items():
        noise = np.random.default_rng([zlib.crc32(name.encode()), seed]).standard_normal(out[name].shape)
        drawn = base * np.exp(spread * noise) if base else spread * noise
        out[name] = jnp.asarray(drawn.astype(out[name].dtype))
    for name, factor in factors.items():
        out[name] = (out[name] * factor).astype(out[name].dtype)
    return out
```

```python
from contextlib import ExitStack

import numpy as np

import concourse.bass as bass
from concourse import mybir

F32 = mybir.dt.float32
BF16 = mybir.dt.bfloat16
I32 = mybir.dt.int32
ALU = mybir.AluOpType
ACT = mybir.ActivationFunctionType
AX = mybir.AxisListType

EPS = 1e-5
B, TF, DI = 32, 125, 23
CTX = 5
L = TF - CTX + 1
N = B * L
D = 128
H, HD = 8, 16
HB = 32
HG = 4
SEG = (L - 1) // 4
RUN = (SEG + CTX) * DI
CH = 4 * L
NCH = N // CH
PL = 2 * L
NP = B // 2
NEDGE = 8192
EC = 2048
E, F = 8, 512
FC = F // 128
NT = (N + E * 127) // 128
RING = 4
NOROW = 8192


def build(nc, x, tok_W, tok_b, gamma, beta, edge_index, edge_attr, q_w, q_b, k_w, k_b, v_w, v_b, o_w, o_b,
          eb_w, eb_b, Wr, br, W1, b1, W2, b2, out):
    with ExitStack() as ctx:
        def sb(name, shape, dt=F32):
            return ctx.enter_context(nc.sbuf_tensor(name, shape, dt))

        def sem(name):
            return ctx.enter_context(nc.semaphore(name))

        rows_d = nc.dram_tensor("rows_d", [N, 2 * D], F32, kind="Internal").ap()
        key_d = nc.dram_tensor("key_d", [128, NEDGE // 128], BF16, kind="Internal").ap()

        psS = ctx.enter_context(nc.psum_tensor("psS", [128, 2, 512], F32))
        psT = ctx.enter_context(nc.psum_tensor("psT", [128, 2, 512], F32))
        psO = ctx.enter_context(nc.psum_tensor("psO", [128, 512], F32))
        psU = ctx.enter_context(nc.psum_tensor("psU", [128, 512], F32))
        psB = ctx.enter_context(nc.psum_tensor("psB", [128, 2, 512], F32))
        banks = [psS[:, 0, :], psS[:, 1, :], psT[:, 0, :], psT[:, 1, :], psO[:, :], psU[:, :],
                 psB[:, 0, :], psB[:, 1, :]]

        ident = sb("ident", [128, 128])
        headmask = sb("headmask", [128, HG])
        before = sb("before", [128, 128], BF16)
        ones_bf = sb("ones_bf", [128, 128], BF16)
        ones_f = sb("ones_f", [128, E * B])
        slot_iota = sb("slot_iota", [128, 128])
        seq_iota = sb("seq_iota", [128, B])
        part1 = sb("part1", [128, 1])
        rank8 = sb("rank8", [128, E])
        tile_starts = sb("tile_starts", [128, B - 1])
        chunk_base = sb("chunk_base", [128, NEDGE // EC])
        minus_half = sb("minus_half", [128, 2])
        tokW_sb = sb("tokW_sb", [128, CTX * DI])
        tokWT = sb("tokWT", [128, 128])
        proj_in = sb("proj_in", [128, 4, D])
        qwT = sb("qwT", [128, H * HB])
        kwT = sb("kwT", [128, H * HB])
        vwT = sb("vwT", [128, D])
        owT = sb("owT", [128, D])
        qk_row = sb("qk_row", [1, 2, H * HB])
        qk_col = sb("qk_col", [128, 4])
        addK = sb("addK", [128, 2, L])
        col3 = sb("col3", [128, 3])
        ob_bc = sb("ob_bc", [128, D])
        vb_bc = sb("vb_bc", [128, D])
        br_bc = sb("br_bc", [128, E])
        ebw_bc = sb("ebw_bc", [128, 3 * H])
        ebb_bc = sb("ebb_bc", [128, H])
        Wr_sb = sb("Wr_sb", [128, E])
        W1_sb = sb("W1_sb", [128, E * F])
        W2_sb = sb("W2_sb", [128, E * F])
        countbc = sb("countbc", [128, E * F])
        b2_bc = sb("b2_bc", [128, E * D])
        xs = sb("xs", [128, RUN])
        patT = sb("patT", [128, N])
        yT = sb("yT", [128, N])
        bn_st = sb("bn_st", [128, NCH, 6])
        bn_mv = sb("bn_mv", [128, 2])
        bn_r = sb("bn_r", [128, 2])
        bn_ac = sb("bn_ac", [128, 2])
        edge_i = sb("edge_i", [128, 2, NEDGE // 128], I32)
        edge_f = sb("edge_f", [128, 2, NEDGE // 128])
        edge_c = sb("edge_c", [128, 2, NEDGE // 128])
        edge_v = sb("edge_v", [128, NEDGE // 128])
        key = sb("key", [128, NEDGE // 128], BF16)
        key_bc = W1_sb[:, :].bitcast(BF16)
        hit_order = W2_sb[:, 0:EC]
        order = W2_sb[:, EC:2 * EC]
        chunk_max = sb("chunk_max", [128, 3, NEDGE // EC])
        last = sb("last", [128, 3])
        last_i = sb("last_i", [128, 1], I32)
        attr = sb("attr", [128, 3])
        ebias = sb("ebias", [128, H])
        bias_pad = sb("bias_pad", [128, H * HB])
        h0T = sb("h0T", [128, PL])
        h0k = sb("h0k", [128, 2, D])
        st1 = sb("st1", [128, 2, 6])
        mv1 = sb("mv1", [128, 2, 2])
        var1 = sb("var1", [128, 2])
        rs1 = sb("rs1", [128, 2])
        nm1 = sb("nm1", [128, 2])
        xn = sb("xn", [128, 2, D])
        xT = sb("xT", [128, 2, PL])
        qT = sb("qT", [128, 2, 2, PL])
        kT = sb("kT", [128, 2, PL])
        kbd = patT[:, :].rearrange("p (s g n) -> p s g n", s=4, g=2)
        V = sb("V", [128, 2, 2, H, HD + 1])
        nmax = sb("nmax", [128, H])
        P = sb("P", [128, 2, H, L])
        PT = sb("PT", [128, 2, 2, HG * L])
        rden = sb("rden", [128, H])
        on = sb("on", [128, H, HD])
        oT = sb("oT", [128, L])
        st2 = sb("st2", [128, 6])
        mv2 = sb("mv2", [128, 2, 2])
        var2 = sb("var2", [128, 2])
        rs2 = sb("rs2", [128, 2])
        x2 = sb("x2", [128, 2, 2, D])
        res = sb("res", [128, B, D])
        x2T = sb("x2T", [128, PL])
        lg = sb("lg", [128, B, E])
        top = sb("top", [128, B])
        eq = sb("eq", [128, B, E])
        onehot = sb("onehot", [128, B, E])
        oh_bf = sb("oh_bf", [128, E, B], BF16)
        incl = sb("incl", [128, E, B])
        posE = sb("posE", [128, E, B])
        cnt = sb("cnt", [128, 6, E])
        cmpt = sb("cmpt", [128, E, B - 1])
        pos = sb("pos", [128, B])
        pos_i = sb("pos_i", [128, 3, B], I32)
        pos_f = sb("pos_f", [128, 2, B])
        onehots = yT[:, :].bitcast(BF16)
        slot1h = onehots[:, 0:B * 128].rearrange("p (b n) -> p b n", b=B)
        tile1h = onehots[:, B * 128:B * (128 + NT)].rearrange("p (b n) -> p b n", b=B)
        tok1h = onehots[:, B * (128 + NT):B * (128 + 3 * NT)].rearrange("p (b a n) -> p b a n", b=B, a=2)
        idf = sb("idf", [128, 2, NT])
        idg = sb("idg", [128, NT, 2])
        idx = sb("idx", [128, NT, 2], I32)
        eidc = sb("eidc", [128, NT, E])
        eidf = sb("eidf", [128, NT])
        eid = sb("eid", [128, NT], I32)
        xg = sb("xg", [128, RING, 2 * D])
        gidx = sb("gidx", [128, RING], I32)
        sidx = sb("sidx", [128, RING], I32)
        xgT = sb("xgT", [128, 2, 128])
        hpre = sb("hpre", [128, 2, F])
        hT = sb("hT", [128, 2, F])
        resid = sb("resid", [128, RING, D])
        y_out = sb("y_out", [128, RING, D])

        l_x, l_tokW, l_proj, l_edges, l_cols, l_rows, l_ffn, l_attr, l_qkb = map(
            sem, "l_x l_tokW l_proj l_edges l_cols l_rows l_ffn l_attr l_qkb".split())
        s_key_out, s_key_in = sem("s_key_out"), sem("s_key_in")
        s_const = sem("s_const")
        s_rowset = sem("s_rowset")
        a_wt, a_w4, a_xt, a_y, a_bias = map(sem, "a_wt a_w4 a_xt a_y a_bias".split())
        a_wts, a_pat_v, a_pat_s, a_relu, a_bst = map(sem, "a_wts a_pat_v a_pat_s a_relu a_bst".split())
        a_var, a_rstd, a_pool, a_ac = map(sem, "a_var a_rstd a_pool a_ac".split())
        a_chain, a_keyed, a_biasT, a_lasti, a_bpad, a_addk = map(
            sem, "a_chain a_keyed a_biasT a_lasti a_bpad a_addk".split())
        s_S, s_T, s_PV, s_U, s_P = map(sem, "s_S s_T s_PV s_U s_P".split())
        s_T1, s_T2, s_k, s_q, s_V, s_R1, s_R2 = map(sem, "s_T1 s_T2 s_k s_q s_V s_R1 s_R2".split())
        s_max, s_sub, s_rd, s_on, s_h1, s_st, s_ag, s_x2 = map(
            sem, "s_max s_sub s_rd s_on s_h1 s_st s_ag s_x2".split())
        s_kT, s_Vs, s_lg, s_st1, s_ag1 = map(sem, "s_kT s_Vs s_lg s_st1 s_ag1".split())
        s_exp, s_PT, s_oT, s_h0T, s_h0k, s_xT, s_qs, s_x2T = map(
            sem, "s_exp s_PT s_oT s_h0T s_h0k s_xT s_qs s_x2T".split())
        s_v1, s_r1, s_nm1, s_xn, s_h0b, s_kbd, s_v2, s_r2 = map(
            sem, "s_v1 s_r1 s_nm1 s_xn s_h0b s_kbd s_v2 s_r2".split())
        s_carry_p, s_carry_v = sem("s_carry_p"), sem("s_carry_v")
        d_x2, d_res = [sem("d_x2_0"), sem("d_x2_1")], sem("d_res")
        r_oh, r_cnt, r_1h, r_ids, r_idx, r_eid, r_chain = map(
            sem, "r_oh r_cnt r_1h r_ids r_idx r_eid r_chain".split())
        f_gat = [sem(f"f_gat{u}") for u in range(RING)]
        f_sca = [sem(f"f_sca{u}") for u in range(RING)]
        f_gi, f_si, f_Xt, f_xT, f_L1, f_hp, f_G, f_hT, f_L2, f_rs, f_y = map(
            sem, "f_gi f_si f_Xt f_xT f_L1 f_hp f_G f_hT f_L2 f_rs f_y".split())

        N_CONST = 21
        N_COLS, N_ROWS = 3, 7

        DRAIN = 6
        PEEL, TAIL = 2, 1

        def attention_steps(eng, step):
            for i in range(4 * PEEL):
                step(i // 4, i, i // 2, i % 4, i)
            with eng.Fori(PEEL, B // 4 - TAIL) as body:
                for u in range(4):
                    step(body, 4 * body + u, 2 * body + u // 2, u, None)
            for i in range(B - 4 * TAIL, B + DRAIN):
                step(i // 4, i, i // 2, i % 4, i)

        def ffn_steps(eng, step, end):
            for s in range(2 * RING):
                step(s, s // RING, s % RING, s)
            with eng.Fori(2, NT // RING - 1) as r:
                for u in range(RING):
                    step(RING * r + u, r, u, None)
            for s in range(RING * (NT // RING - 1), end):
                step(s, s // RING, s % RING, s)

        def has(t, back, n=B):
            return t is None or 0 <= t - back < n

        block = ctx.enter_context(nc.Block())

        @block.sync
        def _(sp):
            sp.dma_start(xs[:, :], bass.AP(x.tensor, 0, [[TF * DI, B], [SEG * DI, 4], [1, RUN]])).then_inc(l_x, 16)
            sp.dma_start(tokW_sb[:, :], tok_W).then_inc(l_tokW, 16)
            sp.dma_start(edge_i[:, :, :], edge_index.rearrange("a (p f) -> p a f", p=128)).then_inc(l_edges, 16)
            for n, w in enumerate((q_w, k_w, v_w, o_w)):
                sp.dma_start(proj_in[:, n, :], w).then_inc(l_proj, 16)
            for n, v in enumerate((tok_b, gamma, beta)):
                sp.dma_start(col3[:, n:n + 1], v.rearrange("(p a) -> p a", a=1)).then_inc(l_cols, 16)
            sp.wait_ge(s_rowset, 2)
            for n, v in enumerate((q_b, k_b)):
                sp.dma_start(qk_row[0:1, n, :].rearrange("p (h c) -> p h c", c=HB)[:, :, 0:HD],
                             v.rearrange("(a h c) -> a h c", a=1, c=HD)).then_inc(l_qkb, 16)
            sp.wait_ge(a_keyed, 1)
            sp.dma_start(key_d, key[:, :]).then_inc(s_key_out, 16)
            sp.wait_ge(s_key_out, 16)
            sp.dma_start(key_bc, key_d.rearrange("(a p) f -> a (p f)", a=1).partition_broadcast(128)
                         .rearrange("q a n -> q (a n)")).then_inc(s_key_in, 16)
            for t, v in ((ob_bc, o_b), (vb_bc, v_b), (br_bc, br), (ebb_bc, eb_b)):
                sp.dma_start(t[:, :], v.partition_broadcast(128)).then_inc(l_rows, 16)
            sp.dma_start(ebw_bc[:, :], eb_w.rearrange("h k -> (h k)").partition_broadcast(128)).then_inc(l_rows, 16)
            sp.dma_start(b2_bc[:, :], b2.rearrange("e d -> (e d)").partition_broadcast(128)).then_inc(l_rows, 16)
            sp.dma_start(Wr_sb[:, :], Wr).then_inc(l_rows, 16)
            sp.wait_ge(a_lasti, 1)
            sp.dma_start(W1_sb[:, :].rearrange("d (e f) -> d e f", e=E), W1.rearrange("e d f -> d e f")).then_inc(l_ffn, 16)
            sp.dma_start(W2_sb[:, :].rearrange("h (g o) -> h g o", o=D),
                         W2.rearrange("e (c h) o -> h (e c) o", h=128)).then_inc(l_ffn, 16)
            sp.dma_start(countbc[:, :], b1.rearrange("e f -> (e f)").partition_broadcast(128)).then_inc(l_ffn, 16)
            rows_v = rows_d.rearrange("(b n) d -> n b d", n=L)
            with sp.Fori(0, NP // 2) as r:
                for par in range(2):
                    b = 4 * r + 2 * par
                    sp.wait_ge(s_x2, b + 2)
                    sp.dma_start(rows_v[:, bass.ds(b, 2), 0:D], x2[0:L, par, :, :]).then_inc(d_x2[par], 16)
                    sp.dma_start(rows_v[:, bass.ds(b, 2), D:2 * D], res[0:L, bass.ds(b, 2), :]).then_inc(d_res, 16)

        @block.gpsimd
        def _(pool):
            pool.memset(qk_row[:, :, :], 0.0).then_inc(s_rowset, 1)
            pool.wait_ge(s_rowset, 1)
            pool.memset(qk_row[:, 0, :].rearrange("p (h c) -> p h c", c=HB)[:, :, HD:HD + 1], 4.0).then_inc(s_rowset, 1)
            pool.memset(ident[:, :], 0.0).then_inc(s_const, 1)
            pool.memset(headmask[:, :], 1.0).then_inc(s_const, 1)
            pool.memset(before[:, :], 1.0).then_inc(s_const, 1)
            pool.memset(ones_bf[:, :], 1.0).then_inc(s_const, 1)
            pool.memset(ones_f[:, :], 1.0).then_inc(s_const, 1)
            pool.memset(minus_half[:, :], -0.5).then_inc(s_const, 1)
            pool.memset(qwT[:, :], 0.0).then_inc(s_const, 1)
            pool.memset(kwT[:, :], 0.0).then_inc(s_const, 1)
            pool.memset(bias_pad[:, :], 0.0).then_inc(s_const, 1)
            pool.memset(V[:, :, :, :, :], 1.0).then_inc(s_const, 1)
            fl = dict(allow_small_or_imprecise_dtypes=True)
            pool.iota(slot_iota[:, :], pattern=[[1, 128]], base=0, channel_multiplier=0, **fl).then_inc(s_const, 1)
            pool.iota(seq_iota[:, :], pattern=[[1, B]], base=0, channel_multiplier=0, **fl).then_inc(s_const, 1)
            pool.iota(part1[:, :], pattern=[[0, 1]], base=1, channel_multiplier=1, **fl).then_inc(s_const, 1)
            pool.iota(rank8[:, :], pattern=[[-1, E]], base=E, channel_multiplier=0, **fl).then_inc(s_const, 1)
            pool.iota(tile_starts[:, :], pattern=[[128, B - 1]], base=0, channel_multiplier=0, **fl).then_inc(s_const, 1)
            pool.iota(chunk_base[:, :], pattern=[[EC, NEDGE // EC]], base=0, channel_multiplier=0, **fl).then_inc(s_const, 1)
            pool.wait_ge(s_const, 16)
            pool.affine_select(out=ident[:, :], in_=ident[:, :], compare_op=ALU.not_equal, fill=1.0, base=0,
                               pattern=[[-1, 128]], channel_multiplier=1).then_inc(s_const, 1)
            pool.affine_select(out=before[:, :], in_=before[:, :], compare_op=ALU.is_ge, fill=0.0, base=-1,
                               pattern=[[1, 128]], channel_multiplier=-1).then_inc(s_const, 1)
            pool.affine_select(out=headmask[:, :], in_=headmask[:, :], compare_op=ALU.is_ge, fill=0.0, base=0,
                               pattern=[[-HB, HG]], channel_multiplier=1).then_inc(s_const, 1)
            pool.wait_ge(s_const, 19)
            pool.affine_select(out=headmask[:, :], in_=headmask[:, :], compare_op=ALU.is_ge, fill=0.0, base=HB - 1,
                               pattern=[[HB, HG]], channel_multiplier=-1).then_inc(s_const, 1)
            pool.iota(order, pattern=[[1, EC]], base=1, channel_multiplier=0, **fl).then_inc(s_const, 1)

            pool.wait_ge(a_var, 1)
            pool.tensor_scalar(bn_r[:, 0:1], bn_mv[:, 1:2], 1.0, EPS, ALU.mult, ALU.add).then_inc(a_pool, 1)
            pool.wait_ge(a_pool, 1)
            pool.tensor_tensor(bn_r[:, 1:2], bn_r[:, 0:1], minus_half[:, 0:1], ALU.pow).then_inc(a_rstd, 1)
            pool.wait_ge(a_lasti, 1)
            pool.indirect_dma_start(attr[:, :], None, edge_attr, bass.IndirectOffsetOnAxis(last_i[:, 0:1], 0),
                                    bounds_check=NEDGE - 1, oob_is_err=False).then_inc(l_attr, 16)

            def norm1(p):
                pool.wait_ge(s_ag1, p + 1)
                pool.sem_inc(s_carry_p, 1)
                pool.tensor_scalar(var1[0:L, :], mv1[0:L, :, 1], 1.0, EPS, ALU.mult, ALU.add).then_inc(s_v1, 1)
                pool.wait_ge(s_v1, p + 1)
                pool.tensor_tensor(rs1[0:L, :], var1[0:L, :], minus_half[0:L, :], ALU.pow).then_inc(s_r1, 1)
                pool.wait_ge(s_r1, p + 1)
                pool.tensor_tensor(nm1[0:L, :], mv1[0:L, :, 0], rs1[0:L, :], ALU.mult).then_inc(s_nm1, 1)
                pool.wait_ge(s_nm1, 2 * p + 1)
                pool.sem_inc(s_carry_p, 1)
                pool.tensor_scalar(nm1[0:L, :], nm1[0:L, :], -1.0, 0.0, ALU.mult, ALU.add).then_inc(s_nm1, 1)
                pool.wait_ge(s_nm1, 2 * p + 2)
                if not (isinstance(p, int) and p == 0):
                    pool.wait_ge(s_T2, p)
                pool.sem_inc(s_carry_p, 1)
                for k in range(2):
                    pool.tensor_scalar(xn[0:L, k, :], h0k[0:L, k, :], rs1[0:L, k:k + 1], nm1[0:L, k:k + 1],
                                       ALU.mult, ALU.add).then_inc(s_xn, 1)
                pool.tensor_tensor(res[0:L, bass.ds(2 * p, 2), :], h0k[0:L, :, :],
                                   ob_bc[0:L, :].unsqueeze(1).to_broadcast([L, 2, D]), ALU.add).then_inc(s_h0b, 1)

            def key_blocks(p, slot):
                pool.wait_ge(s_kT, p + 1)
                for k in range(2):
                    if not (isinstance(p, int) and p < 2):
                        pool.wait_ge(s_S, 2 * p + k - 3)
                    pool.tensor_tensor(kbd[:, slot + k, :, :].rearrange("p g (j m) -> p g j m", m=L),
                                       kT[:, :, k * L:(k + 1) * L].unsqueeze(2).to_broadcast([128, 2, HG, L]),
                                       headmask[:, :].unsqueeze(1).unsqueeze(3).to_broadcast([128, 2, HG, L]),
                                       ALU.mult).then_inc(s_kbd, 1)

            def rstd2(b, par):
                pool.wait_ge(s_ag, b + 1)
                pool.sem_inc(s_carry_p, 1)
                pool.tensor_scalar(var2[0:L, par:par + 1], mv2[0:L, par, 1:2], 1.0, EPS, ALU.mult, ALU.add).then_inc(s_v2, 1)
                pool.wait_ge(s_v2, b + 1)
                pool.tensor_tensor(rs2[0:L, par:par + 1], var2[0:L, par:par + 1], minus_half[0:L, 0:1], ALU.pow).then_inc(s_r2, 1)

            pool.wait_ge(l_rows, 16 * N_ROWS)
            norm1(0)
            key_blocks(0, 0)
            norm1(1)
            key_blocks(1, 2)

            def step(r, i, p, u, t):
                if u % 2 == 1 and (t is None or p + 2 < NP):
                    norm1(p + 2)
                if has(t, 3):
                    rstd2(i - 3, (u + 1) % 2)
                if u % 2 == 1 and (t is None or p + 2 < NP):
                    key_blocks(p + 2, u // 2 * 2)

            attention_steps(pool, step)

            pool.wait_ge(d_res, 16 * NP)
            for par in range(2):
                pool.wait_ge(d_x2[par], 16 * (NP // 2))
            for s in range(RING):
                pool.wait_ge(r_idx, 1)
                pool.wait_ge(f_gi, s + 1)
                pool.indirect_dma_start(xg[:, s, :], None, rows_d, bass.IndirectOffsetOnAxis(gidx[:, s:s + 1], 0),
                                        bounds_check=N - 1, oob_is_err=False).then_inc(f_gat[s], 16)

            def step(s, r, u, t):
                if t is None or t + RING < NT:
                    pool.wait_ge(f_gi, s + RING + 1)
                    pool.wait_ge(f_rs, s + 1)
                    pool.sem_inc(s_carry_p, 1)
                    pool.indirect_dma_start(xg[:, u, :], None, rows_d, bass.IndirectOffsetOnAxis(gidx[:, u:u + 1], 0),
                                            bounds_check=N - 1, oob_is_err=False).then_inc(f_gat[u], 16)
                if t is None or t < NT:
                    pool.wait_ge(r_idx, 1)
                    pool.wait_ge(f_y, s + 1)
                    pool.sem_inc(s_carry_p, 1)
                    pool.indirect_dma_start(out, bass.IndirectOffsetOnAxis(sidx[:, u:u + 1], 0), y_out[:, u, :], None,
                                            bounds_check=N - 1, oob_is_err=False).then_inc(f_sca[u], 16)

            ffn_steps(pool, step, NT)
            for u in range(RING):
                pool.wait_ge(f_sca[u], 16 * len(range(u, NT, RING)))

        @block.scalar
        def _(act):
            def pat_copy(t):
                bank = banks[(3 + t) % 8]
                ni = min(4, SEG - 4 * t)
                dst = patT[0:CTX * DI, :].rearrange("p (b l) -> p b l", l=L)[:, :, 0:4 * SEG] \
                    .rearrange("p b (j i) -> p i b j", i=SEG)[:, 4 * t:4 * t + ni]
                src = bank[0:CTX * DI, 0:128 * ni].rearrange("p (i b j) -> p i b j", i=ni, j=4)
                return dst, src

            for t in range(1, 8, 2):
                act.wait_ge(a_xt, t + 1)
                dst, src = pat_copy(t)
                ins = act.activation(dst, src, ACT.Identity)
                if t < 7:
                    ins.then_inc(a_pat_s, 1)
            bank = banks[(3 + 7) % 8]
            act.activation(patT[0:CTX * DI, :].rearrange("p (b l) -> p b l", l=L)[:, :, L - 1],
                           bank[0:CTX * DI, 256:384].rearrange("p (b j) -> p b j", j=4)[:, :, 3],
                           ACT.Identity).then_inc(a_pat_s, 1)
            act.wait_ge(l_cols, 16 * N_COLS)
            for c in range(NCH):
                act.wait_ge(a_y, c + 1)
                act.activation(yT[:, c * CH:(c + 1) * CH], banks[(3 + c) % 8][:, 0:CH], ACT.Relu,
                               bias=col3[:, 0:1]).then_inc(a_relu, 1)

            def batch_norm(p):
                if not (isinstance(p, int) and p == 0):
                    act.wait_ge(s_T1, p)
                act.activation(h0T[:, :], yT[:, bass.ds(p * PL, PL)], ACT.Identity, bias=bn_ac[:, 1:2],
                               scale=bn_ac[:, 0:1]).then_inc(s_h0T, 1)

            def h0_copy(p, bank):
                act.wait_ge(s_T1, p + 1)
                if not (isinstance(p, int) and p == 0):
                    act.wait_ge(s_h0b, p)
                act.activation(h0k[0:L, :, :], psB[0:L, bank, 0:2 * D].rearrange("p (k d) -> p k d", k=2),
                               ACT.Identity).then_inc(s_h0k, 1)

            def xT_copy(p, par, bank):
                act.wait_ge(s_T2, p + 1)
                act.activation(xT[:, par, :], psB[:, bank, 0:PL], ACT.Identity).then_inc(s_xT, 1)

            def q_copy(p, par, bank):
                act.wait_ge(s_q, p + 1)
                for g in range(2):
                    act.activation(qT[:, par, g, :], psB[:, bank, g * PL:(g + 1) * PL], ACT.Identity,
                                   bias=qk_col[:, g:g + 1], scale=0.25).then_inc(s_qs, 1)

            act.wait_ge(a_ac, 1)
            act.wait_ge(a_wts, 7)
            batch_norm(0)
            h0_copy(0, 0)
            xT_copy(0, 0, 1)
            q_copy(0, 0, 1)
            batch_norm(1)
            h0_copy(1, 1)
            xT_copy(1, 1, 0)

            def step(r, i, p, u, t):
                par = u // 2
                even = u % 2 == 0
                if even and (t is None or p + 2 < NP):
                    batch_norm(p + 2)
                if even and (t is None or p + 1 < NP):
                    q_copy(p + 1, 1 - par, par)
                if has(t, 3):
                    act.wait_ge(s_U, i - 2)
                    act.activation(oT[:, :], psU[:, 0:L], ACT.Identity).then_inc(s_oT, 1)
                if has(t, 1):
                    act.wait_ge(s_T, i)
                    act.activation(PT[0:L, (u + 1) % 2, :, :], psT[0:L, :, 0:HG * L], ACT.Identity).then_inc(s_PT, 1)
                if even and (t is None or 0 <= p - 3 < NP):
                    act.wait_ge(s_R1, p - 2)
                    act.activation(x2T[:, :], psB[:, (1 + par) % 2, 0:PL], ACT.Identity).then_inc(s_x2T, 1)
                if not even and (t is None or p + 2 < NP):
                    xT_copy(p + 2, par, par)
                if has(t, 0):
                    act.wait_ge(s_sub, i + 1)
                    act.activation(P[0:L, u % 2, :, :], P[0:L, u % 2, :, :], ACT.Exp).then_inc(s_exp, 1)
                if even and (t is None or p + 2 < NP):
                    h0_copy(p + 2, par)

            attention_steps(act, step)

            def xgT_copy(s, u, t):
                act.wait_ge(f_Xt, s + 1)
                if t is None or t >= 2:
                    act.wait_ge(f_L1, s - 1)
                act.activation(xgT[:, u % 2, :], psB[:, u % 2, 0:128], ACT.Identity).then_inc(f_xT, 1)

            xgT_copy(0, 0, 0)

            def step(s, r, u, t):
                if t is None or t + 1 < NT:
                    xgT_copy(s + 1, u + 1, None if t is None else t + 1)
                if has(t, 1, NT):
                    act.wait_ge(f_G, s)
                    if t is None or t >= 3:
                        act.wait_ge(f_L2, s - 2)
                    act.activation(hT[:, (u + 1) % 2, :], psT[:, (u + 1) % 2, :], ACT.Relu).then_inc(f_hT, 1)

            ffn_steps(act, step, NT + 1)

        @block.vector
        def _(dve):
            links = [0]

            def link(ins, chain=a_chain, count=links):
                count[0] += 1
                ins.then_inc(chain, 1)
                dve.wait_ge(chain, count[0])

            dve.wait_ge(l_edges, 16)
            dve.wait_ge(s_const, N_CONST)
            link(dve.tensor_copy(edge_f[:, :, :], edge_i[:, :, :]))
            link(dve.tensor_scalar(edge_c[:, :, :], edge_f[:, :, :], 0.0, float(L - 1), ALU.max, ALU.min))
            link(dve.tensor_tensor(edge_c[:, :, :], edge_c[:, :, :], edge_f[:, :, :], ALU.is_equal))
            link(dve.tensor_tensor(edge_v[:, :], edge_c[:, 0, :], edge_c[:, 1, :], ALU.mult))
            dve.scalar_tensor_tensor(out=key[:, :], in0=edge_f[:, 1, :], scalar=1.0, in1=edge_v[:, :],
                                     op0=ALU.add, op1=ALU.mult).then_inc(a_keyed, 1)
            dve.wait_ge(a_wt, 1)
            dve.tensor_copy(tokWT[0:CTX * DI, :], banks[0][0:CTX * DI, 0:128]).then_inc(a_wts, 1)
            dve.wait_ge(a_w4, 1)
            for n, w in enumerate((qwT, kwT)):
                dve.tensor_copy(w[:, :].rearrange("p (h c) -> p h c", c=HB)[:, :, 0:HD],
                                banks[1][:, n * D:(n + 1) * D].rearrange("p (h c) -> p h c", c=HD)).then_inc(a_wts, 1)
            dve.tensor_copy(vwT[:, :], banks[1][:, 2 * D:3 * D]).then_inc(a_wts, 1)
            dve.tensor_copy(owT[:, :], banks[1][:, 3 * D:4 * D]).then_inc(a_wts, 1)
            dve.wait_ge(a_bias, 1)
            dve.tensor_scalar(qk_col[:, 0:2], banks[2][:, 0:2], 0.25, None, ALU.mult).then_inc(a_wts, 1)
            dve.tensor_copy(qk_col[:, 2:4], banks[2][:, 2:4]).then_inc(a_wts, 1)
            for t in range(0, 8, 2):
                dve.wait_ge(a_xt, t + 1)
                bank = banks[(3 + t) % 8]
                dst = patT[0:CTX * DI, :].rearrange("p (b l) -> p b l", l=L)[:, :, 0:4 * SEG] \
                    .rearrange("p b (j i) -> p i b j", i=SEG)[:, 4 * t:4 * t + 4]
                dve.tensor_copy(dst, bank[0:CTX * DI, 0:512].rearrange("p (i b j) -> p i b j", i=4, j=4)) \
                   .then_inc(a_pat_v, 1)
            for c in range(NCH):
                dve.wait_ge(a_relu, c + 1)
                dve.bn_stats(bn_st[:, c, :], yT[:, c * CH:(c + 1) * CH]).then_inc(a_bst, 1)
            dve.wait_ge(a_bst, NCH)
            dve.bn_aggr(bn_mv[:, :], bn_st[:, :, :].rearrange("p a b -> p (a b)")).then_inc(a_var, 1)
            dve.wait_ge(s_key_in, 16)
            for c in range(NEDGE // EC):
                link(dve.scalar_tensor_tensor(out=hit_order, in0=key_bc[:, c * EC:(c + 1) * EC], scalar=part1[:, 0:1],
                                              in1=order, op0=ALU.is_equal, op1=ALU.mult))
                link(dve.tensor_reduce(chunk_max[:, 0, c:c + 1], hit_order, AX.X, ALU.max))
                if c == 0:
                    dve.wait_ge(a_rstd, 1)
                    dve.wait_ge(l_cols, 16 * N_COLS)
                    link(dve.tensor_tensor(bn_ac[:, 0:1], bn_r[:, 1:2], col3[:, 1:2], ALU.mult))
                    link(dve.tensor_tensor(bn_r[:, 0:1], bn_mv[:, 0:1], bn_ac[:, 0:1], ALU.mult))
                    dve.tensor_tensor(bn_ac[:, 1:2], col3[:, 2:3], bn_r[:, 0:1], ALU.subtract).then_inc(a_ac, 1)
            link(dve.tensor_scalar(chunk_max[:, 1, :], chunk_max[:, 0, :], 0.0, None, ALU.is_gt))
            link(dve.tensor_tensor(chunk_max[:, 2, :], chunk_max[:, 0, :], chunk_base[:, :], ALU.add))
            link(dve.tensor_tensor(chunk_max[:, 2, :], chunk_max[:, 2, :], chunk_max[:, 1, :], ALU.mult))
            link(dve.tensor_reduce(last[:, 0:1], chunk_max[:, 2, :], AX.X, ALU.max))
            link(dve.tensor_scalar(last[:, 1:2], last[:, 0:1], 0.0, None, ALU.is_gt))
            dve.tensor_scalar(last_i[:, :], last[:, 0:1], -1.0, 0.0, ALU.add, ALU.max).then_inc(a_lasti, 1)
            dve.wait_ge(l_attr, 16)
            dve.wait_ge(l_rows, 16 * N_ROWS)
            for n in range(3):
                link(dve.scalar_tensor_tensor(
                    out=ebias[:, :], in0=ebw_bc[:, :].rearrange("p (h k) -> p h k", k=3)[:, :, n],
                    scalar=attr[:, n:n + 1], in1=(ebb_bc if n == 0 else ebias)[:, :], op0=ALU.mult, op1=ALU.add))
            dve.tensor_scalar(bias_pad[:, :].rearrange("p (h c) -> p h c", c=HB)[:, :, HD], ebias[:, :],
                              last[:, 1:2], None, ALU.mult).then_inc(a_bpad, 1)
            dve.wait_ge(a_biasT, 1)
            for g in range(2):
                ins = dve.tensor_scalar(addK[:, g, :], banks[5][:, g * 128:g * 128 + L], qk_col[:, 2 + g:3 + g], None, ALU.add)
            ins.then_inc(a_addk, 1)
            dve.wait_ge(a_addk, 1)

            def stats1(p):
                dve.wait_ge(s_h0k, p + 1)
                if not (isinstance(p, int) and p == 0):
                    dve.wait_ge(s_nm1, 2 * p)
                for k in range(2):
                    dve.bn_stats(st1[0:L, k, :], h0k[0:L, k, :]).then_inc(s_st1, 1)
                dve.wait_ge(s_st1, 2 * p + 2)
                if not (isinstance(p, int) and p == 0):
                    dve.wait_ge(s_xn, 2 * p)
                dve.sem_inc(s_carry_v, 1)
                for k in range(2):
                    ins = dve.bn_aggr(mv1[0:L, k, :], st1[0:L, k, :])
                ins.then_inc(s_ag1, 1)

            def k_copy(p, bank):
                dve.wait_ge(s_k, p + 1)
                if not (isinstance(p, int) and p == 0):
                    dve.wait_ge(s_kbd, 2 * p)
                dve.tensor_tensor(kT[:, :, :].rearrange("p g (k m) -> p g k m", m=L),
                                  psB[:, bank, 0:2 * PL].rearrange("p (g k m) -> p g k m", g=2, m=L),
                                  addK[:, :, :].unsqueeze(2).to_broadcast([128, 2, 2, L]), ALU.add).then_inc(s_kT, 1)

            def v_copy(p, par, bank):
                dve.wait_ge(s_V, p + 1)
                for k in range(2):
                    ins = dve.tensor_tensor(V[0:L, par, k, :, 0:HD],
                                            psB[0:L, bank, k * D:(k + 1) * D].rearrange("p (h c) -> p h c", c=HD),
                                            vb_bc[0:L, :].rearrange("p (h c) -> p h c", c=HD), ALU.add)
                ins.then_inc(s_Vs, 1)

            stats1(0)
            k_copy(0, 0)
            v_copy(0, 0, 0)
            stats1(1)
            k_copy(1, 1)

            def step(r, i, p, u, t):
                par = u // 2
                even = u % 2 == 0
                if not even and (t is None or p + 2 < NP):
                    stats1(p + 2)
                if has(t, 0):
                    dve.wait_ge(s_S, i + 1)
                    dve.tensor_reduce(nmax[0:L, :], psS[0:L, :, 0:HG * L].rearrange("p g (j m) -> p g j m", m=L),
                                      AX.X, ALU.max, negate=True).then_inc(s_max, 1)
                    dve.wait_ge(s_max, i + 1)
                    dve.tensor_tensor(P[0:L, u % 2, :, :].rearrange("p (g j) m -> p g j m", g=2),
                                      psS[0:L, :, 0:HG * L].rearrange("p g (j m) -> p g j m", m=L),
                                      nmax[0:L, :].rearrange("p (g j) -> p g j", g=2).unsqueeze(3)
                                      .to_broadcast([L, 2, HG, L]), ALU.add).then_inc(s_sub, 1)
                if not even and (t is None or 0 <= p - 3 < NP):
                    dve.wait_ge(s_R2, p - 2)
                    dve.tensor_tensor(lg[0:L, bass.ds(2 * (p - 3), 2), :],
                                      psB[0:L, (3 + par) % 2, 0:2 * E].rearrange("p (k e) -> p k e", k=2),
                                      br_bc[0:L, :].unsqueeze(1).to_broadcast([L, 2, E]), ALU.add).then_inc(s_lg, 1)
                if has(t, 2):
                    dve.wait_ge(s_PV, i - 1)
                    pv = psO[0:L, 0:H * (HD + 1)].rearrange("p (h c) -> p h c", c=HD + 1)
                    dve.reciprocal(rden[0:L, :], pv[:, :, HD]).then_inc(s_rd, 1)
                    dve.wait_ge(s_rd, i - 1)
                    dve.tensor_tensor(on[0:L, :, :], pv[:, :, 0:HD],
                                      rden[0:L, :].unsqueeze(2).to_broadcast([L, H, HD]), ALU.mult).then_inc(s_on, 1)
                if has(t, 3):
                    b = i - 3
                    dve.wait_ge(s_P, b + 1)
                    h1 = res[0:L, bass.ds(b, 1), :].rearrange("p a d -> p (a d)")
                    dve.tensor_tensor(h1, psU[0:L, 128:256], h1, ALU.add).then_inc(s_h1, 1)
                    dve.wait_ge(s_h1, b + 1)
                    dve.sem_inc(s_carry_v, 1)
                    dve.bn_stats(st2[0:L, :], h1).then_inc(s_st, 1)
                    dve.wait_ge(s_st, b + 1)
                    dve.sem_inc(s_carry_v, 1)
                    dve.bn_aggr(mv2[0:L, (u + 1) % 2, :], st2[0:L, :]).then_inc(s_ag, 1)
                if has(t, 4):
                    b = i - 4
                    dve.wait_ge(s_r2, b + 1)
                    if u % 2 == 0 and (t is None or b >= 4):
                        dve.wait_ge(s_R1, p - 3)
                        dve.wait_ge(d_x2[par], 16 * (r - 1))
                    dve.tensor_scalar(x2[0:L, par, u % 2, :], res[0:L, bass.ds(b, 1), :].rearrange("p a d -> p (a d)"),
                                      mv2[0:L, u % 2, 0:1], rs2[0:L, u % 2:u % 2 + 1],
                                      ALU.subtract, ALU.mult).then_inc(s_x2, 1)
                if not even and (t is None or p + 2 < NP):
                    k_copy(p + 2, (5 + par) % 2)
                if not even and (t is None or p + 1 < NP):
                    v_copy(p + 1, 1 - par, par)

            attention_steps(dve, step)

            rl = [0]

            def rlink(ins):
                link(ins, r_chain, rl)

            def bc(ap, shape):
                return ap.to_broadcast([L] + shape)

            dve.wait_ge(s_lg, NP)
            rlink(dve.tensor_reduce(top[0:L, :], lg[0:L, :, :], AX.X, ALU.max))
            rlink(dve.tensor_tensor(eq[0:L, :, :], lg[0:L, :, :], bc(top[0:L, :].unsqueeze(2), [B, E]), ALU.is_equal))
            rlink(dve.tensor_tensor(eq[0:L, :, :], eq[0:L, :, :], bc(rank8[0:L, :].unsqueeze(1), [B, E]), ALU.mult))
            rlink(dve.tensor_reduce(top[0:L, :], eq[0:L, :, :], AX.X, ALU.max))
            rlink(dve.tensor_tensor(onehot[0:L, :, :], bc(rank8[0:L, :].unsqueeze(1), [B, E]),
                                    bc(top[0:L, :].unsqueeze(2), [B, E]), ALU.is_equal))
            dve.tensor_copy(oh_bf[0:L, :, :], onehot[0:L, :, :].rearrange("p b e -> p e b")).then_inc(r_oh, 1)
            dve.wait_ge(r_cnt, 1)
            cum = psS[0:L, 0, 0:E * B].rearrange("p (e b) -> p e b", e=E)
            tot = psS[0:L, 1, 0:E * B].rearrange("p (e b) -> p e b", e=E)
            rlink(dve.tensor_tensor_scan(incl[0:L, :, :].rearrange("p e b -> p (e b)"), ones_f[0:L, :],
                                         psS[0:L, 1, 0:E * B], 0.0, ALU.mult, ALU.add))
            ends, ne, tiles, tinc, off, nexc = (cnt[0:L, n, :] for n in range(6))
            rlink(dve.tensor_copy(ends, incl[0:L, :, B - 1]))
            rlink(dve.tensor_copy(ne, ends))
            rlink(dve.tensor_tensor(ne[:, 1:E], ends[:, 1:E], ends[:, 0:E - 1], ALU.subtract))
            rlink(dve.tensor_tensor(cmpt[0:L, :, :], bc(ne.unsqueeze(2), [E, B - 1]),
                                    bc(tile_starts[0:L, :].unsqueeze(1), [E, B - 1]), ALU.is_gt))
            rlink(dve.tensor_reduce(tiles, cmpt[0:L, :, :], AX.X, ALU.add))
            rlink(dve.tensor_tensor_scan(tinc, ones_f[0:L, 0:E], tiles, 0.0, ALU.mult, ALU.add))
            rlink(dve.tensor_tensor(nexc, ends, ne, ALU.subtract))
            rlink(dve.tensor_tensor(off, tinc, tiles, ALU.subtract))
            rlink(dve.scalar_tensor_tensor(out=off, in0=off, scalar=128.0, in1=nexc, op0=ALU.mult, op1=ALU.subtract))
            rlink(dve.tensor_tensor(posE[0:L, :, :], incl[0:L, :, :], tot, ALU.subtract))
            rlink(dve.tensor_tensor(posE[0:L, :, :], posE[0:L, :, :], cum, ALU.add))
            rlink(dve.tensor_tensor(posE[0:L, :, :], posE[0:L, :, :], bc(off.unsqueeze(2), [E, B]), ALU.add))
            rlink(dve.tensor_tensor(posE[0:L, :, :], posE[0:L, :, :], onehot[0:L, :, :].rearrange("p b e -> p e b"), ALU.mult))
            rlink(dve.tensor_reduce(pos[0:L, :], posE[0:L, :, :].rearrange("p e b -> p b e"), AX.X, ALU.add))
            rlink(dve.tensor_copy(pos_i[0:L, 0, :], pos[0:L, :]))
            rlink(dve.tensor_scalar(pos_i[0:L, 1, :], pos_i[0:L, 0, :], 7, None, ALU.arith_shift_right))
            rlink(dve.tensor_scalar(pos_i[0:L, 2, :], pos_i[0:L, 0, :], 127, None, ALU.bitwise_and))
            rlink(dve.tensor_copy(pos_f[0:L, :, :], pos_i[0:L, 1:3, :]))
            rlink(dve.tensor_tensor(tile1h[0:L, :, :], bc(slot_iota[0:L, 0:NT].unsqueeze(1), [B, NT]),
                                    bc(pos_f[0:L, 0, :].unsqueeze(2), [B, NT]), ALU.is_equal))
            rlink(dve.tensor_scalar(tok1h[0:L, :, 0, :], tile1h[0:L, :, :], part1[0:L, 0:1], None, ALU.mult))
            rlink(dve.tensor_tensor(tok1h[0:L, :, 1, :], tile1h[0:L, :, :], bc(seq_iota[0:L, :].unsqueeze(2), [B, NT]), ALU.mult))
            QB = B // 4
            for q in range(4):
                b0 = q * QB
                dve.tensor_tensor(slot1h[0:L, b0:b0 + QB, :], bc(slot_iota[0:L, :].unsqueeze(1), [QB, 128]),
                                  bc(pos_f[0:L, 1, b0:b0 + QB].unsqueeze(2), [QB, 128]), ALU.is_equal).then_inc(r_1h, 1)
            rlink(dve.tensor_tensor(eidc[0:L, :, :], bc(tinc.unsqueeze(1), [NT, E]),
                                    bc(slot_iota[0:L, 0:NT].unsqueeze(2), [NT, E]), ALU.is_le))
            rlink(dve.tensor_reduce(eidf[0:L, :], eidc[0:L, :, :], AX.X, ALU.add))
            dve.tensor_scalar(eid[0:L, :], eidf[0:L, :], float(E - 1), None, ALU.min).then_inc(r_eid, 1)
            dve.wait_ge(r_ids, 1)
            rlink(dve.tensor_copy(idf[:, :, :], psO[:, 0:2 * NT].rearrange("p (a t) -> p a t", a=2)))
            rlink(dve.scalar_tensor_tensor(out=idg[:, :, 1], in0=idf[:, 1, :], scalar=float(L), in1=idf[:, 0, :],
                                           op0=ALU.mult, op1=ALU.add))
            rlink(dve.tensor_scalar(idf[:, 0, :], idf[:, 0, :], 0.0, float(NOROW), ALU.is_equal, ALU.mult))
            rlink(dve.scalar_tensor_tensor(out=idg[:, :, 1], in0=idg[:, :, 1], scalar=-1.0, in1=idf[:, 0, :],
                                           op0=ALU.add, op1=ALU.add))
            rlink(dve.tensor_scalar(idg[:, :, 0], idg[:, :, 1], float(N - 1), None, ALU.min))
            dve.tensor_copy(idx[:, :, :], idg[:, :, :]).then_inc(r_idx, 1)
            dve.wait_ge(r_idx, 1)

            def gather_rows(s, u):
                dve.tensor_copy(gidx[:, u:u + 1], idx[:, bass.ds(s, 1), 0]).then_inc(f_gi, 1)

            for s in range(RING):
                gather_rows(s, s)
            dve.wait_ge(r_eid, 1)
            dve.wait_ge(l_ffn, 48)

            def step(s, r, u, t):
                if t is None or t < NT:
                    e = dve.value_load(eid[0:1, bass.ds(s, 1)], min_val=0, max_val=E - 1)
                    dve.wait_ge(f_L1, s + 1)
                    if t is None or t >= 2:
                        dve.wait_ge(f_G, s - 1)
                    dve.tensor_tensor(hpre[:, u % 2, :], psS[:, u % 2, :], countbc[:, bass.ds(e * F, F)],
                                      ALU.add).then_inc(f_hp, 1)
                    if t is None or t + RING < NT:
                        gather_rows(s + RING, u)
                    dve.tensor_tensor(resid[:, u, :], xg[:, u, D:2 * D], b2_bc[:, bass.ds(e * D, D)],
                                      ALU.add).then_inc(f_rs, 1)
                if has(t, 2, NT):
                    v = (u + 2) % RING
                    if t is None or t - 2 >= RING:
                        dve.wait_ge(f_sca[v], 16 * (r + (u - 2) // RING))
                    dve.tensor_copy(sidx[:, v:v + 1], idx[:, bass.ds(s - 2, 1), 1]).then_inc(f_si, 1)
                    dve.wait_ge(f_L2, s - 1)
                    dve.wait_ge(f_rs, s - 1)
                    dve.wait_ge(f_si, s - 1)
                    dve.tensor_tensor(y_out[:, v, :], (psO if u % 2 == 0 else psU)[:, 0:D], resid[:, v, :],
                                      ALU.add).then_inc(f_y, 1)

            ffn_steps(dve, step, NT + 2)

        @block.tensor
        def _(pe):
            pe.wait_ge(s_const, N_CONST)
            pe.wait_ge(l_tokW, 16)
            pe.transpose(banks[0][0:CTX * DI, 0:128], tokW_sb[:, :], ident[:, :]).then_inc(a_wt, 1)
            pe.wait_ge(l_proj, 64)
            for n in range(4):
                ins = pe.transpose(banks[1][:, n * D:(n + 1) * D], proj_in[:, n, :], ident[:, :])
            ins.then_inc(a_w4, 1)
            pe.wait_ge(l_qkb, 32)
            for n in range(4):
                ins = pe.matmul(banks[2][:, n:n + 1], qk_row[0:1, n // 2, n % 2 * 128:n % 2 * 128 + 128],
                                ident[0:1, 0:1], start=True, stop=True)
            ins.then_inc(a_bias, 1)
            pe.wait_ge(l_x, 16)
            for t in range(8):
                bank = banks[(3 + t) % 8]
                if t >= 5:
                    pe.wait_ge(a_wts, (1, 5, 7)[t - 5])
                for i in range(4 * t, min(4 * t + 4, SEG + 1)):
                    ins = pe.transpose(bank[0:CTX * DI, (i - 4 * t) * 128:(i - 4 * t + 1) * 128],
                                       xs[:, i * DI:(i + CTX) * DI], ident[:, :])
                ins.then_inc(a_xt, 1)
            pe.wait_ge(a_pat_v, 4)
            pe.wait_ge(a_pat_s, 4)
            for c in range(NCH):
                pe.matmul(banks[(3 + c) % 8][:, 0:CH], tokWT[0:CTX * DI, :], patT[0:CTX * DI, c * CH:(c + 1) * CH],
                          start=True, stop=True).then_inc(a_y, 1)
            pe.wait_ge(a_bpad, 1)
            pe.wait_ge(a_relu, NCH)
            for g in range(2):
                ins = pe.transpose(banks[5][:, g * 128:g * 128 + L], bias_pad[0:L, g * 128:(g + 1) * 128], ident[0:L, 0:L])
            ins.then_inc(a_biasT, 1)

            def transpose_h0(p, bank):
                pe.wait_ge(s_h0T, p + 1)
                for k in range(2):
                    ins = pe.transpose(psB[0:L, bank, k * D:(k + 1) * D], h0T[:, k * L:(k + 1) * L], ident[:, :])
                ins.then_inc(s_T1, 1)

            def transpose_xn(p, bank):
                pe.wait_ge(s_xn, 2 * p + 2)
                for k in range(2):
                    ins = pe.transpose(psB[:, bank, k * L:(k + 1) * L], xn[0:L, k, :], ident[0:L, 0:L])
                ins.then_inc(s_T2, 1)

            def project(p, par, bank, w, done):
                pe.wait_ge(s_xT, p + 1)
                for g in range(2):
                    ins = pe.matmul(psB[:, bank, g * PL:(g + 1) * PL], w[:, g * 128:(g + 1) * 128], xT[:, par, :],
                                    start=True, stop=True)
                ins.then_inc(done, 1)

            def values(p, par, bank):
                for k in range(2):
                    ins = pe.matmul(psB[0:L, bank, k * D:(k + 1) * D], xT[:, par, k * L:(k + 1) * L], vwT[:, :],
                                    start=True, stop=True)
                ins.then_inc(s_V, 1)

            transpose_h0(0, 0)
            transpose_xn(0, 1)
            project(0, 0, 0, kwT, s_k)
            project(0, 0, 1, qwT, s_q)
            pe.wait_ge(s_kT, 1)
            values(0, 0, 0)
            pe.wait_ge(s_qs, 2)
            transpose_h0(1, 1)
            pe.wait_ge(s_Vs, 1)
            transpose_xn(1, 0)
            project(1, 1, 1, kwT, s_k)

            def step(r, i, p, u, t):
                par = u // 2
                even = u % 2 == 0
                if has(t, 0):
                    pe.wait_ge(s_kbd, i + 1)
                    if even:
                        pe.wait_ge(s_qs, 2 * p + 2)
                    if t is None or t >= 1:
                        pe.wait_ge(s_sub, i)
                    for g in range(2):
                        ins = pe.matmul(psS[0:L, g, 0:HG * L], qT[:, par, g, u % 2 * L:u % 2 * L + L],
                                        kbd[:, u, g, :], start=True, stop=True)
                    ins.then_inc(s_S, 1)
                if even and (t is None or p + 1 < NP):
                    pe.wait_ge(s_kT, p + 2)
                    project(p + 1, 1 - par, par, qwT, s_q)
                if not even and (t is None or 0 <= p - 3 < NP):
                    pe.wait_ge(s_x2T, p - 2)
                    for k in range(2):
                        ins = pe.matmul(psB[0:L, (3 + par) % 2, k * E:(k + 1) * E], x2T[:, k * L:(k + 1) * L],
                                        Wr_sb[:, :], start=True, stop=True)
                    ins.then_inc(s_R2, 1)
                if has(t, 3):
                    pe.wait_ge(s_on, i - 2)
                    if t is None or t >= 4:
                        pe.wait_ge(s_h1, i - 3)
                    pe.transpose(psU[:, 0:L], on[0:L, :, :].rearrange("p h c -> p (h c)"), ident[0:L, 0:L]).then_inc(s_U, 1)
                if has(t, 1):
                    pe.wait_ge(s_exp, i)
                    if t is None or t >= 2:
                        pe.wait_ge(s_PT, i - 1)
                    for h in range(H):
                        ins = pe.transpose(psT[0:L, h // HG, h % HG * L:(h % HG + 1) * L], P[0:L, (u + 1) % 2, h, :],
                                           ident[0:L, 0:L])
                    ins.then_inc(s_T, 1)
                if even and (t is None or 0 <= p - 3 < NP):
                    pe.wait_ge(s_x2, 2 * p - 4)
                    pe.wait_ge(s_Vs, p + 1 if t is None else min(p + 1, NP))
                    if t is None or p >= 4:
                        pe.wait_ge(s_lg, p - 3)
                    for k in range(2):
                        ins = pe.transpose(psB[:, (1 + par) % 2, k * L:(k + 1) * L],
                                           x2[0:L, 1 - par, k, :], ident[0:L, 0:L])
                    ins.then_inc(s_R1, 1)
                if not even and (t is None or p + 2 < NP):
                    transpose_xn(p + 2, par)
                if has(t, 2):
                    pe.wait_ge(s_PT, i - 1)
                    if t is None or t >= 3:
                        pe.wait_ge(s_on, i - 2)
                    pe.wait_ge(s_Vs, p if even else p)
                    for h in range(H):
                        ins = pe.matmul(psO[0:L, h * (HD + 1):(h + 1) * (HD + 1)], PT[0:L, u % 2, h // HG, h % HG * L:(h % HG + 1) * L],
                                        V[0:L, (par + 1) % 2, u % 2, h, :], start=True, stop=True)
                    ins.then_inc(s_PV, 1)
                if has(t, 3):
                    pe.wait_ge(s_oT, i - 2)
                    pe.matmul(psU[0:L, 128:256], oT[:, :], owT[:, :], start=True, stop=True).then_inc(s_P, 1)
                if even and (t is None or p + 2 < NP):
                    pe.wait_ge(s_qs, 2 * p + 4)
                    transpose_h0(p + 2, par)
                if not even and (t is None or p + 2 < NP):
                    if t is None or p >= 3:
                        pe.wait_ge(s_lg, p - 2)
                    pe.wait_ge(s_Vs, p + 1)
                    project(p + 2, par, (5 + par) % 2, kwT, s_k)
                if not even and (t is None or p + 1 < NP):
                    pe.wait_ge(s_qs, 2 * p + 4)
                    if t is None or p + 2 < NP:
                        pe.wait_ge(s_xT, p + 3)
                    values(p + 1, 1 - par, par)

            pe.wait_ge(l_rows, 16 * N_ROWS)
            attention_steps(pe, step)

            pe.wait_ge(r_oh, 1)
            pe.matmul(psS[0:L, 0, 0:E * B], before[0:L, 0:L], oh_bf[0:L, :, :].rearrange("p e b -> p (e b)"),
                      start=True, stop=True)
            pe.matmul(psS[0:L, 1, 0:E * B], ones_bf[0:L, 0:L], oh_bf[0:L, :, :].rearrange("p e b -> p (e b)"),
                      start=True, stop=True).then_inc(r_cnt, 1)
            for b in range(B):
                pe.wait_ge(r_1h, b // (B // 4) + 1)
                ins = pe.matmul(psO[:, 0:2 * NT], slot1h[0:L, b, :], tok1h[0:L, b, :, :].rearrange("p a t -> p (a t)"),
                                start=(b == 0), stop=(b == B - 1))
            ins.then_inc(r_ids, 1)

            def transpose_rows(s, r, u, t):
                pe.wait_ge(f_gat[u], 16 * (r + 1))
                if t is None or t >= 2:
                    pe.wait_ge(f_xT, s - 1)
                pe.transpose(psB[:, u % 2, 0:128], xg[:, u, 0:D], ident[:, :]).then_inc(f_Xt, 1)

            pe.wait_ge(r_idx, 1)
            pe.wait_ge(r_eid, 1)
            pe.wait_ge(l_ffn, 48)
            transpose_rows(0, 0, 0, 0)

            def step(s, r, u, t):
                if t is None or t + 1 < NT:
                    transpose_rows(s + 1, r + (u + 1) // RING, (u + 1) % RING, None if t is None else t + 1)
                if t is None or t < NT:
                    e = pe.value_load(eid[0:1, bass.ds(s, 1)], min_val=0, max_val=E - 1)
                    pe.wait_ge(f_xT, s + 1)
                    if t is None or t >= 2:
                        pe.wait_ge(f_hp, s - 1)
                    pe.matmul(psS[:, u % 2, :], xgT[:, u % 2, :], W1_sb[:, bass.ds(e * F, F)],
                              start=True, stop=True).then_inc(f_L1, 1)
                if has(t, 1, NT):
                    pe.wait_ge(f_hp, s)
                    if t is None or t >= 3:
                        pe.wait_ge(f_hT, s - 2)
                    for c in range(FC):
                        ins = pe.transpose(psT[:, (u + 1) % 2, c * 128:(c + 1) * 128],
                                           hpre[:, (u + 1) % 2, c * 128:(c + 1) * 128], ident[:, :])
                    ins.then_inc(f_G, 1)
                if has(t, 2, NT):
                    e = pe.value_load(eid[0:1, bass.ds(s - 2, 1)], min_val=0, max_val=E - 1)
                    pe.wait_ge(f_hT, s - 1)
                    if t is None or t >= 4:
                        pe.wait_ge(f_y, s - 3)
                    for c in range(FC):
                        ins = pe.matmul((psO if u % 2 == 0 else psU)[:, 0:D], hT[:, u % 2, c * 128:(c + 1) * 128],
                                        W2_sb[:, bass.ds(e * F + c * D, D)], start=(c == 0), stop=(c == FC - 1))
                    ins.then_inc(f_L2, 1)

            ffn_steps(pe, step, NT + 2)


_INS = ['x', 'L0_tok_W', 'L0_tok_b', 'L0_tok_gamma', 'L0_tok_beta', 'L0_attn_edge_index', 'L0_attn_edge_attr',
        'L0_attn_q_w', 'L0_attn_q_b', 'L0_attn_k_w', 'L0_attn_k_b', 'L0_attn_v_w', 'L0_attn_v_b', 'L0_attn_o_w',
        'L0_attn_o_b', 'L0_attn_eb_w', 'L0_attn_eb_b', 'L0_ffn_Wr', 'L0_ffn_br', 'L0_ffn_W1', 'L0_ffn_b1',
        'L0_ffn_W2', 'L0_ffn_b2']


def kernel(**inputs):
    import concourse.bacc as bacc
    from concourse.bass_utils import run_bass_kernel_spmd

    nc = bacc.Bacc("TRN2", target_bir_lowering=False, num_devices=1)
    arrays, args = {}, []
    for name in _INS:
        a = np.ascontiguousarray(inputs[name])
        arrays[f"in_{name}"] = a
        args.append(nc.dram_tensor(f"in_{name}", a.shape, mybir.dt.from_np(a.dtype), kind="ExternalInput").ap())
    out = nc.dram_tensor("out_0", (N, D), F32, kind="ExternalOutput").ap()
    build(nc, *args, out)
    r = run_bass_kernel_spmd(nc, [arrays], core_ids=[0])
    return r.results[0]["out_0"].reshape(B, L, D)
```

```python
from contextlib import ExitStack

import numpy as np

import concourse.bass as bass
from concourse import mybir

F32 = mybir.dt.float32
BF16 = mybir.dt.bfloat16
I32 = mybir.dt.int32
ALU = mybir.AluOpType
ACT = mybir.ActivationFunctionType
AX = mybir.AxisListType

EPS = 1e-5
B, TF, DI = 32, 125, 23
CTX = 5
L = TF - CTX + 1
N = B * L
D = 128
H, HD = 8, 16
HB = 32
HG = 4
SEG = (L - 1) // 4
RUN = (SEG + CTX) * DI
CH = 4 * L
NCH = N // CH
PL = 2 * L
NP = B // 2
NEDGE = 8192
EF = NEDGE // 128
EG = 8
E, F = 8, 512
FC = F // 128
NT = (N + E * 127) // 128
RING = 4
NOROW = 8192


def build(nc, x, tok_W, tok_b, gamma, beta, edge_index, edge_attr, q_w, q_b, k_w, k_b, v_w, v_b, o_w, o_b,
          eb_w, eb_b, Wr, br, W1, b1, W2, b2, out):
    with ExitStack() as ctx:
        def sb(name, shape, dt=F32):
            return ctx.enter_context(nc.sbuf_tensor(name, shape, dt))

        def sem(name):
            return ctx.enter_context(nc.semaphore(name))

        rows_d = nc.dram_tensor("rows_d", [N, 2 * D], F32, kind="Internal").ap()

        psS = ctx.enter_context(nc.psum_tensor("psS", [128, 2, 512], F32))
        psT = ctx.enter_context(nc.psum_tensor("psT", [128, 2, 512], F32))
        psO = ctx.enter_context(nc.psum_tensor("psO", [128, 512], F32))
        psU = ctx.enter_context(nc.psum_tensor("psU", [128, 512], F32))
        psB = ctx.enter_context(nc.psum_tensor("psB", [128, 2, 512], F32))
        banks = [psS[:, 0, :], psS[:, 1, :], psT[:, 0, :], psT[:, 1, :], psO[:, :], psU[:, :],
                 psB[:, 0, :], psB[:, 1, :]]

        ident = sb("ident", [128, 128])
        headmask = sb("headmask", [128, HG])
        before = sb("before", [128, 128], BF16)
        ones_bf = sb("ones_bf", [128, 128], BF16)
        ones_f = sb("ones_f", [128, E * B])
        slot_iota = sb("slot_iota", [128, 128])
        seq_iota = sb("seq_iota", [128, B])
        part1 = sb("part1", [128, 1])
        rank8 = sb("rank8", [128, E])
        tile_starts = sb("tile_starts", [128, B - 1])
        col_iota = sb("col_iota", [128, EF * EG])
        minus_half = sb("minus_half", [128, 2])
        tokW_sb = sb("tokW_sb", [128, CTX * DI])
        tokWT = sb("tokWT", [128, 128])
        proj_in = sb("proj_in", [128, 4, D])
        qwT = sb("qwT", [128, H * HB])
        kwT = sb("kwT", [128, H * HB])
        vwT = sb("vwT", [128, D])
        owT = sb("owT", [128, D])
        qk_row = sb("qk_row", [1, 2, H * HB])
        qk_col = sb("qk_col", [128, 4])
        addK = sb("addK", [128, 2, L])
        col3 = sb("col3", [128, 3])
        ob_bc = sb("ob_bc", [128, D])
        vb_bc = sb("vb_bc", [128, D])
        br_bc = sb("br_bc", [128, E])
        ebw_bc = sb("ebw_bc", [128, 3 * H])
        ebb_bc = sb("ebb_bc", [128, H])
        Wr_sb = sb("Wr_sb", [128, E])
        W1_sb = sb("W1_sb", [128, E * F])
        W2_sb = sb("W2_sb", [128, E * F])
        countbc = sb("countbc", [128, E * F])
        b2_bc = sb("b2_bc", [128, E * D])
        xs = sb("xs", [128, RUN])
        patT = sb("patT", [128, N])
        yT = sb("yT", [128, N])
        bn_st = sb("bn_st", [128, NCH, 6])
        bn_mv = sb("bn_mv", [128, 2])
        bn_r = sb("bn_r", [128, 2])
        bn_ac = sb("bn_ac", [128, 2])
        edge_i = sb("edge_i", [EF, 2, 128], I32)
        edge_f = sb("edge_f", [EF, 2, 128])
        edge_c = sb("edge_c", [EF, 2, 128])
        edge_v = sb("edge_v", [EF, 128])
        key = sb("key", [EF, 128])
        keyT = sb("keyT", [128, EF])
        power = sb("power", [128, 3, EG])
        power_bf = sb("power_bf", [128, EG], BF16)
        target1h = W1_sb[:, 0:EF * L // 2].bitcast(BF16).rearrange("p (f t) -> p f t", f=EF)
        col_hit = W2_sb[:, 0:EF * EG]
        picked = W2_sb[:, EF * EG:2 * EF * EG]
        found = sb("found", [128, 3])
        last = sb("last", [128, 3])
        last_i = sb("last_i", [128, 1], I32)
        attr = sb("attr", [128, 3])
        ebias = sb("ebias", [128, H])
        bias_pad = sb("bias_pad", [128, H * HB])
        h0T = sb("h0T", [128, PL])
        h0k = sb("h0k", [128, 2, D])
        st1 = sb("st1", [128, 2, 6])
        mv1 = sb("mv1", [128, 2, 2])
        var1 = sb("var1", [128, 2])
        rs1 = sb("rs1", [128, 2])
        nm1 = sb("nm1", [128, 2])
        xn = sb("xn", [128, 2, D])
        xT = sb("xT", [128, 2, PL])
        qT = sb("qT", [128, 2, 2, PL])
        kT = sb("kT", [128, 2, PL])
        kbd = patT[:, :].rearrange("p (s g n) -> p s g n", s=4, g=2)
        V = sb("V", [128, 2, 2, H, HD + 1])
        nmax = sb("nmax", [128, H])
        P = sb("P", [128, 2, H, L])
        PT = sb("PT", [128, 2, 2, HG * L])
        rden = sb("rden", [128, H])
        on = sb("on", [128, H, HD])
        oT = sb("oT", [128, L])
        st2 = sb("st2", [128, 6])
        mv2 = sb("mv2", [128, 2, 2])
        var2 = sb("var2", [128, 2])
        rs2 = sb("rs2", [128, 2])
        x2 = sb("x2", [128, 2, 2, D])
        res = sb("res", [128, B, D])
        x2T = sb("x2T", [128, PL])
        lg = sb("lg", [128, B, E])
        top = sb("top", [128, B])
        eq = sb("eq", [128, B, E])
        onehot = sb("onehot", [128, B, E])
        oh_bf = sb("oh_bf", [128, E, B], BF16)
        incl = sb("incl", [128, E, B])
        posE = sb("posE", [128, E, B])
        cnt = sb("cnt", [128, 6, E])
        cmpt = sb("cmpt", [128, E, B - 1])
        pos = sb("pos", [128, B])
        pos_i = sb("pos_i", [128, 3, B], I32)
        pos_f = sb("pos_f", [128, 2, B])
        onehots = yT[:, :].bitcast(BF16)
        slot1h = onehots[:, 0:B * 128].rearrange("p (b n) -> p b n", b=B)
        tile1h = onehots[:, B * 128:B * (128 + NT)].rearrange("p (b n) -> p b n", b=B)
        tok1h = onehots[:, B * (128 + NT):B * (128 + 3 * NT)].rearrange("p (b a n) -> p b a n", b=B, a=2)
        idf = sb("idf", [128, 2, NT])
        idg = sb("idg", [128, NT, 2])
        idx = sb("idx", [128, NT, 2], I32)
        eidc = sb("eidc", [128, NT, E])
        eidf = sb("eidf", [128, NT])
        eid = sb("eid", [128, NT], I32)
        xg = sb("xg", [128, RING, 2 * D])
        gidx = sb("gidx", [128, RING], I32)
        sidx = sb("sidx", [128, RING], I32)
        xgT = sb("xgT", [128, 2, 128])
        hpre = sb("hpre", [128, 2, F])
        hT = sb("hT", [128, 2, F])
        resid = sb("resid", [128, RING, D])
        y_out = sb("y_out", [128, RING, D])

        l_x, l_tokW, l_proj, l_edges, l_cols, l_rows, l_ffn, l_attr, l_qkb = map(
            sem, "l_x l_tokW l_proj l_edges l_cols l_rows l_ffn l_attr l_qkb".split())
        s_power, s_colio = sem("s_power"), sem("s_colio")
        a_keyT, a_1h, a_bits = sem("a_keyT"), sem("a_1h"), sem("a_bits")
        s_const = sem("s_const")
        s_rowset = sem("s_rowset")
        a_wt, a_w4, a_xt, a_y, a_bias = map(sem, "a_wt a_w4 a_xt a_y a_bias".split())
        a_wts, a_pat_v, a_pat_s, a_relu, a_bst = map(sem, "a_wts a_pat_v a_pat_s a_relu a_bst".split())
        a_var, a_rstd, a_pool, a_ac = map(sem, "a_var a_rstd a_pool a_ac".split())
        a_chain, a_keyed, a_biasT, a_lasti, a_bpad, a_addk = map(
            sem, "a_chain a_keyed a_biasT a_lasti a_bpad a_addk".split())
        s_S, s_T, s_PV, s_U, s_P = map(sem, "s_S s_T s_PV s_U s_P".split())
        s_T1, s_T2, s_k, s_q, s_V, s_R1, s_R2 = map(sem, "s_T1 s_T2 s_k s_q s_V s_R1 s_R2".split())
        s_max, s_rd, s_on, s_h1, s_st, s_ag, s_x2 = map(
            sem, "s_max s_rd s_on s_h1 s_st s_ag s_x2".split())
        s_kT, s_Vs, s_lg, s_st1, s_ag1 = map(sem, "s_kT s_Vs s_lg s_st1 s_ag1".split())
        s_exp, s_PT, s_oT, s_h0T, s_h0k, s_xT, s_qs, s_x2T = map(
            sem, "s_exp s_PT s_oT s_h0T s_h0k s_xT s_qs s_x2T".split())
        s_v1, s_r1, s_nm1, s_xn, s_h0b, s_kbd, s_v2, s_r2 = map(
            sem, "s_v1 s_r1 s_nm1 s_xn s_h0b s_kbd s_v2 s_r2".split())
        s_carry_p, s_carry_v = sem("s_carry_p"), sem("s_carry_v")
        d_x2, d_res = [sem("d_x2_0"), sem("d_x2_1")], sem("d_res")
        r_oh, r_cnt, r_1h, r_ids, r_idx, r_eid, r_chain = map(
            sem, "r_oh r_cnt r_1h r_ids r_idx r_eid r_chain".split())
        f_gat = [sem(f"f_gat{u}") for u in range(RING)]
        f_sca = [sem(f"f_sca{u}") for u in range(RING)]
        f_gi, f_si, f_Xt, f_xT, f_L1, f_hp, f_G, f_hT, f_L2, f_rs, f_y = map(
            sem, "f_gi f_si f_Xt f_xT f_L1 f_hp f_G f_hT f_L2 f_rs f_y".split())

        N_CONST = 20
        N_COLS, N_ROWS = 3, 7

        DRAIN = 7
        PEEL, TAIL = 2, 2

        def attention_steps(eng, step):
            for i in range(4 * PEEL):
                step(i // 4, i, i // 2, i % 4, i)
            with eng.Fori(PEEL, B // 4 - TAIL) as body:
                for u in range(4):
                    step(body, 4 * body + u, 2 * body + u // 2, u, None)
            for i in range(B - 4 * TAIL, B + DRAIN):
                step(i // 4, i, i // 2, i % 4, i)

        def ffn_steps(eng, step, end):
            for s in range(2 * RING):
                step(s, s // RING, s % RING, s)
            with eng.Fori(2, NT // RING - 1) as r:
                for u in range(RING):
                    step(RING * r + u, r, u, None)
            for s in range(RING * (NT // RING - 1), end):
                step(s, s // RING, s % RING, s)

        def has(t, back, n=B):
            return t is None or 0 <= t - back < n

        block = ctx.enter_context(nc.Block())

        @block.sync
        def _(sp):
            sp.dma_start(xs[:, :], bass.AP(x.tensor, 0, [[TF * DI, B], [SEG * DI, 4], [1, RUN]])).then_inc(l_x, 16)
            sp.dma_start(tokW_sb[:, :], tok_W).then_inc(l_tokW, 16)
            sp.dma_start(edge_i[:, :, :], edge_index.rearrange("a (f p) -> f a p", p=128)).then_inc(l_edges, 16)
            for n, w in enumerate((q_w, k_w, v_w, o_w)):
                sp.dma_start(proj_in[:, n, :], w).then_inc(l_proj, 16)
            for n, v in enumerate((tok_b, gamma, beta)):
                sp.dma_start(col3[:, n:n + 1], v.rearrange("(p a) -> p a", a=1)).then_inc(l_cols, 16)
            sp.wait_ge(s_rowset, 2)
            for n, v in enumerate((q_b, k_b)):
                sp.dma_start(qk_row[0:1, n, :].rearrange("p (h c) -> p h c", c=HB)[:, :, 0:HD],
                             v.rearrange("(a h c) -> a h c", a=1, c=HD)).then_inc(l_qkb, 16)
            for t, v in ((ob_bc, o_b), (vb_bc, v_b), (br_bc, br), (ebb_bc, eb_b)):
                sp.dma_start(t[:, :], v.partition_broadcast(128)).then_inc(l_rows, 16)
            sp.dma_start(ebw_bc[:, :], eb_w.rearrange("h k -> (h k)").partition_broadcast(128)).then_inc(l_rows, 16)
            sp.dma_start(b2_bc[:, :], b2.rearrange("e d -> (e d)").partition_broadcast(128)).then_inc(l_rows, 16)
            sp.dma_start(Wr_sb[:, :], Wr).then_inc(l_rows, 16)
            sp.wait_ge(l_attr, 16)
            sp.dma_start(W1_sb[:, :].rearrange("d (e f) -> d e f", e=E), W1.rearrange("e d f -> d e f")).then_inc(l_ffn, 16)
            sp.dma_start(W2_sb[:, :].rearrange("h (g o) -> h g o", o=D),
                         W2.rearrange("e (c h) o -> h (e c) o", h=128)).then_inc(l_ffn, 16)
            sp.dma_start(countbc[:, :], b1.rearrange("e f -> (e f)").partition_broadcast(128)).then_inc(l_ffn, 16)
            rows_v = rows_d.rearrange("(b n) d -> n b d", n=L)
            with sp.Fori(0, NP // 2) as r:
                for par in range(2):
                    b = 4 * r + 2 * par
                    sp.wait_ge(s_x2, b + 2)
                    sp.dma_start(rows_v[:, bass.ds(b, 2), 0:D], x2[0:L, par, :, :]).then_inc(d_x2[par], 16)
                    sp.dma_start(rows_v[:, bass.ds(b, 2), D:2 * D], res[0:L, bass.ds(b, 2), :]).then_inc(d_res, 16)

        @block.gpsimd
        def _(pool):
            pool.memset(qk_row[:, :, :], 0.0).then_inc(s_rowset, 1)
            pool.wait_ge(s_rowset, 1)
            pool.memset(qk_row[:, 0, :].rearrange("p (h c) -> p h c", c=HB)[:, :, HD:HD + 1], 4.0).then_inc(s_rowset, 1)
            pool.memset(ident[:, :], 0.0).then_inc(s_const, 1)
            pool.memset(headmask[:, :], 1.0).then_inc(s_const, 1)
            pool.memset(before[:, :], 1.0).then_inc(s_const, 1)
            pool.memset(ones_bf[:, :], 1.0).then_inc(s_const, 1)
            pool.memset(ones_f[:, :], 1.0).then_inc(s_const, 1)
            pool.memset(minus_half[:, :], -0.5).then_inc(s_const, 1)
            pool.memset(qwT[:, :], 0.0).then_inc(s_const, 1)
            pool.memset(kwT[:, :], 0.0).then_inc(s_const, 1)
            pool.memset(bias_pad[:, :], 0.0).then_inc(s_const, 1)
            pool.memset(V[:, :, :, :, :], 1.0).then_inc(s_const, 1)
            fl = dict(allow_small_or_imprecise_dtypes=True)
            pool.iota(slot_iota[:, :], pattern=[[1, 128]], base=0, channel_multiplier=0, **fl).then_inc(s_const, 1)
            pool.iota(seq_iota[:, :], pattern=[[1, B]], base=0, channel_multiplier=0, **fl).then_inc(s_const, 1)
            pool.iota(part1[:, :], pattern=[[0, 1]], base=1, channel_multiplier=1, **fl).then_inc(s_const, 1)
            pool.iota(rank8[:, :], pattern=[[-1, E]], base=E, channel_multiplier=0, **fl).then_inc(s_const, 1)
            pool.iota(tile_starts[:, :], pattern=[[128, B - 1]], base=0, channel_multiplier=0, **fl).then_inc(s_const, 1)
            pool.iota(power[:, 0, :], pattern=[[-128 // EG, EG]], base=127, channel_multiplier=1, **fl).then_inc(s_const, 1)
            pool.wait_ge(s_const, 16)
            pool.affine_select(out=ident[:, :], in_=ident[:, :], compare_op=ALU.not_equal, fill=1.0, base=0,
                               pattern=[[-1, 128]], channel_multiplier=1).then_inc(s_const, 1)
            pool.affine_select(out=before[:, :], in_=before[:, :], compare_op=ALU.is_ge, fill=0.0, base=-1,
                               pattern=[[1, 128]], channel_multiplier=-1).then_inc(s_const, 1)
            pool.affine_select(out=headmask[:, :], in_=headmask[:, :], compare_op=ALU.is_ge, fill=0.0, base=0,
                               pattern=[[-HB, HG]], channel_multiplier=1).then_inc(s_const, 1)
            pool.wait_ge(s_const, 19)
            pool.affine_select(out=headmask[:, :], in_=headmask[:, :], compare_op=ALU.is_ge, fill=0.0, base=HB - 1,
                               pattern=[[HB, HG]], channel_multiplier=-1).then_inc(s_const, 1)
            pool.affine_select(out=power[:, 0, :], in_=power[:, 0, :], compare_op=ALU.is_ge, fill=0.0, base=0,
                               pattern=[[-128 // EG, EG]], channel_multiplier=1).then_inc(s_power, 1)
            pool.wait_ge(s_power, 1)
            pool.affine_select(out=power[:, 0, :], in_=power[:, 0, :], compare_op=ALU.is_ge, fill=0.0, base=128 // EG - 1,
                               pattern=[[128 // EG, EG]], channel_multiplier=-1).then_inc(s_power, 1)
            pool.iota(col_iota[:, :], pattern=[[1, EF * EG]], base=1, channel_multiplier=0, **fl).then_inc(s_colio, 1)

            pool.wait_ge(a_var, 1)
            pool.tensor_scalar(bn_r[:, 0:1], bn_mv[:, 1:2], 1.0, EPS, ALU.mult, ALU.add).then_inc(a_pool, 1)
            pool.wait_ge(a_pool, 1)
            pool.tensor_tensor(bn_r[:, 1:2], bn_r[:, 0:1], minus_half[:, 0:1], ALU.pow).then_inc(a_rstd, 1)
            pool.wait_ge(a_lasti, 1)
            pool.indirect_dma_start(attr[0:L, :], None, edge_attr, bass.IndirectOffsetOnAxis(last_i[0:L, 0:1], 0),
                                    bounds_check=NEDGE - 1, oob_is_err=False).then_inc(l_attr, 16)

            def norm1(p):
                pool.wait_ge(s_ag1, p + 1)
                pool.sem_inc(s_carry_p, 1)
                pool.tensor_scalar(var1[0:L, :], mv1[0:L, :, 1], 1.0, EPS, ALU.mult, ALU.add).then_inc(s_v1, 1)
                pool.wait_ge(s_v1, p + 1)
                pool.tensor_tensor(rs1[0:L, :], var1[0:L, :], minus_half[0:L, :], ALU.pow).then_inc(s_r1, 1)
                pool.wait_ge(s_r1, p + 1)
                pool.tensor_tensor(nm1[0:L, :], mv1[0:L, :, 0], rs1[0:L, :], ALU.mult).then_inc(s_nm1, 1)
                pool.wait_ge(s_nm1, 2 * p + 1)
                pool.sem_inc(s_carry_p, 1)
                pool.tensor_scalar(nm1[0:L, :], nm1[0:L, :], -1.0, 0.0, ALU.mult, ALU.add).then_inc(s_nm1, 1)
                pool.wait_ge(s_nm1, 2 * p + 2)
                if not (isinstance(p, int) and p == 0):
                    pool.wait_ge(s_T2, p)
                pool.sem_inc(s_carry_p, 1)
                for k in range(2):
                    pool.tensor_scalar(xn[0:L, k, :], h0k[0:L, k, :], rs1[0:L, k:k + 1], nm1[0:L, k:k + 1],
                                       ALU.mult, ALU.add).then_inc(s_xn, 1)
                pool.tensor_tensor(res[0:L, bass.ds(2 * p, 2), :], h0k[0:L, :, :],
                                   ob_bc[0:L, :].unsqueeze(1).to_broadcast([L, 2, D]), ALU.add).then_inc(s_h0b, 1)

            def key_blocks(p, slot, which):
                pool.wait_ge(s_kT, p + 1)
                for k in which:
                    if not (isinstance(p, int) and p < 2):
                        pool.wait_ge(s_S, 4 * p + 2 * k - 6)
                    pool.tensor_tensor(kbd[:, slot + k, :, :].rearrange("p g (j m) -> p g j m", m=L),
                                       kT[:, :, k * L:(k + 1) * L].unsqueeze(2).to_broadcast([128, 2, HG, L]),
                                       headmask[:, :].unsqueeze(1).unsqueeze(3).to_broadcast([128, 2, HG, L]),
                                       ALU.mult).then_inc(s_kbd, 1)

            def rstd2(b, par):
                pool.wait_ge(s_ag, b + 1)
                pool.sem_inc(s_carry_p, 1)
                pool.tensor_scalar(var2[0:L, par:par + 1], mv2[0:L, par, 1:2], 1.0, EPS, ALU.mult, ALU.add).then_inc(s_v2, 1)
                pool.wait_ge(s_v2, b + 1)
                pool.tensor_tensor(rs2[0:L, par:par + 1], var2[0:L, par:par + 1], minus_half[0:L, 0:1], ALU.pow).then_inc(s_r2, 1)

            pool.wait_ge(l_rows, 16 * N_ROWS)
            norm1(0)
            key_blocks(0, 0, (0, 1))
            norm1(1)

            def step(r, i, p, u, t):
                even = u % 2 == 0
                if t is None or p + 1 < NP:
                    key_blocks(p + 1, 2 - u // 2 * 2, (u % 2,))
                if has(t, 3):
                    rstd2(i - 3, (u + 1) % 2)
                if even and (t is None or p + 2 < NP):
                    norm1(p + 2)

            attention_steps(pool, step)

            pool.wait_ge(d_res, 16 * NP)
            for par in range(2):
                pool.wait_ge(d_x2[par], 16 * (NP // 2))
            for s in range(RING):
                pool.wait_ge(r_idx, 1)
                pool.wait_ge(f_gi, s + 1)
                pool.indirect_dma_start(xg[:, s, :], None, rows_d, bass.IndirectOffsetOnAxis(gidx[:, s:s + 1], 0),
                                        bounds_check=N - 1, oob_is_err=False).then_inc(f_gat[s], 16)

            def step(s, r, u, t):
                if t is None or t + RING < NT:
                    pool.wait_ge(f_gi, s + RING + 1)
                    pool.wait_ge(f_rs, s + 1)
                    pool.sem_inc(s_carry_p, 1)
                    pool.indirect_dma_start(xg[:, u, :], None, rows_d, bass.IndirectOffsetOnAxis(gidx[:, u:u + 1], 0),
                                            bounds_check=N - 1, oob_is_err=False).then_inc(f_gat[u], 16)
                if has(t, 2, NT):
                    v = (u - 2) % RING
                    pool.wait_ge(f_y, s - 1)
                    pool.sem_inc(s_carry_p, 1)
                    pool.indirect_dma_start(out, bass.IndirectOffsetOnAxis(sidx[:, v:v + 1], 0), y_out[:, v, :], None,
                                            bounds_check=N - 1, oob_is_err=False).then_inc(f_sca[v], 16)

            ffn_steps(pool, step, NT + 2)
            for u in range(RING):
                pool.wait_ge(f_sca[u], 16 * len(range(u, NT, RING)))

        @block.scalar
        def _(act):
            def pat_copy(t):
                bank = banks[(3 + t) % 8]
                ni = min(4, SEG - 4 * t)
                dst = patT[0:CTX * DI, :].rearrange("p (b l) -> p b l", l=L)[:, :, 0:4 * SEG] \
                    .rearrange("p b (j i) -> p i b j", i=SEG)[:, 4 * t:4 * t + ni]
                src = bank[0:CTX * DI, 0:128 * ni].rearrange("p (i b j) -> p i b j", i=ni, j=4)
                return dst, src

            for t in range(1, 8, 2):
                act.wait_ge(a_xt, t + 1)
                dst, src = pat_copy(t)
                ins = act.activation(dst, src, ACT.Identity)
                if t < 7:
                    ins.then_inc(a_pat_s, 1)
            bank = banks[(3 + 7) % 8]
            act.activation(patT[0:CTX * DI, :].rearrange("p (b l) -> p b l", l=L)[:, :, L - 1],
                           bank[0:CTX * DI, 256:384].rearrange("p (b j) -> p b j", j=4)[:, :, 3],
                           ACT.Identity).then_inc(a_pat_s, 1)
            act.wait_ge(l_cols, 16 * N_COLS)
            for c in range(NCH):
                act.wait_ge(a_y, c + 1)
                act.activation(yT[:, c * CH:(c + 1) * CH], banks[(3 + c) % 8][:, 0:CH], ACT.Relu,
                               bias=col3[:, 0:1]).then_inc(a_relu, 1)

            def batch_norm(p):
                if not (isinstance(p, int) and p == 0):
                    act.wait_ge(s_T1, p)
                act.activation(h0T[:, :], yT[:, bass.ds(p * PL, PL)], ACT.Identity, bias=bn_ac[:, 1:2],
                               scale=bn_ac[:, 0:1]).then_inc(s_h0T, 1)

            def h0_copy(p, bank):
                act.wait_ge(s_T1, p + 1)
                if not (isinstance(p, int) and p == 0):
                    act.wait_ge(s_h0b, p)
                act.activation(h0k[0:L, :, :], psB[0:L, bank, 0:2 * D].rearrange("p (k d) -> p k d", k=2),
                               ACT.Identity).then_inc(s_h0k, 1)

            def xT_copy(p, par, bank):
                act.wait_ge(s_T2, p + 1)
                act.activation(xT[:, par, :], psB[:, bank, 0:PL], ACT.Identity).then_inc(s_xT, 1)

            def q_copy(p, par, bank):
                act.wait_ge(s_q, p + 1)
                for g in range(2):
                    act.activation(qT[:, par, g, :], psB[:, bank, g * PL:(g + 1) * PL], ACT.Identity,
                                   bias=qk_col[:, g:g + 1], scale=0.25).then_inc(s_qs, 1)

            act.wait_ge(a_ac, 1)
            act.wait_ge(a_wts, 7)
            batch_norm(0)
            h0_copy(0, 0)
            batch_norm(1)
            xT_copy(0, 0, 1)
            q_copy(0, 0, 1)
            h0_copy(1, 1)
            batch_norm(2)
            xT_copy(1, 1, 1)

            def step(r, i, p, u, t):
                par = u // 2
                even = u % 2 == 0
                if has(t, 3):
                    act.wait_ge(s_U, i - 2)
                    act.activation(oT[:, :], psU[:, 0:L], ACT.Identity).then_inc(s_oT, 1)
                if has(t, 0):
                    for h in range(H):
                        if h % HG == 0:
                            act.wait_ge(s_max, 2 * i + 1 + h // HG)
                        ins = act.activation(P[0:L, u % 2, h, :], psS[0:L, h // HG, h % HG * L:(h % HG + 1) * L],
                                             ACT.Exp, bias=nmax[0:L, h:h + 1])
                        if h % HG == HG - 1:
                            ins.then_inc(s_exp, 1)
                if not even and (t is None or 0 <= p - 3 < NP):
                    act.wait_ge(s_R1, p - 2)
                    act.activation(x2T[:, :], psB[:, 1 - par, 0:PL], ACT.Identity).then_inc(s_x2T, 1)
                if has(t, 1):
                    act.wait_ge(s_T, i)
                    act.activation(PT[0:L, (u + 1) % 2, :, :], psT[0:L, :, 0:HG * L], ACT.Identity).then_inc(s_PT, 1)
                if even and (t is None or p + 2 < NP):
                    h0_copy(p + 2, 1 - par)
                if even and (t is None or p + 1 < NP):
                    q_copy(p + 1, 1 - par, par)
                if not even and (t is None or p + 3 < NP):
                    batch_norm(p + 3)
                if not even and (t is None or p + 2 < NP):
                    xT_copy(p + 2, par, 1 - par)

            attention_steps(act, step)

            def xgT_copy(s, u, t):
                act.wait_ge(f_Xt, s + 1)
                if t is None or t >= 2:
                    act.wait_ge(f_L1, s - 1)
                act.activation(xgT[:, u % 2, :], psB[:, u % 2, 0:128], ACT.Identity).then_inc(f_xT, 1)

            xgT_copy(0, 0, 0)

            def step(s, r, u, t):
                if t is None or t + 1 < NT:
                    xgT_copy(s + 1, u + 1, None if t is None else t + 1)
                if has(t, 1, NT):
                    act.wait_ge(f_G, s)
                    if t is None or t >= 3:
                        act.wait_ge(f_L2, s - 2)
                    act.activation(hT[:, (u + 1) % 2, :], psT[:, (u + 1) % 2, :], ACT.Relu).then_inc(f_hT, 1)

            ffn_steps(act, step, NT + 1)

        @block.vector
        def _(dve):
            links = [0]

            def link(ins, chain=a_chain, count=links):
                count[0] += 1
                ins.then_inc(chain, 1)
                dve.wait_ge(chain, count[0])

            dve.wait_ge(l_edges, 16)
            dve.wait_ge(s_const, N_CONST)
            link(dve.tensor_copy(edge_f[:, :, :], edge_i[:, :, :]))
            link(dve.tensor_scalar(edge_c[:, :, :], edge_f[:, :, :], 0.0, float(L - 1), ALU.max, ALU.min))
            link(dve.tensor_tensor(edge_c[:, :, :], edge_c[:, :, :], edge_f[:, :, :], ALU.is_equal))
            link(dve.tensor_tensor(edge_v[:, :], edge_c[:, 0, :], edge_c[:, 1, :], ALU.mult))
            dve.scalar_tensor_tensor(out=key[:, :], in0=edge_f[:, 1, :], scalar=1.0, in1=edge_v[:, :],
                                     op0=ALU.add, op1=ALU.mult).then_inc(a_keyed, 1)
            dve.wait_ge(s_power, 2)
            link(dve.tensor_copy(power[:, 1, :].bitcast(I32), power[:, 0, :]))
            link(dve.tensor_scalar(power[:, 2, :].bitcast(I32), power[:, 1, :].bitcast(I32), 23, None, ALU.logical_shift_left))
            dve.tensor_copy(power_bf[:, :], power[:, 2, :]).then_inc(s_power, 1)
            dve.wait_ge(a_wt, 1)
            dve.wait_ge(a_keyT, 1)
            dve.tensor_copy(tokWT[0:CTX * DI, :], banks[0][0:CTX * DI, 0:128]).then_inc(a_wts, 1)
            dve.wait_ge(a_w4, 1)
            for n, w in enumerate((qwT, kwT)):
                dve.tensor_copy(w[:, :].rearrange("p (h c) -> p h c", c=HB)[:, :, 0:HD],
                                banks[1][:, n * D:(n + 1) * D].rearrange("p (h c) -> p h c", c=HD)).then_inc(a_wts, 1)
            dve.tensor_copy(vwT[:, :], banks[1][:, 2 * D:3 * D]).then_inc(a_wts, 1)
            dve.tensor_copy(owT[:, :], banks[1][:, 3 * D:4 * D]).then_inc(a_wts, 1)
            dve.wait_ge(a_bias, 1)
            dve.tensor_scalar(qk_col[:, 0:2], banks[2][:, 0:2], 0.25, None, ALU.mult).then_inc(a_wts, 1)
            dve.tensor_copy(qk_col[:, 2:4], banks[2][:, 2:4]).then_inc(a_wts, 1)
            link(dve.tensor_copy(keyT[:, :], banks[0][:, 128:128 + EF]))

            def target_onehots(c):
                dve.tensor_tensor(target1h[:, 8 * c:8 * c + 8, :],
                                  slot_iota[:, 1:L + 1].unsqueeze(1).to_broadcast([128, 8, L]),
                                  keyT[:, 8 * c:8 * c + 8].unsqueeze(2).to_broadcast([128, 8, L]),
                                  ALU.is_equal).then_inc(a_1h, 1)

            for t in range(0, 8, 2):
                target_onehots(t // 2)
                dve.wait_ge(a_xt, t + 1)
                bank = banks[(3 + t) % 8]
                dst = patT[0:CTX * DI, :].rearrange("p (b l) -> p b l", l=L)[:, :, 0:4 * SEG] \
                    .rearrange("p b (j i) -> p i b j", i=SEG)[:, 4 * t:4 * t + 4]
                dve.tensor_copy(dst, bank[0:CTX * DI, 0:512].rearrange("p (i b j) -> p i b j", i=4, j=4)) \
                   .then_inc(a_pat_v, 1)
            for c in range(NCH):
                dve.wait_ge(a_relu, c + 1)
                dve.bn_stats(bn_st[:, c, :], yT[:, c * CH:(c + 1) * CH]).then_inc(a_bst, 1)
                if c % 2 == 0 and 4 + c // 2 < EF // 8:
                    target_onehots(4 + c // 2)
            dve.wait_ge(a_bst, NCH)
            dve.bn_aggr(bn_mv[:, :], bn_st[:, :, :].rearrange("p a b -> p (a b)")).then_inc(a_var, 1)
            dve.wait_ge(a_rstd, 1)
            dve.wait_ge(l_cols, 16 * N_COLS)
            link(dve.tensor_tensor(bn_ac[:, 0:1], bn_r[:, 1:2], col3[:, 1:2], ALU.mult))
            link(dve.tensor_tensor(bn_r[:, 0:1], bn_mv[:, 0:1], bn_ac[:, 0:1], ALU.mult))
            dve.tensor_tensor(bn_ac[:, 1:2], col3[:, 2:3], bn_r[:, 0:1], ALU.subtract).then_inc(a_ac, 1)
            bits = banks[3][0:L, 0:EF * EG]
            dve.wait_ge(a_bits, 1)
            dve.wait_ge(s_colio, 1)
            link(dve.scalar_tensor_tensor(out=col_hit[0:L, :], in0=bits, scalar=0.0, in1=col_iota[0:L, :],
                                          op0=ALU.is_gt, op1=ALU.mult))
            link(dve.tensor_reduce(found[0:L, 0:1], col_hit[0:L, :], AX.X, ALU.max))
            link(dve.scalar_tensor_tensor(out=picked[0:L, :], in0=col_iota[0:L, :], scalar=found[0:L, 0:1], in1=bits,
                                          op0=ALU.is_equal, op1=ALU.mult, accum_out=found[0:L, 1:2]))
            link(dve.tensor_scalar(found[0:L, 2:3].bitcast(I32), found[0:L, 1:2].bitcast(I32), 23, None,
                                   ALU.arith_shift_right))
            link(dve.tensor_copy(last[0:L, 0:1], found[0:L, 2:3].bitcast(I32)))
            link(dve.scalar_tensor_tensor(out=last[0:L, 0:1], in0=found[0:L, 0:1], scalar=float(128 // EG),
                                          in1=last[0:L, 0:1], op0=ALU.mult, op1=ALU.add))
            link(dve.tensor_scalar(last[0:L, 1:2], found[0:L, 0:1], 0.0, None, ALU.is_gt))
            dve.tensor_scalar(last_i[0:L, :], last[0:L, 0:1], -127.0 - 128 // EG, 0.0, ALU.add, ALU.max).then_inc(a_lasti, 1)
            dve.wait_ge(l_attr, 16)
            dve.wait_ge(l_rows, 16 * N_ROWS)
            for n in range(3):
                link(dve.scalar_tensor_tensor(
                    out=ebias[0:L, :], in0=ebw_bc[0:L, :].rearrange("p (h k) -> p h k", k=3)[:, :, n],
                    scalar=attr[0:L, n:n + 1], in1=(ebb_bc if n == 0 else ebias)[0:L, :], op0=ALU.mult, op1=ALU.add))
            dve.tensor_scalar(bias_pad[0:L, :].rearrange("p (h c) -> p h c", c=HB)[:, :, HD], ebias[0:L, :],
                              last[0:L, 1:2], None, ALU.mult).then_inc(a_bpad, 1)
            dve.wait_ge(a_biasT, 1)
            for g in range(2):
                ins = dve.tensor_scalar(addK[:, g, :], banks[5][:, g * 128:g * 128 + L], qk_col[:, 2 + g:3 + g], None, ALU.add)
            ins.then_inc(a_addk, 1)
            dve.wait_ge(a_addk, 1)

            def stats1(p):
                dve.wait_ge(s_h0k, p + 1)
                if not (isinstance(p, int) and p == 0):
                    dve.wait_ge(s_nm1, 2 * p)
                for k in range(2):
                    dve.bn_stats(st1[0:L, k, :], h0k[0:L, k, :]).then_inc(s_st1, 1)
                dve.wait_ge(s_st1, 2 * p + 2)
                if not (isinstance(p, int) and p == 0):
                    dve.wait_ge(s_xn, 2 * p)
                dve.sem_inc(s_carry_v, 1)
                for k in range(2):
                    ins = dve.bn_aggr(mv1[0:L, k, :], st1[0:L, k, :])
                ins.then_inc(s_ag1, 1)

            def k_copy(p, bank):
                dve.wait_ge(s_k, p + 1)
                if not (isinstance(p, int) and p == 0):
                    dve.wait_ge(s_kbd, 2 * p)
                dve.tensor_tensor(kT[:, :, :].rearrange("p g (k m) -> p g k m", m=L),
                                  psB[:, bank, 0:2 * PL].rearrange("p (g k m) -> p g k m", g=2, m=L),
                                  addK[:, :, :].unsqueeze(2).to_broadcast([128, 2, 2, L]), ALU.add).then_inc(s_kT, 1)

            def v_copy(p, par, bank):
                dve.wait_ge(s_V, p + 1)
                if not (isinstance(p, int) and p < 2):
                    dve.wait_ge(s_PV, 2 * p - 2)
                for k in range(2):
                    ins = dve.tensor_tensor(V[0:L, par, k, :, 0:HD],
                                            psB[0:L, bank, k * D:(k + 1) * D].rearrange("p (h c) -> p h c", c=HD),
                                            vb_bc[0:L, :].rearrange("p (h c) -> p h c", c=HD), ALU.add)
                ins.then_inc(s_Vs, 1)

            def row_max(i, g):
                dve.wait_ge(s_S, 2 * i + 1 + g)
                dve.tensor_reduce(nmax[0:L, g * HG:(g + 1) * HG],
                                  psS[0:L, g, 0:HG * L].rearrange("p (j m) -> p j m", m=L),
                                  AX.X, ALU.max, negate=True).then_inc(s_max, 1)

            stats1(0)
            k_copy(0, 0)
            v_copy(0, 0, 0)
            stats1(1)

            def step(r, i, p, u, t):
                par = u // 2
                even = u % 2 == 0
                if has(t, 0):
                    row_max(i, 0)
                if has(t, 4):
                    b = i - 4
                    if u % 2 == 0 and (t is None or b >= 4):
                        dve.wait_ge(s_R1, p - 3)
                        dve.wait_ge(d_x2[par], 16 * (r - 1))
                    dve.wait_ge(s_r2, b + 1)
                    dve.tensor_scalar(x2[0:L, par, u % 2, :], res[0:L, bass.ds(b, 1), :].rearrange("p a d -> p (a d)"),
                                      mv2[0:L, u % 2, 0:1], rs2[0:L, u % 2:u % 2 + 1],
                                      ALU.subtract, ALU.mult).then_inc(s_x2, 1)
                if has(t, 0):
                    row_max(i, 1)
                if even and (t is None or 0 <= p - 4 < NP):
                    dve.wait_ge(s_R2, p - 3)
                    dve.tensor_tensor(lg[0:L, bass.ds(2 * (p - 4), 2), :],
                                      psB[0:L, 1 - par, 0:2 * E].rearrange("p (k e) -> p k e", k=2),
                                      br_bc[0:L, :].unsqueeze(1).to_broadcast([L, 2, E]), ALU.add).then_inc(s_lg, 1)
                if has(t, 3):
                    b = i - 3
                    dve.wait_ge(s_P, b + 1)
                    h1 = res[0:L, bass.ds(b, 1), :].rearrange("p a d -> p (a d)")
                    dve.tensor_tensor(h1, psU[0:L, 128:256], h1, ALU.add).then_inc(s_h1, 1)
                if even and (t is None or p + 1 < NP):
                    k_copy(p + 1, par)
                if has(t, 3):
                    dve.wait_ge(s_h1, b + 1)
                    dve.sem_inc(s_carry_v, 1)
                    dve.bn_stats(st2[0:L, :], h1).then_inc(s_st, 1)
                if has(t, 3):
                    dve.wait_ge(s_st, b + 1)
                    dve.sem_inc(s_carry_v, 1)
                    dve.bn_aggr(mv2[0:L, (u + 1) % 2, :], st2[0:L, :]).then_inc(s_ag, 1)
                if has(t, 2):
                    dve.wait_ge(s_PV, i - 1)
                    pv = psO[0:L, 0:H * (HD + 1)].rearrange("p (h c) -> p h c", c=HD + 1)
                    dve.reciprocal(rden[0:L, :], pv[:, :, HD]).then_inc(s_rd, 1)
                    dve.wait_ge(s_rd, i - 1)
                    dve.tensor_tensor(on[0:L, :, :], pv[:, :, 0:HD],
                                      rden[0:L, :].unsqueeze(2).to_broadcast([L, H, HD]), ALU.mult).then_inc(s_on, 1)
                if not even and (t is None or p + 1 < NP):
                    v_copy(p + 1, 1 - par, par)
                if even and (t is None or p + 2 < NP):
                    stats1(p + 2)

            attention_steps(dve, step)

            rl = [0]

            def rlink(ins):
                link(ins, r_chain, rl)

            def bc(ap, shape):
                return ap.to_broadcast([L] + shape)

            dve.wait_ge(s_lg, NP)
            rlink(dve.tensor_reduce(top[0:L, :], lg[0:L, :, :], AX.X, ALU.max))
            rlink(dve.tensor_tensor(eq[0:L, :, :], lg[0:L, :, :], bc(top[0:L, :].unsqueeze(2), [B, E]), ALU.is_equal))
            rlink(dve.tensor_tensor(eq[0:L, :, :], eq[0:L, :, :], bc(rank8[0:L, :].unsqueeze(1), [B, E]), ALU.mult))
            rlink(dve.tensor_reduce(top[0:L, :], eq[0:L, :, :], AX.X, ALU.max))
            rlink(dve.tensor_tensor(onehot[0:L, :, :], bc(rank8[0:L, :].unsqueeze(1), [B, E]),
                                    bc(top[0:L, :].unsqueeze(2), [B, E]), ALU.is_equal))
            dve.tensor_copy(oh_bf[0:L, :, :], onehot[0:L, :, :].rearrange("p b e -> p e b")).then_inc(r_oh, 1)
            dve.wait_ge(r_cnt, 1)
            cum = psS[0:L, 0, 0:E * B].rearrange("p (e b) -> p e b", e=E)
            tot = psS[0:L, 1, 0:E * B].rearrange("p (e b) -> p e b", e=E)
            rlink(dve.tensor_tensor_scan(incl[0:L, :, :].rearrange("p e b -> p (e b)"), ones_f[0:L, :],
                                         psS[0:L, 1, 0:E * B], 0.0, ALU.mult, ALU.add))
            ends, ne, tiles, tinc, off, nexc = (cnt[0:L, n, :] for n in range(6))
            rlink(dve.tensor_copy(ends, incl[0:L, :, B - 1]))
            rlink(dve.tensor_copy(ne, ends))
            rlink(dve.tensor_tensor(ne[:, 1:E], ends[:, 1:E], ends[:, 0:E - 1], ALU.subtract))
            rlink(dve.tensor_tensor(cmpt[0:L, :, :], bc(ne.unsqueeze(2), [E, B - 1]),
                                    bc(tile_starts[0:L, :].unsqueeze(1), [E, B - 1]), ALU.is_gt))
            rlink(dve.tensor_reduce(tiles, cmpt[0:L, :, :], AX.X, ALU.add))
            rlink(dve.tensor_tensor_scan(tinc, ones_f[0:L, 0:E], tiles, 0.0, ALU.mult, ALU.add))
            rlink(dve.tensor_tensor(nexc, ends, ne, ALU.subtract))
            rlink(dve.tensor_tensor(off, tinc, tiles, ALU.subtract))
            rlink(dve.scalar_tensor_tensor(out=off, in0=off, scalar=128.0, in1=nexc, op0=ALU.mult, op1=ALU.subtract))
            rlink(dve.tensor_tensor(posE[0:L, :, :], incl[0:L, :, :], tot, ALU.subtract))
            rlink(dve.tensor_tensor(posE[0:L, :, :], posE[0:L, :, :], cum, ALU.add))
            rlink(dve.tensor_tensor(posE[0:L, :, :], posE[0:L, :, :], bc(off.unsqueeze(2), [E, B]), ALU.add))
            rlink(dve.tensor_tensor(posE[0:L, :, :], posE[0:L, :, :], onehot[0:L, :, :].rearrange("p b e -> p e b"), ALU.mult))
            rlink(dve.tensor_reduce(pos[0:L, :], posE[0:L, :, :].rearrange("p e b -> p b e"), AX.X, ALU.add))
            rlink(dve.tensor_copy(pos_i[0:L, 0, :], pos[0:L, :]))
            rlink(dve.tensor_scalar(pos_i[0:L, 1, :], pos_i[0:L, 0, :], 7, None, ALU.arith_shift_right))
            rlink(dve.tensor_scalar(pos_i[0:L, 2, :], pos_i[0:L, 0, :], 127, None, ALU.bitwise_and))
            rlink(dve.tensor_copy(pos_f[0:L, :, :], pos_i[0:L, 1:3, :]))
            rlink(dve.tensor_tensor(tile1h[0:L, :, :], bc(slot_iota[0:L, 0:NT].unsqueeze(1), [B, NT]),
                                    bc(pos_f[0:L, 0, :].unsqueeze(2), [B, NT]), ALU.is_equal))
            rlink(dve.tensor_scalar(tok1h[0:L, :, 0, :], tile1h[0:L, :, :], part1[0:L, 0:1], None, ALU.mult))
            rlink(dve.tensor_tensor(tok1h[0:L, :, 1, :], tile1h[0:L, :, :], bc(seq_iota[0:L, :].unsqueeze(2), [B, NT]), ALU.mult))
            QB = B // 4
            for q in range(4):
                b0 = q * QB
                dve.tensor_tensor(slot1h[0:L, b0:b0 + QB, :], bc(slot_iota[0:L, :].unsqueeze(1), [QB, 128]),
                                  bc(pos_f[0:L, 1, b0:b0 + QB].unsqueeze(2), [QB, 128]), ALU.is_equal).then_inc(r_1h, 1)
            rlink(dve.tensor_tensor(eidc[0:L, :, :], bc(tinc.unsqueeze(1), [NT, E]),
                                    bc(slot_iota[0:L, 0:NT].unsqueeze(2), [NT, E]), ALU.is_le))
            rlink(dve.tensor_reduce(eidf[0:L, :], eidc[0:L, :, :], AX.X, ALU.add))
            dve.tensor_scalar(eid[0:L, :], eidf[0:L, :], float(E - 1), None, ALU.min).then_inc(r_eid, 1)
            dve.wait_ge(r_ids, 1)
            rlink(dve.tensor_copy(idf[:, :, :], psO[:, 0:2 * NT].rearrange("p (a t) -> p a t", a=2)))
            rlink(dve.scalar_tensor_tensor(out=idg[:, :, 1], in0=idf[:, 1, :], scalar=float(L), in1=idf[:, 0, :],
                                           op0=ALU.mult, op1=ALU.add))
            rlink(dve.tensor_scalar(idf[:, 0, :], idf[:, 0, :], 0.0, float(NOROW), ALU.is_equal, ALU.mult))
            rlink(dve.scalar_tensor_tensor(out=idg[:, :, 1], in0=idg[:, :, 1], scalar=-1.0, in1=idf[:, 0, :],
                                           op0=ALU.add, op1=ALU.add))
            rlink(dve.tensor_scalar(idg[:, :, 0], idg[:, :, 1], float(N - 1), None, ALU.min))
            dve.tensor_copy(idx[:, :, :], idg[:, :, :]).then_inc(r_idx, 1)
            dve.wait_ge(r_idx, 1)

            def gather_rows(s, u):
                dve.tensor_copy(gidx[:, u:u + 1], idx[:, bass.ds(s, 1), 0]).then_inc(f_gi, 1)

            for s in range(RING):
                gather_rows(s, s)
            dve.wait_ge(r_eid, 1)
            dve.wait_ge(l_ffn, 48)

            def step(s, r, u, t):
                if t is None or t < NT:
                    e = dve.value_load(eid[0:1, bass.ds(s, 1)], min_val=0, max_val=E - 1)
                    dve.wait_ge(f_L1, s + 1)
                    if t is None or t >= 2:
                        dve.wait_ge(f_G, s - 1)
                    dve.tensor_tensor(hpre[:, u % 2, :], psS[:, u % 2, :], countbc[:, bass.ds(e * F, F)],
                                      ALU.add).then_inc(f_hp, 1)
                    if t is None or t + RING < NT:
                        gather_rows(s + RING, u)
                    dve.tensor_tensor(resid[:, u, :], xg[:, u, D:2 * D], b2_bc[:, bass.ds(e * D, D)],
                                      ALU.add).then_inc(f_rs, 1)
                if has(t, 2, NT):
                    v = (u - 2) % RING
                    if t is None or t - 2 >= RING:
                        dve.wait_ge(f_sca[v], 16 * (r + (u - 2) // RING))
                    dve.tensor_copy(sidx[:, v:v + 1], idx[:, bass.ds(s - 2, 1), 1]).then_inc(f_si, 1)
                    dve.wait_ge(f_L2, s - 1)
                    dve.wait_ge(f_rs, s - 1)
                    dve.wait_ge(f_si, s - 1)
                    dve.tensor_tensor(y_out[:, v, :], (psO if u % 2 == 0 else psU)[:, 0:D], resid[:, v, :],
                                      ALU.add).then_inc(f_y, 1)

            ffn_steps(dve, step, NT + 2)

        @block.tensor
        def _(pe):
            pe.wait_ge(s_const, N_CONST)
            pe.wait_ge(l_tokW, 16)
            pe.transpose(banks[0][0:CTX * DI, 0:128], tokW_sb[:, :], ident[:, :]).then_inc(a_wt, 1)
            pe.wait_ge(a_keyed, 1)
            pe.transpose(banks[0][:, 128:128 + EF], key[:, :], ident[0:EF, 0:EF]).then_inc(a_keyT, 1)
            pe.wait_ge(l_proj, 64)
            for n in range(4):
                ins = pe.transpose(banks[1][:, n * D:(n + 1) * D], proj_in[:, n, :], ident[:, :])
            ins.then_inc(a_w4, 1)
            pe.wait_ge(l_qkb, 32)
            for n in range(4):
                ins = pe.matmul(banks[2][:, n:n + 1], qk_row[0:1, n // 2, n % 2 * 128:n % 2 * 128 + 128],
                                ident[0:1, 0:1], start=True, stop=True)
            ins.then_inc(a_bias, 1)
            pe.wait_ge(l_x, 16)
            for t in range(8):
                bank = banks[(3 + t) % 8]
                if t >= 5:
                    pe.wait_ge(a_wts, (1, 5, 7)[t - 5])
                    pe.wait_ge(a_1h, 1)
                for i in range(4 * t, min(4 * t + 4, SEG + 1)):
                    ins = pe.transpose(bank[0:CTX * DI, (i - 4 * t) * 128:(i - 4 * t + 1) * 128],
                                       xs[:, i * DI:(i + CTX) * DI], ident[:, :])
                ins.then_inc(a_xt, 1)
            pe.wait_ge(a_pat_v, 4)
            pe.wait_ge(a_pat_s, 4)
            for c in range(NCH):
                pe.matmul(banks[(3 + c) % 8][:, 0:CH], tokWT[0:CTX * DI, :], patT[0:CTX * DI, c * CH:(c + 1) * CH],
                          start=True, stop=True).then_inc(a_y, 1)
            pe.wait_ge(a_relu, 1)
            pe.wait_ge(s_power, 3)
            for f in range(EF):
                if f % 8 == 0:
                    pe.wait_ge(a_1h, f // 8 + 1)
                ins = pe.matmul(banks[3][0:L, f * EG:(f + 1) * EG], target1h[:, f, :], power_bf[:, :], start=True, stop=True)
            ins.then_inc(a_bits, 1)
            pe.wait_ge(a_bpad, 1)
            pe.wait_ge(a_relu, NCH)
            for g in range(2):
                ins = pe.transpose(banks[5][:, g * 128:g * 128 + L], bias_pad[0:L, g * 128:(g + 1) * 128], ident[0:L, 0:L])
            ins.then_inc(a_biasT, 1)

            def transpose_h0(p, bank):
                pe.wait_ge(s_h0T, p + 1)
                for k in range(2):
                    ins = pe.transpose(psB[0:L, bank, k * D:(k + 1) * D], h0T[:, k * L:(k + 1) * L], ident[:, :])
                ins.then_inc(s_T1, 1)

            def transpose_xn(p, bank):
                pe.wait_ge(s_xn, 2 * p + 2)
                for k in range(2):
                    ins = pe.transpose(psB[:, bank, k * L:(k + 1) * L], xn[0:L, k, :], ident[0:L, 0:L])
                ins.then_inc(s_T2, 1)

            def project(p, par, bank, w, done):
                pe.wait_ge(s_xT, p + 1)
                for g in range(2):
                    ins = pe.matmul(psB[:, bank, g * PL:(g + 1) * PL], w[:, g * 128:(g + 1) * 128], xT[:, par, :],
                                    start=True, stop=True)
                ins.then_inc(done, 1)

            def values(p, par, bank):
                for k in range(2):
                    ins = pe.matmul(psB[0:L, bank, k * D:(k + 1) * D], xT[:, par, k * L:(k + 1) * L], vwT[:, :],
                                    start=True, stop=True)
                ins.then_inc(s_V, 1)

            transpose_h0(0, 0)
            transpose_xn(0, 1)
            project(0, 0, 0, kwT, s_k)
            project(0, 0, 1, qwT, s_q)
            pe.wait_ge(s_kT, 1)
            values(0, 0, 0)
            pe.wait_ge(s_qs, 2)
            transpose_h0(1, 1)
            pe.wait_ge(s_h0k, 2)
            transpose_xn(1, 1)

            def scores(i, u, g, t):
                if t is None or t >= 1:
                    pe.wait_ge(s_exp, 2 * i - 1 + g)
                pe.matmul(psS[0:L, g, 0:HG * L], qT[:, u // 2, g, u % 2 * L:u % 2 * L + L],
                          kbd[:, u, g, :], start=True, stop=True).then_inc(s_S, 1)

            def step(r, i, p, u, t):
                par = u // 2
                even = u % 2 == 0
                if has(t, 0):
                    pe.wait_ge(s_kbd, i + 1)
                    if even:
                        pe.wait_ge(s_qs, 2 * p + 2)
                    scores(i, u, 0, t)
                if has(t, 3):
                    pe.wait_ge(s_on, i - 2)
                    if t is None or t >= 4:
                        pe.wait_ge(s_h1, i - 3)
                    pe.transpose(psU[:, 0:L], on[0:L, :, :].rearrange("p h c -> p (h c)"), ident[0:L, 0:L]).then_inc(s_U, 1)
                if has(t, 0):
                    scores(i, u, 1, t)
                if even and (t is None or 0 <= p - 4 < NP):
                    pe.wait_ge(s_x2T, p - 3)
                    pe.wait_ge(s_Vs, p + 1 if t is None else min(p + 1, NP))
                    for k in range(2):
                        ins = pe.matmul(psB[0:L, 1 - par, k * E:(k + 1) * E], x2T[:, k * L:(k + 1) * L],
                                        Wr_sb[:, :], start=True, stop=True)
                    ins.then_inc(s_R2, 1)
                if even and (t is None or p + 1 < NP):
                    project(p + 1, 1 - par, par, kwT, s_k)
                if not even and (t is None or 0 <= p - 3 < NP):
                    pe.wait_ge(s_x2, 2 * p - 4)
                    pe.wait_ge(s_h0k, p + 3 if t is None else min(p + 3, NP))
                    if t is None or p >= 4:
                        pe.wait_ge(s_lg, p - 3)
                    for k in range(2):
                        ins = pe.transpose(psB[:, 1 - par, k * L:(k + 1) * L], x2[0:L, 1 - par, k, :], ident[0:L, 0:L])
                    ins.then_inc(s_R1, 1)
                if has(t, 3):
                    pe.wait_ge(s_oT, i - 2)
                    pe.matmul(psU[0:L, 128:256], oT[:, :], owT[:, :], start=True, stop=True).then_inc(s_P, 1)
                if has(t, 1):
                    pe.wait_ge(s_exp, 2 * i)
                    if t is None or t >= 2:
                        pe.wait_ge(s_PT, i - 1)
                    for h in range(H):
                        ins = pe.transpose(psT[0:L, h // HG, h % HG * L:(h % HG + 1) * L], P[0:L, (u + 1) % 2, h, :],
                                           ident[0:L, 0:L])
                    ins.then_inc(s_T, 1)
                if even and (t is None or p + 2 < NP):
                    pe.wait_ge(s_Vs, p + 1)
                    if t is None or p >= 4:
                        pe.wait_ge(s_lg, p - 3)
                    transpose_h0(p + 2, 1 - par)
                if not even and (t is None or p + 1 < NP):
                    pe.wait_ge(s_qs, 2 * p + 4)
                    values(p + 1, 1 - par, par)
                if has(t, 2):
                    pe.wait_ge(s_PT, i - 1)
                    if t is None or t >= 3:
                        pe.wait_ge(s_on, i - 2)
                    pe.wait_ge(s_Vs, p)
                    for h in range(H):
                        ins = pe.matmul(psO[0:L, h * (HD + 1):(h + 1) * (HD + 1)], PT[0:L, u % 2, h // HG, h % HG * L:(h % HG + 1) * L],
                                        V[0:L, (par + 1) % 2, u % 2, h, :], start=True, stop=True)
                    ins.then_inc(s_PV, 1)
                if even and (t is None or p + 1 < NP):
                    pe.wait_ge(s_kT, p + 2)
                    project(p + 1, 1 - par, par, qwT, s_q)
                if not even and (t is None or p + 2 < NP):
                    if t is None or p >= 3:
                        pe.wait_ge(s_x2T, p - 2)
                    transpose_xn(p + 2, 1 - par)

            pe.wait_ge(l_rows, 16 * N_ROWS)
            attention_steps(pe, step)

            pe.wait_ge(r_oh, 1)
            pe.matmul(psS[0:L, 0, 0:E * B], before[0:L, 0:L], oh_bf[0:L, :, :].rearrange("p e b -> p (e b)"),
                      start=True, stop=True)
            pe.matmul(psS[0:L, 1, 0:E * B], ones_bf[0:L, 0:L], oh_bf[0:L, :, :].rearrange("p e b -> p (e b)"),
                      start=True, stop=True).then_inc(r_cnt, 1)
            for b in range(B):
                pe.wait_ge(r_1h, b // (B // 4) + 1)
                ins = pe.matmul(psO[:, 0:2 * NT], slot1h[0:L, b, :], tok1h[0:L, b, :, :].rearrange("p a t -> p (a t)"),
                                start=(b == 0), stop=(b == B - 1))
            ins.then_inc(r_ids, 1)

            def transpose_rows(s, r, u, t):
                pe.wait_ge(f_gat[u], 16 * (r + 1))
                if t is None or t >= 2:
                    pe.wait_ge(f_xT, s - 1)
                pe.transpose(psB[:, u % 2, 0:128], xg[:, u, 0:D], ident[:, :]).then_inc(f_Xt, 1)

            pe.wait_ge(r_idx, 1)
            pe.wait_ge(r_eid, 1)
            pe.wait_ge(l_ffn, 48)
            transpose_rows(0, 0, 0, 0)

            def step(s, r, u, t):
                if t is None or t + 1 < NT:
                    transpose_rows(s + 1, r + (u + 1) // RING, (u + 1) % RING, None if t is None else t + 1)
                if t is None or t < NT:
                    e = pe.value_load(eid[0:1, bass.ds(s, 1)], min_val=0, max_val=E - 1)
                    pe.wait_ge(f_xT, s + 1)
                    if t is None or t >= 2:
                        pe.wait_ge(f_hp, s - 1)
                    pe.matmul(psS[:, u % 2, :], xgT[:, u % 2, :], W1_sb[:, bass.ds(e * F, F)],
                              start=True, stop=True).then_inc(f_L1, 1)
                if has(t, 1, NT):
                    pe.wait_ge(f_hp, s)
                    if t is None or t >= 3:
                        pe.wait_ge(f_hT, s - 2)
                    for c in range(FC):
                        ins = pe.transpose(psT[:, (u + 1) % 2, c * 128:(c + 1) * 128],
                                           hpre[:, (u + 1) % 2, c * 128:(c + 1) * 128], ident[:, :])
                    ins.then_inc(f_G, 1)
                if has(t, 2, NT):
                    e = pe.value_load(eid[0:1, bass.ds(s - 2, 1)], min_val=0, max_val=E - 1)
                    pe.wait_ge(f_hT, s - 1)
                    if t is None or t >= 4:
                        pe.wait_ge(f_y, s - 3)
                    for c in range(FC):
                        ins = pe.matmul((psO if u % 2 == 0 else psU)[:, 0:D], hT[:, u % 2, c * 128:(c + 1) * 128],
                                        W2_sb[:, bass.ds(e * F + c * D, D)], start=(c == 0), stop=(c == FC - 1))
                    ins.then_inc(f_L2, 1)

            ffn_steps(pe, step, NT + 2)


_INS = ['x', 'L0_tok_W', 'L0_tok_b', 'L0_tok_gamma', 'L0_tok_beta', 'L0_attn_edge_index', 'L0_attn_edge_attr',
        'L0_attn_q_w', 'L0_attn_q_b', 'L0_attn_k_w', 'L0_attn_k_b', 'L0_attn_v_w', 'L0_attn_v_b', 'L0_attn_o_w',
        'L0_attn_o_b', 'L0_attn_eb_w', 'L0_attn_eb_b', 'L0_ffn_Wr', 'L0_ffn_br', 'L0_ffn_W1', 'L0_ffn_b1',
        'L0_ffn_W2', 'L0_ffn_b2']


def kernel(**inputs):
    import concourse.bacc as bacc
    from concourse.bass_utils import run_bass_kernel_spmd

    nc = bacc.Bacc("TRN2", target_bir_lowering=False, num_devices=1)
    arrays, args = {}, []
    for name in _INS:
        a = np.ascontiguousarray(inputs[name])
        arrays[f"in_{name}"] = a
        args.append(nc.dram_tensor(f"in_{name}", a.shape, mybir.dt.from_np(a.dtype), kind="ExternalInput").ap())
    out = nc.dram_tensor("out_0", (N, D), F32, kind="ExternalOutput").ap()
    build(nc, *args, out)
    r = run_bass_kernel_spmd(nc, [arrays], core_ids=[0])
    return r.results[0]["out_0"].reshape(B, L, D)
```

```python
from contextlib import ExitStack

import numpy as np

import concourse.bass as bass
from concourse import mybir

F32 = mybir.dt.float32
BF16 = mybir.dt.bfloat16
I32 = mybir.dt.int32
ALU = mybir.AluOpType
ACT = mybir.ActivationFunctionType
AX = mybir.AxisListType

EPS = 1e-5
B, TF, DI = 32, 125, 23
CTX = 5
L = TF - CTX + 1
N = B * L
D = 128
H, HD = 8, 16
HB = 32
HG = 4
SEG = (L - 1) // 4
RUN = (SEG + CTX) * DI
CH = 4 * L
NCH = N // CH
PL = 2 * L
NP = B // 2
NEDGE = 8192
EF = NEDGE // 128
EG = 8
E, F = 8, 512
FC = F // 128
NT = (N + E * 127) // 128
RING = 8
NOROW = 8192


def build(nc, x, tok_W, tok_b, gamma, beta, edge_index, edge_attr, q_w, q_b, k_w, k_b, v_w, v_b, o_w, o_b,
          eb_w, eb_b, Wr, br, W1, b1, W2, b2, out):
    with ExitStack() as ctx:
        def sb(name, shape, dt=F32):
            return ctx.enter_context(nc.sbuf_tensor(name, shape, dt))

        def sem(name):
            return ctx.enter_context(nc.semaphore(name))

        rows_d = nc.dram_tensor("rows_d", [N, 2 * D], F32, kind="Internal").ap()

        psS = ctx.enter_context(nc.psum_tensor("psS", [128, 2, 512], F32))
        psT = ctx.enter_context(nc.psum_tensor("psT", [128, 2, 512], F32))
        psO = ctx.enter_context(nc.psum_tensor("psO", [128, 512], F32))
        psU = ctx.enter_context(nc.psum_tensor("psU", [128, 512], F32))
        psB = ctx.enter_context(nc.psum_tensor("psB", [128, 2, 512], F32))
        banks = [psS[:, 0, :], psS[:, 1, :], psT[:, 0, :], psT[:, 1, :], psO[:, :], psU[:, :],
                 psB[:, 0, :], psB[:, 1, :]]

        ident = sb("ident", [128, 128])
        headmask = sb("headmask", [128, HG])
        before = sb("before", [128, 128], BF16)
        ones_bf = sb("ones_bf", [128, 128], BF16)
        ones_f = sb("ones_f", [128, E * B])
        slot_iota = sb("slot_iota", [128, 128], BF16)
        seq_iota = sb("seq_iota", [128, B], BF16)
        part1 = sb("part1", [128, 1])
        rank8 = sb("rank8", [128, E])
        tile_starts = sb("tile_starts", [128, B - 1])
        col_iota = sb("col_iota", [128, EF * EG])
        minus_half = sb("minus_half", [128, 2])
        tokW_sb = sb("tokW_sb", [128, CTX * DI])
        tokWT = sb("tokWT", [128, 128])
        proj_in = sb("proj_in", [128, 4, D])
        qwT = sb("qwT", [128, H * HB])
        kwT = sb("kwT", [128, H * HB])
        vwT = sb("vwT", [128, D])
        o_perm = sb("o_perm", [128, D])
        owT = sb("owT", [128, D])
        qk_row = sb("qk_row", [1, 2, H * HB])
        qk_col = sb("qk_col", [128, 4])
        addK = sb("addK", [128, 2, L])
        col3 = sb("col3", [128, 3])
        ob_bc = sb("ob_bc", [128, D])
        vb_bc = sb("vb_bc", [128, D])
        br_bc = sb("br_bc", [128, E])
        ebw_bc = sb("ebw_bc", [128, 3 * H])
        ebb_bc = sb("ebb_bc", [128, H])
        Wr_sb = sb("Wr_sb", [128, E])
        W1_sb = sb("W1_sb", [128, E * F])
        W2_sb = sb("W2_sb", [128, E * F])
        b1_in = sb("b1_in", [E * FC, 128])
        b1T = sb("b1T", [128, E * FC])
        b2_bc = sb("b2_bc", [128, E * D])
        xs = sb("xs", [128, RUN])
        patT = sb("patT", [128, N])
        yT = sb("yT", [128, N])
        bn_st = sb("bn_st", [128, NCH, 6])
        bn_mv = sb("bn_mv", [128, 2])
        bn_r = sb("bn_r", [128, 2])
        bn_ac = sb("bn_ac", [128, 2])
        edge_i = sb("edge_i", [EF, 2, 128], I32)
        edge_f = sb("edge_f", [EF, 2, 128])
        edge_c = sb("edge_c", [EF, 2, 128])
        edge_v = sb("edge_v", [EF, 128])
        key = sb("key", [EF, 128])
        keyT = sb("keyT", [128, EF], BF16)
        power = sb("power", [128, 3, EG])
        power_bf = sb("power_bf", [128, EG], BF16)
        target1h = W1_sb[:, 0:EF * L // 2].bitcast(BF16).rearrange("p (f t) -> p f t", f=EF)
        col_hit = W2_sb[:, 0:EF * EG]
        picked = W2_sb[:, EF * EG:2 * EF * EG]
        found = sb("found", [128, 3])
        last = sb("last", [128, 3])
        last_i = sb("last_i", [128, 1], I32)
        attr = sb("attr", [128, 3])
        ebias = sb("ebias", [128, H])
        bias_pad = sb("bias_pad", [128, H * HB])
        h0T = sb("h0T", [128, PL])
        h0k = sb("h0k", [128, 2, D])
        st1 = sb("st1", [128, 2, 6])
        mv1 = sb("mv1", [128, 2, 2])
        var1 = sb("var1", [128, 2])
        rs1 = sb("rs1", [128, 2])
        nm1 = sb("nm1", [128, 2])
        xn = sb("xn", [128, 2, D])
        xT = sb("xT", [128, 2, PL])
        qT = sb("qT", [128, 2, 2, PL])
        kT = sb("kT", [128, 2, PL])
        kbd = patT[:, :].rearrange("p (s g n) -> p s g n", s=4, g=2)
        V = sb("V", [128, 2, 2, 2 * (HG * HB + HD)])
        nmax = sb("nmax", [128, H])
        P = sb("P", [128, 2, H, L])
        PT = sb("PT", [128, 2, 2, HG * L])
        den = sb("den", [128, 2, H])
        rden = sb("rden", [128, 2, H])
        oT = sb("oT", [128, L])
        st2 = sb("st2", [128, 6])
        mv2 = sb("mv2", [128, 2, 2])
        var2 = sb("var2", [128, 2])
        rs2 = sb("rs2", [128, 2])
        x2 = sb("x2", [128, 2, 2, D])
        res = sb("res", [128, B, D])
        x2T = sb("x2T", [128, PL])
        lg = sb("lg", [128, 2, E])
        top = sb("top", [128, 2, 2])
        eq = sb("eq", [128, 2, 2, E])
        oh_bf = sb("oh_bf", [128, E, B], BF16)
        scan = sb("scan", [128, 1 + E * B])
        posE = sb("posE", [128, E, B])
        cnt = sb("cnt", [128, 3, E])
        tscan = sb("tscan", [128, 1 + E])
        cmpt = sb("cmpt", [128, E, B - 1])
        pos = sb("pos", [128, B])
        pos_i = sb("pos_i", [128, 3, B], I32)
        pos_f = sb("pos_f", [128, 2, B], BF16)
        neg_slot = sb("neg_slot", [128, B])
        onehots = yT[:, :].bitcast(BF16)
        slot1h = onehots[:, 0:B * 128].rearrange("p (b n) -> p b n", b=B)
        tile1h = onehots[:, B * 128:B * (128 + NT)].rearrange("p (b n) -> p b n", b=B)
        tok1h = onehots[:, B * (128 + NT):B * (128 + 3 * NT)].rearrange("p (b a n) -> p b a n", b=B, a=2)
        idf = sb("idf", [128, 2, NT])
        idg = sb("idg", [128, 2, NT])
        idx = sb("idx", [128, 2, NT], I32)
        eidc = sb("eidc", [128, NT, E])
        eidf = sb("eidf", [128, NT])
        eid = sb("eid", [128, NT], I32)
        xg = sb("xg", [128, RING, 2 * D])
        gidx = sb("gidx", [128, RING], I32)
        sidx = sb("sidx", [128, RING], I32)
        xgT = sb("xgT", [128, 2, 128])
        W1_tile = sb("W1_tile", [128, 2, F])
        hpre = sb("hpre", [128, 2, F])
        hT = sb("hT", [128, 2, F])
        resid = sb("resid", [128, RING, D])
        y_out = sb("y_out", [128, RING, D])

        l_x, l_tokW, l_proj, l_edges, l_cols, l_rows, l_ffn, l_attr, l_qkb = map(
            sem, "l_x l_tokW l_proj l_edges l_cols l_rows l_ffn l_attr l_qkb".split())
        a_operm, s_kzero = sem("a_operm"), sem("s_kzero")
        s_power, s_colio = sem("s_power"), sem("s_colio")
        a_keyT, a_1h, a_bits = sem("a_keyT"), sem("a_1h"), sem("a_bits")
        s_const = sem("s_const")
        s_rowset = sem("s_rowset")
        a_wt, a_w4, a_xt, a_y, a_bias = map(sem, "a_wt a_w4 a_xt a_y a_bias".split())
        a_wts, a_pat, a_relu, a_bst = map(sem, "a_wts a_pat a_relu a_bst".split())
        a_var, a_rstd, a_pool, a_ac = map(sem, "a_var a_rstd a_pool a_ac".split())
        a_chain, a_keyed, a_biasT, a_lasti, a_bpad, a_addk = map(
            sem, "a_chain a_keyed a_biasT a_lasti a_bpad a_addk".split())
        s_S, s_T, s_PV, s_P = map(sem, "s_S s_T s_PV s_P".split())
        s_T1, s_T2, s_k, s_q, s_V, s_R1, s_R2 = map(sem, "s_T1 s_T2 s_k s_q s_V s_R1 s_R2".split())
        s_max, s_rd, s_Pn, s_h1, s_st, s_ag, s_x2 = map(
            sem, "s_max s_rd s_Pn s_h1 s_st s_ag s_x2".split())
        s_kT, s_Vs, s_lg, s_st1, s_ag1 = map(sem, "s_kT s_Vs s_lg s_st1 s_ag1".split())
        s_exp, s_PT, s_oT, s_h0T, s_h0k, s_xT, s_qs, s_x2T = map(
            sem, "s_exp s_PT s_oT s_h0T s_h0k s_xT s_qs s_x2T".split())
        s_v1, s_r1, s_nm1, s_xn, s_h0b, s_kbd, s_v2, s_r2 = map(
            sem, "s_v1 s_r1 s_nm1 s_xn s_h0b s_kbd s_v2 s_r2".split())
        s_carry_p, s_carry_v = sem("s_carry_p"), sem("s_carry_v")
        s_top, s_first, r_zero, r_tile, r_seq = map(sem, "s_top s_first r_zero r_tile r_seq".split())
        d_x2, d_res = [sem("d_x2_0"), sem("d_x2_1")], sem("d_res")
        r_oh, r_cnt, r_1h, r_ids, r_idx, r_eid, r_chain = map(
            sem, "r_oh r_cnt r_1h r_ids r_idx r_eid r_chain".split())
        f_gat = [sem(f"f_gat{u}") for u in range(RING)]
        f_sca = [sem(f"f_sca{u}") for u in range(RING)]
        f_gi, f_si, f_Xt, f_xT, f_L1, f_hp, f_hT, f_L2, f_rs, f_y = map(
            sem, "f_gi f_si f_Xt f_xT f_L1 f_hp f_hT f_L2 f_rs f_y".split())
        s_Pn_last = sem("s_Pn_last")
        r_slot, r_1ha = sem("r_slot"), sem("r_1ha")
        f_b1, f_b1T, f_w1 = sem("f_b1"), sem("f_b1T"), sem("f_w1")

        N_CONST = 20
        SLOT_GROUPS = ((0, 8), (8, 16), (16, 22))
        ACT_SEQ = SLOT_GROUPS[-1][1]
        N_COLS, N_ROWS = 3, 7

        DRAIN = 9
        PEEL, TAIL = 3, 2

        def attention_steps(eng, step):
            for i in range(4 * PEEL):
                step(i // 4, i, i // 2, i % 4, i)
            with eng.Fori(PEEL, B // 4 - TAIL) as body:
                for u in range(4):
                    step(body, 4 * body + u, 2 * body + u // 2, u, None)
            for i in range(B - 4 * TAIL, B + DRAIN):
                step(i // 4, i, i // 2, i % 4, i)

        BODIES = (NT - 1) // RING - 2

        def ffn_steps(eng, step, end):
            for s in range(RING + 1):
                step(s, s // RING, s % RING, s)
            with eng.Fori(1, 1 + BODIES) as r:
                for u in range(1, RING):
                    step(RING * r + u, r, u, None)
                step(RING * r + RING, r + 1, 0, None)
            for s in range(RING * (1 + BODIES) + 1, end):
                step(s, s // RING, s % RING, s)

        def has(t, back, n=B):
            return t is None or 0 <= t - back < n

        block = ctx.enter_context(nc.Block())

        @block.sync
        def _(sp):
            sp.dma_start(edge_i[:, :, :], edge_index.rearrange("a (f p) -> f a p", p=128)).then_inc(l_edges, 16)
            sp.dma_start(tokW_sb[:, :], tok_W).then_inc(l_tokW, 16)
            for n, w in enumerate((q_w, k_w, v_w, o_w)):
                sp.dma_start(proj_in[:, n, :], w).then_inc(l_proj, 16)
            for n, v in enumerate((tok_b, gamma, beta)):
                sp.dma_start(col3[:, n:n + 1], v.rearrange("(p a) -> p a", a=1)).then_inc(l_cols, 16)
            sp.wait_ge(s_rowset, 2)
            for n, v in enumerate((q_b, k_b)):
                sp.dma_start(qk_row[0:1, n, :].rearrange("p (h c) -> p h c", c=HB)[:, :, 0:HD],
                             v.rearrange("(a h c) -> a h c", a=1, c=HD)).then_inc(l_qkb, 16)
            for t, v in ((ob_bc, o_b), (vb_bc, v_b), (br_bc, br), (ebb_bc, eb_b)):
                sp.dma_start(t[:, :], v.partition_broadcast(128)).then_inc(l_rows, 16)
            sp.dma_start(ebw_bc[:, :], eb_w.rearrange("h k -> (h k)").partition_broadcast(128)).then_inc(l_rows, 16)
            sp.dma_start(b2_bc[:, :], b2.rearrange("e d -> (e d)").partition_broadcast(128)).then_inc(l_rows, 16)
            sp.dma_start(Wr_sb[:, :], Wr).then_inc(l_rows, 16)
            sp.wait_ge(l_attr, 16)
            sp.dma_start(W1_sb[:, :].rearrange("d (e f) -> d e f", e=E), W1.rearrange("e d f -> d e f")).then_inc(l_ffn, 16)
            sp.dma_start(W2_sb[:, :].rearrange("h (g o) -> h g o", o=D),
                         W2.rearrange("e (c h) o -> h (e c) o", h=128)).then_inc(l_ffn, 16)
            sp.dma_start(b1_in[:, :], b1.rearrange("e (c h) -> (e c) h", h=128)).then_inc(l_ffn, 16)
            rows_v = rows_d.rearrange("(b n) d -> n b d", n=L)
            with sp.Fori(0, NP // 2) as r:
                for par in range(2):
                    b = 4 * r + 2 * par
                    sp.wait_ge(s_x2, b + 2)
                    sp.dma_start(rows_v[:, bass.ds(b, 2), 0:D], x2[0:L, par, :, :]).then_inc(d_x2[par], 16)
                    sp.dma_start(rows_v[:, bass.ds(b, 2), D:2 * D], res[0:L, bass.ds(b, 2), :]).then_inc(d_res, 16)

        @block.gpsimd
        def _(pool):
            pool.memset(qk_row[:, :, :], 0.0).then_inc(s_rowset, 1)
            pool.wait_ge(s_rowset, 1)
            pool.memset(qk_row[:, 0, :].rearrange("p (h c) -> p h c", c=HB)[:, :, HD:HD + 1], 4.0).then_inc(s_rowset, 1)
            pool.memset(ident[:, :], 0.0).then_inc(s_const, 1)
            pool.memset(headmask[:, :], 1.0).then_inc(s_const, 1)
            pool.memset(before[:, :], 1.0).then_inc(s_const, 1)
            pool.memset(ones_bf[:, :], 1.0).then_inc(s_const, 1)
            pool.memset(ones_f[:, :], 1.0).then_inc(s_const, 1)
            pool.memset(minus_half[:, :], -0.5).then_inc(s_const, 1)
            pool.memset(qwT[:, :], 0.0).then_inc(s_const, 1)
            pool.memset(kwT[:, :], 0.0).then_inc(s_const, 1)
            pool.memset(bias_pad[:, :], 0.0).then_inc(s_const, 1)
            pool.memset(V[:, :, :, :], 0.0).then_inc(s_const, 1)
            fl = dict(allow_small_or_imprecise_dtypes=True)
            pool.iota(slot_iota[:, :], pattern=[[1, 128]], base=0, channel_multiplier=0, **fl).then_inc(s_const, 1)
            pool.iota(seq_iota[:, :], pattern=[[1, B]], base=0, channel_multiplier=0, **fl).then_inc(s_const, 1)
            pool.iota(part1[:, :], pattern=[[0, 1]], base=1, channel_multiplier=1, **fl).then_inc(s_const, 1)
            pool.iota(rank8[:, :], pattern=[[-1, E]], base=E, channel_multiplier=0, **fl).then_inc(s_const, 1)
            pool.iota(tile_starts[:, :], pattern=[[128, B - 1]], base=0, channel_multiplier=0, **fl).then_inc(s_const, 1)
            pool.iota(power[:, 0, :], pattern=[[-128 // EG, EG]], base=127, channel_multiplier=1, **fl).then_inc(s_const, 1)
            pool.wait_ge(s_const, 16)
            pool.affine_select(out=ident[:, :], in_=ident[:, :], compare_op=ALU.not_equal, fill=1.0, base=0,
                               pattern=[[-1, 128]], channel_multiplier=1).then_inc(s_const, 1)
            pool.affine_select(out=before[:, :], in_=before[:, :], compare_op=ALU.is_ge, fill=0.0, base=-1,
                               pattern=[[1, 128]], channel_multiplier=-1).then_inc(s_const, 1)
            pool.affine_select(out=headmask[:, :], in_=headmask[:, :], compare_op=ALU.is_ge, fill=0.0, base=0,
                               pattern=[[-HB, HG]], channel_multiplier=1).then_inc(s_const, 1)
            pool.wait_ge(s_const, 19)
            pool.affine_select(out=headmask[:, :], in_=headmask[:, :], compare_op=ALU.is_ge, fill=0.0, base=HB - 1,
                               pattern=[[HB, HG]], channel_multiplier=-1).then_inc(s_const, 1)
            pool.affine_select(out=power[:, 0, :], in_=power[:, 0, :], compare_op=ALU.is_ge, fill=0.0, base=0,
                               pattern=[[-128 // EG, EG]], channel_multiplier=1).then_inc(s_power, 1)
            pool.wait_ge(s_power, 1)
            pool.affine_select(out=power[:, 0, :], in_=power[:, 0, :], compare_op=ALU.is_ge, fill=0.0, base=128 // EG - 1,
                               pattern=[[128 // EG, EG]], channel_multiplier=-1).then_inc(s_power, 1)
            pool.memset(scan[:, 0:1], 0.0).then_inc(r_zero, 1)
            pool.memset(tscan[:, 0:1], 0.0).then_inc(r_zero, 1)
            pool.iota(col_iota[:, :], pattern=[[1, EF * EG]], base=1, channel_multiplier=0, **fl).then_inc(s_colio, 1)

            pool.wait_ge(a_y, NCH)
            pool.memset(patT[:, :], 0.0).then_inc(s_kzero, 1)
            pool.wait_ge(a_var, 1)
            pool.tensor_scalar(bn_r[:, 0:1], bn_mv[:, 1:2], 1.0, EPS, ALU.mult, ALU.add).then_inc(a_pool, 1)
            pool.wait_ge(a_pool, 1)
            pool.tensor_tensor(bn_r[:, 1:2], bn_r[:, 0:1], minus_half[:, 0:1], ALU.pow).then_inc(a_rstd, 1)
            pool.wait_ge(a_lasti, 1)
            pool.indirect_dma_start(attr[0:L, :], None, edge_attr, bass.IndirectOffsetOnAxis(last_i[0:L, 0:1], 0),
                                    bounds_check=NEDGE - 1, oob_is_err=False).then_inc(l_attr, 16)

            def norm1(p):
                pool.wait_ge(s_ag1, p + 1)
                pool.sem_inc(s_carry_p, 1)
                pool.tensor_scalar(var1[0:L, :], mv1[0:L, :, 1], 1.0, EPS, ALU.mult, ALU.add).then_inc(s_v1, 1)
                pool.wait_ge(s_v1, p + 1)
                pool.tensor_tensor(rs1[0:L, :], var1[0:L, :], minus_half[0:L, :], ALU.pow).then_inc(s_r1, 1)
                pool.wait_ge(s_r1, p + 1)
                pool.tensor_tensor(nm1[0:L, :], mv1[0:L, :, 0], rs1[0:L, :], ALU.mult).then_inc(s_nm1, 1)
                pool.wait_ge(s_nm1, 2 * p + 1)
                pool.sem_inc(s_carry_p, 1)
                pool.tensor_scalar(nm1[0:L, :], nm1[0:L, :], -1.0, 0.0, ALU.mult, ALU.add).then_inc(s_nm1, 1)
                pool.wait_ge(s_nm1, 2 * p + 2)
                if not (isinstance(p, int) and p == 0):
                    pool.wait_ge(s_T2, p)
                pool.sem_inc(s_carry_p, 1)
                for k in range(2):
                    pool.tensor_scalar(xn[0:L, k, :], h0k[0:L, k, :], rs1[0:L, k:k + 1], nm1[0:L, k:k + 1],
                                       ALU.mult, ALU.add).then_inc(s_xn, 1)
                pool.tensor_tensor(res[0:L, bass.ds(2 * p, 2), :], h0k[0:L, :, :],
                                   ob_bc[0:L, :].unsqueeze(1).to_broadcast([L, 2, D]), ALU.add).then_inc(s_h0b, 1)

            def normalize(i, par):
                pool.wait_ge(s_rd, i + 1)
                pool.tensor_tensor(P[0:L, par, :, :], P[0:L, par, :, :],
                                   rden[0:L, par, :].unsqueeze(2).to_broadcast([L, H, L]), ALU.mult).then_inc(s_Pn, 1)

            def rstd2(b, par):
                pool.wait_ge(s_ag, b + 1)
                pool.sem_inc(s_carry_p, 1)
                pool.tensor_scalar(var2[0:L, par:par + 1], mv2[0:L, par, 1:2], 1.0, EPS, ALU.mult, ALU.add).then_inc(s_v2, 1)
                pool.wait_ge(s_v2, b + 1)
                pool.tensor_tensor(rs2[0:L, par:par + 1], var2[0:L, par:par + 1], minus_half[0:L, 0:1], ALU.pow).then_inc(s_r2, 1)

            pool.wait_ge(l_rows, 16 * N_ROWS)
            norm1(0)
            norm1(1)

            def step(r, i, p, u, t):
                if has(t, 1) and t != B:
                    normalize(i - 1, (u + 1) % 2)
                if u % 2 == 1 and (t is None or p + 2 < NP):
                    norm1(p + 2)
                if has(t, 3):
                    rstd2(i - 3, (u + 1) % 2)

            attention_steps(pool, step)

            pool.wait_ge(r_tile, 1)
            for b0 in (0, B // 2):
                pool.tensor_tensor(tok1h[0:L, b0:b0 + B // 2, 1, :], tile1h[0:L, b0:b0 + B // 2, :],
                                   seq_iota[0:L, b0:b0 + B // 2].unsqueeze(2).to_broadcast([L, B // 2, NT]),
                                   ALU.mult).then_inc(r_seq, 1)

            pool.wait_ge(d_res, 16 * NP)
            for par in range(2):
                pool.wait_ge(d_x2[par], 16 * (NP // 2))
            for s in range(RING):
                pool.wait_ge(r_idx, 1)
                pool.indirect_dma_start(xg[:, s, :], None, rows_d, bass.IndirectOffsetOnAxis(idx[:, 0, s:s + 1], 0),
                                        bounds_check=N - 1, oob_is_err=False).then_inc(f_gat[s], 16)

            def step(s, r, u, t):
                if t is None or t + RING < NT:
                    pool.wait_ge(f_gi, s + 1)
                    pool.wait_ge(f_rs, s + 1)
                    pool.sem_inc(s_carry_p, 1)
                    pool.indirect_dma_start(xg[:, u, :], None, rows_d, bass.IndirectOffsetOnAxis(gidx[:, u:u + 1], 0),
                                            bounds_check=N - 1, oob_is_err=False).then_inc(f_gat[u], 16)
                if has(t, 1, NT):
                    v = (u - 1) % RING
                    pool.wait_ge(f_y, s)
                    pool.sem_inc(s_carry_p, 1)
                    pool.indirect_dma_start(out, bass.IndirectOffsetOnAxis(sidx[:, v:v + 1], 0), y_out[:, v, :], None,
                                            bounds_check=N - 1, oob_is_err=False).then_inc(f_sca[v], 16)

            ffn_steps(pool, step, NT + 1)
            for u in range(RING):
                pool.wait_ge(f_sca[u], 16 * len(range(u, NT, RING)))

        @block.scalar
        def _(act):
            act.dma_start(xs[:, :], bass.AP(x.tensor, 0, [[TF * DI, B], [SEG * DI, 4], [1, RUN]])).then_inc(l_x, 16)
            for t in range(8):
                act.wait_ge(a_xt, t + 1)
                bank = banks[(3 + t) % 8]
                ni = min(4, SEG - 4 * t)
                dst = patT[0:CTX * DI, :].rearrange("p (b l) -> p b l", l=L)[:, :, 0:4 * SEG] \
                    .rearrange("p b (j i) -> p i b j", i=SEG)[:, 4 * t:4 * t + ni]
                src = bank[0:CTX * DI, 0:128 * ni].rearrange("p (i b j) -> p i b j", i=ni, j=4)
                act.activation(dst, src, ACT.Identity).then_inc(a_pat, 1)
            act.activation(patT[0:CTX * DI, :].rearrange("p (b l) -> p b l", l=L)[:, :, L - 1],
                           bank[0:CTX * DI, 256:384].rearrange("p (b j) -> p b j", j=4)[:, :, 3],
                           ACT.Identity).then_inc(a_pat, 1)
            act.wait_ge(l_cols, 16 * N_COLS)
            for c in range(NCH):
                act.wait_ge(a_y, c + 1)
                act.activation(yT[:, c * CH:(c + 1) * CH], banks[(3 + c) % 8][:, 0:CH], ACT.Relu,
                               bias=col3[:, 0:1]).then_inc(a_relu, 1)

            def batch_norm(p):
                if not (isinstance(p, int) and p == 0):
                    act.wait_ge(s_T1, p)
                act.activation(h0T[:, :], yT[:, bass.ds(p * PL, PL)], ACT.Identity, bias=bn_ac[:, 1:2],
                               scale=bn_ac[:, 0:1]).then_inc(s_h0T, 1)

            def h0_copy(p, bank):
                act.wait_ge(s_T1, p + 1)
                if not (isinstance(p, int) and p == 0):
                    act.wait_ge(s_h0b, p)
                act.activation(h0k[0:L, :, :], bank[0:L, 0:2 * D].rearrange("p (k d) -> p k d", k=2),
                               ACT.Identity).then_inc(s_h0k, 1)

            def xT_copy(p, par, bank):
                act.wait_ge(s_T2, p + 1)
                act.activation(xT[:, par, :], psB[:, bank, 0:PL], ACT.Identity).then_inc(s_xT, 1)

            def q_copy(p, par, bank):
                act.wait_ge(s_q, p + 1)
                for g in range(2):
                    act.activation(qT[:, par, g, :], psB[:, bank, g * PL:(g + 1) * PL], ACT.Identity,
                                   bias=qk_col[:, g:g + 1], scale=0.25).then_inc(s_qs, 1)

            act.wait_ge(a_ac, 1)
            act.wait_ge(a_wts, 7)
            batch_norm(0)
            h0_copy(0, psB[:, 0, :])
            batch_norm(1)
            xT_copy(0, 0, 1)
            h0_copy(1, psT[:, 0, :])
            batch_norm(2)
            q_copy(0, 0, 1)

            def step(r, i, p, u, t):
                par = u // 2
                even = u % 2 == 0
                if has(t, 3):
                    act.wait_ge(s_PV, i - 2)
                    act.activation(oT[:, :], psO[:, 0:L], ACT.Identity).then_inc(s_oT, 1)
                if even and (t is None or p + 1 < NP):
                    xT_copy(p + 1, 1 - par, par)
                if has(t, 0):
                    for h in range(H):
                        if h % HG == 0:
                            act.wait_ge(s_max, 2 * i + 1 + h // HG)
                        ins = act.activation(P[0:L, u % 2, h, :], psS[0:L, h // HG, h % HG * L:(h % HG + 1) * L],
                                             ACT.Exp, bias=nmax[0:L, h:h + 1], accum_out=den[0:L, u % 2, h:h + 1])
                        if h % HG == HG - 1:
                            ins.then_inc(s_exp, 1)
                if not even and (t is None or 0 <= p - 3 < NP):
                    act.wait_ge(s_R1, p - 2)
                    act.activation(x2T[:, :], psB[:, 1 - par, 0:PL], ACT.Identity).then_inc(s_x2T, 1)
                if has(t, 1):
                    act.wait_ge(s_T, i)
                    act.activation(PT[0:L, (u + 1) % 2, :, :], psT[0:L, :, 0:HG * L], ACT.Identity).then_inc(s_PT, 1)
                if even and (t is None or p + 2 < NP):
                    h0_copy(p + 2, psB[:, 1 - par, :])
                if even and (t is None or p + 3 < NP):
                    batch_norm(p + 3)
                if even and (t is None or p + 1 < NP):
                    q_copy(p + 1, 1 - par, par)

            attention_steps(act, step)

            def W1_copy(s, u, t):
                e = act.value_load(eid[0:1, bass.ds(s, 1)], min_val=0, max_val=E - 1)
                if t is None or t >= 2:
                    act.wait_ge(f_L1, s - 1)
                act.activation(W1_tile[:, u % 2, :], W1_sb[:, bass.ds(e * F, F)], ACT.Identity).then_inc(f_w1, 1)

            def xgT_copy(s, u, t):
                act.wait_ge(f_Xt, s + 1)
                if t is None or t >= 2:
                    act.wait_ge(f_L1, s - 1)
                act.activation(xgT[:, u % 2, :], psB[:, u % 2, 0:128], ACT.Identity).then_inc(f_xT, 1)

            act.wait_ge(f_b1, 1)
            act.activation(b1T[:, :], psT[:, 0, 0:E * FC], ACT.Identity).then_inc(f_b1T, 1)
            act.wait_ge(r_slot, 1)
            act.activation(neg_slot[0:L, :], pos_f[0:L, 1, :], ACT.Identity, scale=-1.0).then_inc(r_1ha, 1)
            act.wait_ge(r_1ha, 1)
            for b in range(ACT_SEQ, B):
                act.activation(slot1h[0:L, b, :], slot_iota[0:L, :], ACT.Square, bias=neg_slot[0:L, b:b + 1]).then_inc(r_1ha, 1)
            act.wait_ge(r_1ha, B - ACT_SEQ + 1)
            act.activation(slot1h[0:L, ACT_SEQ:B, :], slot1h[0:L, ACT_SEQ:B, :], ACT.Relu, bias=ones_f[0:L, 0:1],
                           scale=-1.0).then_inc(r_1ha, 1)
            act.wait_ge(r_eid, 1)
            W1_copy(0, 0, 0)
            xgT_copy(0, 0, 0)

            def step(s, r, u, t):
                if t is None or t + 1 < NT:
                    W1_copy(s + 1, (u + 1) % RING, None if t is None else t + 1)
                    xgT_copy(s + 1, (u + 1) % RING, None if t is None else t + 1)
                act.wait_ge(f_hp, s + 1)
                if t is None or t >= 2:
                    act.wait_ge(f_L2, s - 1)
                act.activation(hT[:, u % 2, :], hpre[:, u % 2, :], ACT.Relu).then_inc(f_hT, 1)

            ffn_steps(act, step, NT)

        @block.vector
        def _(dve):
            links = [0]

            def link(ins, chain=a_chain, count=links):
                count[0] += 1
                ins.then_inc(chain, 1)
                dve.wait_ge(chain, count[0])

            dve.wait_ge(l_edges, 16)
            dve.wait_ge(s_const, N_CONST)
            link(dve.tensor_copy(edge_f[:, :, :], edge_i[:, :, :]))
            link(dve.tensor_scalar(edge_c[:, :, :], edge_f[:, :, :], 0.0, float(L - 1), ALU.max, ALU.min))
            link(dve.tensor_tensor(edge_c[:, :, :], edge_c[:, :, :], edge_f[:, :, :], ALU.is_equal))
            link(dve.tensor_tensor(edge_v[:, :], edge_c[:, 0, :], edge_c[:, 1, :], ALU.mult))
            dve.scalar_tensor_tensor(out=key[:, :], in0=edge_f[:, 1, :], scalar=1.0, in1=edge_v[:, :],
                                     op0=ALU.add, op1=ALU.mult).then_inc(a_keyed, 1)
            dve.wait_ge(s_power, 2)
            link(dve.tensor_copy(power[:, 1, :].bitcast(I32), power[:, 0, :]))
            link(dve.tensor_scalar(power[:, 2, :].bitcast(I32), power[:, 1, :].bitcast(I32), 23, None, ALU.logical_shift_left))
            dve.tensor_copy(power_bf[:, :], power[:, 2, :]).then_inc(s_power, 1)
            dve.wait_ge(a_wt, 1)
            dve.wait_ge(a_keyT, 1)
            link(dve.tensor_copy(keyT[:, :], banks[0][:, 128:128 + EF]))
            dve.tensor_copy(tokWT[0:CTX * DI, :], banks[0][0:CTX * DI, 0:128]).then_inc(a_wts, 1)

            def target_onehots(c):
                dve.tensor_tensor(target1h[:, 8 * c:8 * c + 8, :],
                                  slot_iota[:, 1:L + 1].unsqueeze(1).to_broadcast([128, 8, L]),
                                  keyT[:, 8 * c:8 * c + 8].unsqueeze(2).to_broadcast([128, 8, L]),
                                  ALU.is_equal).then_inc(a_1h, 1)

            target_onehots(0)
            dve.wait_ge(l_proj, 64)
            dve.tensor_copy(o_perm[:, :].rearrange("p (j a c) -> p a j c", j=HG, a=2),
                            proj_in[:, 3, :].rearrange("p (a j c) -> p a j c", a=2, j=HG)).then_inc(a_operm, 1)
            target_onehots(1)
            dve.wait_ge(a_w4, 1)
            for n, w in enumerate((qwT, kwT)):
                dve.tensor_copy(w[:, :].rearrange("p (h c) -> p h c", c=HB)[:, :, 0:HD],
                                banks[1][:, n * D:(n + 1) * D].rearrange("p (h c) -> p h c", c=HD)).then_inc(a_wts, 1)
            dve.tensor_copy(vwT[:, :], banks[1][:, 2 * D:3 * D]).then_inc(a_wts, 1)
            dve.tensor_copy(owT[:, :], banks[1][:, 3 * D:4 * D]).then_inc(a_wts, 1)
            target_onehots(2)
            dve.wait_ge(a_bias, 1)
            dve.tensor_scalar(qk_col[:, 0:2], banks[2][:, 0:2], 0.25, None, ALU.mult).then_inc(a_wts, 1)
            dve.tensor_copy(qk_col[:, 2:4], banks[2][:, 2:4]).then_inc(a_wts, 1)
            target_onehots(3)
            target_onehots(4)
            for c in range(NCH):
                dve.wait_ge(a_relu, c + 1)
                dve.bn_stats(bn_st[:, c, :], yT[:, c * CH:(c + 1) * CH]).then_inc(a_bst, 1)
                if c % 2 == 1 and c < 7:
                    target_onehots(5 + c // 2)
            dve.wait_ge(a_bst, NCH)
            dve.bn_aggr(bn_mv[:, :], bn_st[:, :, :].rearrange("p a b -> p (a b)")).then_inc(a_var, 1)
            dve.wait_ge(a_rstd, 1)
            dve.wait_ge(l_cols, 16 * N_COLS)
            link(dve.tensor_tensor(bn_ac[:, 0:1], bn_r[:, 1:2], col3[:, 1:2], ALU.mult))
            link(dve.tensor_tensor(bn_r[:, 0:1], bn_mv[:, 0:1], bn_ac[:, 0:1], ALU.mult))
            dve.tensor_tensor(bn_ac[:, 1:2], col3[:, 2:3], bn_r[:, 0:1], ALU.subtract).then_inc(a_ac, 1)
            bits = banks[3][0:L, 0:EF * EG]
            dve.wait_ge(a_bits, 1)
            dve.wait_ge(s_colio, 1)
            link(dve.scalar_tensor_tensor(out=col_hit[0:L, :], in0=bits, scalar=0.0, in1=col_iota[0:L, :],
                                          op0=ALU.is_gt, op1=ALU.mult))
            link(dve.tensor_reduce(found[0:L, 0:1], col_hit[0:L, :], AX.X, ALU.max))
            link(dve.scalar_tensor_tensor(out=picked[0:L, :], in0=col_iota[0:L, :], scalar=found[0:L, 0:1], in1=bits,
                                          op0=ALU.is_equal, op1=ALU.mult, accum_out=found[0:L, 1:2]))
            link(dve.tensor_scalar(found[0:L, 2:3].bitcast(I32), found[0:L, 1:2].bitcast(I32), 23, None,
                                   ALU.arith_shift_right))
            link(dve.tensor_copy(last[0:L, 0:1], found[0:L, 2:3].bitcast(I32)))
            link(dve.scalar_tensor_tensor(out=last[0:L, 0:1], in0=found[0:L, 0:1], scalar=float(128 // EG),
                                          in1=last[0:L, 0:1], op0=ALU.mult, op1=ALU.add))
            link(dve.tensor_scalar(last[0:L, 1:2], found[0:L, 0:1], 0.0, None, ALU.is_gt))
            dve.tensor_scalar(last_i[0:L, :], last[0:L, 0:1], -127.0 - 128 // EG, 0.0, ALU.add, ALU.max).then_inc(a_lasti, 1)
            def stats1(p):
                dve.wait_ge(s_h0k, p + 1)
                if not (isinstance(p, int) and p == 0):
                    dve.wait_ge(s_nm1, 2 * p)
                for k in range(2):
                    dve.bn_stats(st1[0:L, k, :], h0k[0:L, k, :]).then_inc(s_st1, 1)
                dve.wait_ge(s_st1, 2 * p + 2)
                if not (isinstance(p, int) and p == 0):
                    dve.wait_ge(s_xn, 2 * p)
                dve.sem_inc(s_carry_v, 1)
                for k in range(2):
                    ins = dve.bn_aggr(mv1[0:L, k, :], st1[0:L, k, :])
                ins.then_inc(s_ag1, 1)

            stats1(0)
            dve.wait_ge(l_attr, 16)
            dve.wait_ge(l_rows, 16 * N_ROWS)
            for n in range(3):
                link(dve.scalar_tensor_tensor(
                    out=ebias[0:L, :], in0=ebw_bc[0:L, :].rearrange("p (h k) -> p h k", k=3)[:, :, n],
                    scalar=attr[0:L, n:n + 1], in1=(ebb_bc if n == 0 else ebias)[0:L, :], op0=ALU.mult, op1=ALU.add))
            dve.tensor_scalar(bias_pad[0:L, :].rearrange("p (h c) -> p h c", c=HB)[:, :, HD], ebias[0:L, :],
                              last[0:L, 1:2], None, ALU.mult).then_inc(a_bpad, 1)
            dve.wait_ge(a_biasT, 1)
            for g in range(2):
                ins = dve.tensor_scalar(addK[:, g, :], banks[5][:, g * 128:g * 128 + L], qk_col[:, 2 + g:3 + g], None, ALU.add)
            ins.then_inc(a_addk, 1)
            dve.wait_ge(a_addk, 1)

            def k_copy(p, bank):
                dve.wait_ge(s_k, p + 1)
                if not (isinstance(p, int) and p == 0):
                    dve.wait_ge(s_kbd, 2 * p)
                dve.tensor_tensor(kT[:, :, :].rearrange("p g (k m) -> p g k m", m=L),
                                  psB[:, bank, 0:2 * PL].rearrange("p (g k m) -> p g k m", g=2, m=L),
                                  addK[:, :, :].unsqueeze(2).to_broadcast([128, 2, 2, L]), ALU.add).then_inc(s_kT, 1)

            def key_blocks(p, par, which):
                dve.wait_ge(s_kT, p + 1)
                if not (isinstance(p, int) and p < 2):
                    dve.wait_ge(s_S, 4 * p - 4)
                for j in which:
                    rows = slice(j * HB, (j + 1) * HB)
                    ins = dve.tensor_copy(kbd[rows, 2 * par:2 * par + 2, :, j * L:(j + 1) * L],
                                          kT[rows, :, :].rearrange("p g (k m) -> p k g m", m=L))
                ins.then_inc(s_kbd, len(which) // 2)

            def v_copy(p, par, bank):
                dve.wait_ge(s_V, p + 1)
                if not (isinstance(p, int) and p < 2):
                    dve.wait_ge(s_PV, 2 * p - 2)
                for k in range(2):
                    halves = V[0:L, par, k, :].rearrange("p (a x) -> p a x", a=2)[:, :, 0:HG * HB]
                    ins = dve.tensor_tensor(halves.rearrange("p a (j c) -> p a j c", c=HB)[:, :, :, 0:HD],
                                            psB[0:L, bank, k * D:(k + 1) * D].rearrange("p (a j c) -> p a j c", a=2, j=HG),
                                            vb_bc[0:L, :].rearrange("p (a j c) -> p a j c", a=2, j=HG), ALU.add)
                ins.then_inc(s_Vs, 1)

            def expert_first(q):
                dve.wait_ge(s_lg, q + 1)
                dve.tensor_reduce(top[0:L, 0, :], lg[0:L, :, :], AX.X, ALU.max).then_inc(s_top, 1)
                dve.wait_ge(s_top, 3 * q + 1)
                dve.tensor_tensor(eq[0:L, 0, :, :], lg[0:L, :, :], top[0:L, 0, :].unsqueeze(2).to_broadcast([L, 2, E]),
                                  ALU.is_equal).then_inc(s_top, 1)
                dve.wait_ge(s_top, 3 * q + 2)
                dve.tensor_tensor(eq[0:L, 1, :, :], eq[0:L, 0, :, :], rank8[0:L, :].unsqueeze(1).to_broadcast([L, 2, E]),
                                  ALU.mult).then_inc(s_top, 1)

            def expert_second(q):
                dve.wait_ge(s_top, 3 * q + 3)
                dve.tensor_reduce(top[0:L, 1, :], eq[0:L, 1, :, :], AX.X, ALU.max).then_inc(s_first, 1)
                dve.wait_ge(s_first, q + 1)
                dve.tensor_tensor(oh_bf[0:L, :, bass.ds(2 * q, 2)].rearrange("p e b -> p b e"),
                                  rank8[0:L, :].unsqueeze(1).to_broadcast([L, 2, E]),
                                  top[0:L, 1, :].unsqueeze(2).to_broadcast([L, 2, E]), ALU.is_equal).then_inc(r_oh, 1)

            def row_max(i, g):
                dve.wait_ge(s_S, 2 * i + 1 + g)
                dve.tensor_reduce(nmax[0:L, g * HG:(g + 1) * HG],
                                  psS[0:L, g, 0:HG * L].rearrange("p (j m) -> p j m", m=L),
                                  AX.X, ALU.max, negate=True).then_inc(s_max, 1)

            stats1(1)
            k_copy(0, 0)
            dve.wait_ge(s_kzero, 1)
            key_blocks(0, 0, range(HG))
            v_copy(0, 0, 0)

            def step(r, i, p, u, t):
                par = u // 2
                even = u % 2 == 0
                rows_first = t is not None and B <= t <= B + 2

                def second_norm():
                    if has(t, 4):
                        b = i - 4
                        if u % 2 == 0 and (t is None or b >= 4):
                            dve.wait_ge(s_R1, p - 3)
                            dve.wait_ge(d_x2[par], 16 * (r - 1))
                        dve.wait_ge(s_r2, b + 1)
                        dve.tensor_scalar(x2[0:L, par, u % 2, :], res[0:L, bass.ds(b, 1), :].rearrange("p a d -> p (a d)"),
                                          mv2[0:L, u % 2, 0:1], rs2[0:L, u % 2:u % 2 + 1],
                                          ALU.subtract, ALU.mult).then_inc(s_x2, 1)

                def logits():
                    if even and (t is None or 0 <= p - 4 < NP):
                        dve.wait_ge(s_R2, p - 3)
                        dve.tensor_tensor(lg[0:L, :, :], psB[0:L, 1 - par, 0:2 * E].rearrange("p (k e) -> p k e", k=2),
                                          br_bc[0:L, :].unsqueeze(1).to_broadcast([L, 2, E]), ALU.add).then_inc(s_lg, 1)

                if has(t, 0):
                    row_max(i, 0)
                last_first = t == B + 3
                if last_first:
                    expert_first(p - 4)
                if not rows_first:
                    second_norm()
                if has(t, 0):
                    row_max(i, 1)
                if not rows_first:
                    logits()
                if has(t, 3):
                    b = i - 3
                    dve.wait_ge(s_P, b + 1)
                    h1 = res[0:L, bass.ds(b, 1), :].rearrange("p a d -> p (a d)")
                    dve.tensor_tensor(h1, psU[0:L, 0:128], h1, ALU.add).then_inc(s_h1, 1)
                if rows_first:
                    logits()
                if even and (t is None or p + 1 < NP):
                    k_copy(p + 1, par)
                if not even and (t is None or p + 1 < NP):
                    key_blocks(p + 1, 1 - par, range(HG // 2, HG))
                if has(t, 3):
                    dve.wait_ge(s_h1, b + 1)
                    dve.sem_inc(s_carry_v, 1)
                    dve.bn_stats(st2[0:L, :], h1).then_inc(s_st, 1)
                if not even and (t is None or 0 <= p - 4 < NP) and not last_first:
                    expert_first(p - 4)
                if even and (t is None or 0 <= p - 5 < NP):
                    expert_second(p - 5)
                if has(t, 3):
                    dve.wait_ge(s_st, b + 1)
                    dve.sem_inc(s_carry_v, 1)
                    dve.bn_aggr(mv2[0:L, (u + 1) % 2, :], st2[0:L, :]).then_inc(s_ag, 1)
                if rows_first:
                    second_norm()
                if not even and (t is None or p + 1 < NP):
                    v_copy(p + 1, 1 - par, par)
                if has(t, 0):
                    dve.wait_ge(s_exp, 2 * i + 2)
                    dve.reciprocal(rden[0:L, u % 2, :], den[0:L, u % 2, :]).then_inc(s_rd, 1)
                if t == B - 1:
                    dve.wait_ge(s_rd, B)
                    dve.tensor_tensor(P[0:L, u % 2, :, :], P[0:L, u % 2, :, :],
                                      rden[0:L, u % 2, :].unsqueeze(2).to_broadcast([L, H, L]), ALU.mult).then_inc(s_Pn_last, 1)
                if even and (t is None or p + 1 < NP):
                    key_blocks(p + 1, 1 - par, range(HG // 2))
                if even and (t is None or p + 2 < NP):
                    stats1(p + 2)

            attention_steps(dve, step)

            rl = [0]

            def rlink(ins):
                link(ins, r_chain, rl)

            def bc(ap, shape):
                return ap.to_broadcast([L] + shape)

            dve.wait_ge(r_cnt, 1)
            dve.wait_ge(r_zero, 2)
            cum = psS[0:L, 0, 0:E * B].rearrange("p (e b) -> p e b", e=E)
            rlink(dve.tensor_tensor_scan(scan[0:L, 1:1 + E * B], ones_f[0:L, :],
                                         psS[0:L, 1, 0:E * B], 0.0, ALU.mult, ALU.add))
            incl = scan[0:L, 1:1 + E * B].rearrange("p (e b) -> p e b", e=E)
            excl = scan[0:L, 0:E * B].rearrange("p (e b) -> p e b", e=E)
            ne, tiles, off = (cnt[0:L, n, :] for n in range(3))
            texc, tinc = tscan[0:L, 0:E], tscan[0:L, 1:1 + E]
            rlink(dve.tensor_tensor(ne, incl[:, :, B - 1], excl[:, :, 0], ALU.subtract))
            dve.tensor_tensor(posE[0:L, :, :], excl, cum, ALU.add).then_inc(r_chain, 1)
            rl[0] += 1
            rlink(dve.tensor_tensor(cmpt[0:L, :, :], bc(ne.unsqueeze(2), [E, B - 1]),
                                    bc(tile_starts[0:L, :].unsqueeze(1), [E, B - 1]), ALU.is_gt))
            rlink(dve.tensor_reduce(tiles, cmpt[0:L, :, :], AX.X, ALU.add))
            rlink(dve.tensor_tensor_scan(tinc, ones_f[0:L, 0:E], tiles, 0.0, ALU.mult, ALU.add))
            rlink(dve.scalar_tensor_tensor(out=off, in0=texc, scalar=128.0, in1=excl[:, :, 0], op0=ALU.mult, op1=ALU.subtract))
            rlink(dve.tensor_tensor(posE[0:L, :, :], posE[0:L, :, :], bc(off.unsqueeze(2), [E, B]), ALU.add))
            rlink(dve.tensor_tensor(posE[0:L, :, :], posE[0:L, :, :], oh_bf[0:L, :, :], ALU.mult))
            rlink(dve.tensor_reduce(pos[0:L, :], posE[0:L, :, :].rearrange("p e b -> p b e"), AX.X, ALU.add))
            rlink(dve.tensor_copy(pos_i[0:L, 0, :], pos[0:L, :]))
            dve.tensor_scalar(pos_i[0:L, 1, :], pos_i[0:L, 0, :], 7, None, ALU.arith_shift_right).then_inc(r_chain, 1)
            rl[0] += 1
            rlink(dve.tensor_scalar(pos_i[0:L, 2, :], pos_i[0:L, 0, :], 127, None, ALU.bitwise_and))
            dve.tensor_copy(pos_f[0:L, :, :], pos_i[0:L, 1:3, :]).then_inc(r_slot, 1)
            dve.wait_ge(r_slot, 1)
            dve.tensor_tensor(tile1h[0:L, :, :], bc(slot_iota[0:L, 0:NT].unsqueeze(1), [B, NT]),
                              bc(pos_f[0:L, 0, :].unsqueeze(2), [B, NT]), ALU.is_equal).then_inc(r_tile, 1)
            dve.wait_ge(r_tile, 1)
            rlink(dve.tensor_scalar(tok1h[0:L, :, 0, :], tile1h[0:L, :, :], part1[0:L, 0:1], None, ALU.mult))
            for b0, b1 in SLOT_GROUPS:
                dve.tensor_tensor(slot1h[0:L, b0:b1, :], bc(slot_iota[0:L, :].unsqueeze(1), [b1 - b0, 128]),
                                  bc(pos_f[0:L, 1, b0:b1].unsqueeze(2), [b1 - b0, 128]), ALU.is_equal).then_inc(r_1h, 1)
            dve.wait_ge(r_ids, 1)
            rlink(dve.tensor_copy(idf[:, :, :], psO[:, 0:2 * NT].rearrange("p (a t) -> p a t", a=2)))
            rlink(dve.scalar_tensor_tensor(out=idg[:, 0, :], in0=idf[:, 1, :], scalar=float(L), in1=idf[:, 0, :],
                                           op0=ALU.mult, op1=ALU.add))
            dve.tensor_scalar(idx[:, 0, :], idg[:, 0, :], -1.0, 0.0, ALU.add, ALU.max).then_inc(r_idx, 1)
            rlink(dve.tensor_tensor(eidc[0:L, :, :], bc(tinc.unsqueeze(1), [NT, E]),
                                    bc(slot_iota[0:L, 0:NT].unsqueeze(2), [NT, E]), ALU.is_le))
            rlink(dve.tensor_reduce(eidf[0:L, :], eidc[0:L, :, :], AX.X, ALU.add))
            dve.tensor_scalar(eid[0:L, :], eidf[0:L, :], float(E - 1), None, ALU.min).then_inc(r_eid, 1)
            rlink(dve.tensor_scalar(idf[:, 0, :], idf[:, 0, :], 0.0, float(NOROW), ALU.is_equal, ALU.mult))
            rlink(dve.scalar_tensor_tensor(out=idg[:, 1, :], in0=idg[:, 0, :], scalar=-1.0, in1=idf[:, 0, :],
                                           op0=ALU.add, op1=ALU.add))
            rlink(dve.tensor_copy(idx[:, 1, :], idg[:, 1, :]))
            dve.wait_ge(r_idx, 1)
            dve.wait_ge(r_eid, 1)

            def gather_rows(s, u):
                dve.tensor_copy(gidx[:, u:u + 1], idx[:, 0, bass.ds(s, 1)]).then_inc(f_gi, 1)

            dve.wait_ge(l_ffn, 48)
            dve.wait_ge(f_b1T, 1)
            expert = {}

            def load_expert(s):
                return dve.value_load(eid[0:1, bass.ds(s, 1)], min_val=0, max_val=E - 1)

            def step(s, r, u, t):
                if t is None or t < NT:
                    if u == 1 or t == 0:
                        expert[u] = load_expert(s)
                    e = expert[u]
                    dve.wait_ge(f_L1, s + 1)
                    if t is None or t >= 2:
                        dve.wait_ge(f_hT, s - 1)
                    dve.tensor_tensor(hpre[:, u % 2, :].rearrange("p (c n) -> p c n", c=FC),
                                      psS[:, u % 2, :].rearrange("p (c n) -> p c n", c=FC),
                                      b1T[:, bass.ds(e * FC, FC)].unsqueeze(2).to_broadcast([128, FC, 128]),
                                      ALU.add).then_inc(f_hp, 1)
                    if u > 0 and (t is None or t + 1 < NT):
                        expert[(u + 1) % RING] = load_expert(s + 1)
                    if t is None or t + RING < NT:
                        gather_rows(s + RING, u)
                    dve.tensor_tensor(resid[:, u, :], xg[:, u, D:2 * D], b2_bc[:, bass.ds(e * D, D)],
                                      ALU.add).then_inc(f_rs, 1)
                if has(t, 1, NT):
                    v = (u - 1) % RING
                    if t is None or t - 1 >= RING:
                        dve.wait_ge(f_sca[v], 16 * (r + (u - 1) // RING))
                    dve.tensor_copy(sidx[:, v:v + 1], idx[:, 1, bass.ds(s - 1, 1)]).then_inc(f_si, 1)
                    dve.wait_ge(f_L2, s)
                    dve.wait_ge(f_rs, s)
                    dve.wait_ge(f_si, s)
                    dve.tensor_tensor(y_out[:, v, :], (psU if u % 2 == 0 else psO)[:, 0:D], resid[:, v, :],
                                      ALU.add).then_inc(f_y, 1)

            ffn_steps(dve, step, NT + 1)

        @block.tensor
        def _(pe):
            pe.wait_ge(s_const, N_CONST)
            pe.wait_ge(l_tokW, 16)
            pe.transpose(banks[0][0:CTX * DI, 0:128], tokW_sb[:, :], ident[:, :]).then_inc(a_wt, 1)
            pe.wait_ge(l_x, 16)
            for t in range(8):
                if t == 2:
                    pe.wait_ge(a_keyed, 1)
                    pe.transpose(banks[0][:, 128:128 + EF], key[:, :], ident[0:EF, 0:EF]).then_inc(a_keyT, 1)
                if t == 5:
                    pe.wait_ge(l_proj, 64)
                    pe.wait_ge(a_operm, 1)
                    for n in range(4):
                        ins = pe.transpose(banks[1][:, n * D:(n + 1) * D], proj_in[:, n, :] if n < 3 else o_perm[:, :],
                                           ident[:, :])
                    ins.then_inc(a_w4, 1)
                if t == 6:
                    pe.wait_ge(l_qkb, 32)
                    for n in range(4):
                        ins = pe.matmul(banks[2][:, n:n + 1], qk_row[0:1, n // 2, n % 2 * 128:n % 2 * 128 + 128],
                                        ident[0:1, 0:1], start=True, stop=True)
                    ins.then_inc(a_bias, 1)
                if t >= 5:
                    pe.wait_ge(a_wts, (1, 5, 7)[t - 5])
                bank = banks[(3 + t) % 8]
                for i in range(4 * t, min(4 * t + 4, SEG + 1)):
                    ins = pe.transpose(bank[0:CTX * DI, (i - 4 * t) * 128:(i - 4 * t + 1) * 128],
                                       xs[:, i * DI:(i + CTX) * DI], ident[:, :])
                ins.then_inc(a_xt, 1)
            pe.wait_ge(a_pat, 9)
            for c in range(NCH):
                pe.matmul(banks[(3 + c) % 8][:, 0:CH], tokWT[0:CTX * DI, :], patT[0:CTX * DI, c * CH:(c + 1) * CH],
                          start=True, stop=True).then_inc(a_y, 1)
            pe.wait_ge(a_relu, 1)
            pe.wait_ge(s_power, 3)
            for f in range(EF):
                if f % 8 == 0:
                    pe.wait_ge(a_1h, f // 8 + 1)
                ins = pe.matmul(banks[3][0:L, f * EG:(f + 1) * EG], target1h[:, f, :], power_bf[:, :], start=True, stop=True)
            ins.then_inc(a_bits, 1)

            def transpose_h0(p, bank):
                pe.wait_ge(s_h0T, p + 1)
                for k in range(2):
                    ins = pe.transpose(bank[0:L, k * D:(k + 1) * D], h0T[:, k * L:(k + 1) * L], ident[:, :])
                ins.then_inc(s_T1, 1)

            def transpose_xn(p, bank):
                pe.wait_ge(s_xn, 2 * p + 2)
                for k in range(2):
                    ins = pe.transpose(psB[:, bank, k * L:(k + 1) * L], xn[0:L, k, :], ident[0:L, 0:L])
                ins.then_inc(s_T2, 1)

            def project(p, par, bank, w, done):
                pe.wait_ge(s_xT, p + 1)
                for g in range(2):
                    ins = pe.matmul(psB[:, bank, g * PL:(g + 1) * PL], w[:, g * 128:(g + 1) * 128], xT[:, par, :],
                                    start=True, stop=True)
                ins.then_inc(done, 1)

            def values(p, par, bank):
                for k in range(2):
                    ins = pe.matmul(psB[0:L, bank, k * D:(k + 1) * D], xT[:, par, k * L:(k + 1) * L], vwT[:, :],
                                    start=True, stop=True)
                ins.then_inc(s_V, 1)

            pe.wait_ge(a_relu, NCH)
            transpose_h0(0, psB[:, 0, :])
            transpose_xn(0, 1)
            transpose_h0(1, psT[:, 0, :])
            pe.wait_ge(a_bpad, 1)
            for g in range(2):
                ins = pe.transpose(banks[5][:, g * 128:g * 128 + L], bias_pad[0:L, g * 128:(g + 1) * 128], ident[0:L, 0:L])
            ins.then_inc(a_biasT, 1)
            project(0, 0, 0, kwT, s_k)
            project(0, 0, 1, qwT, s_q)
            pe.wait_ge(s_kT, 1)
            values(0, 0, 0)

            def scores(i, u, g, t):
                if t is None or t >= 1:
                    pe.wait_ge(s_exp, 2 * i - 1 + g)
                pe.matmul(psS[0:L, g, 0:HG * L], qT[:, u // 2, g, u % 2 * L:u % 2 * L + L],
                          kbd[:, u, g, :], start=True, stop=True).then_inc(s_S, 1)

            def step(r, i, p, u, t):
                par = u // 2
                even = u % 2 == 0
                if has(t, 0):
                    if even:
                        pe.wait_ge(s_kbd, 2 * p + 2)
                        pe.wait_ge(s_qs, 2 * p + 2)
                    scores(i, u, 0, t)
                if even and (t is None or p + 1 < NP):
                    if t is None or p >= 4:
                        pe.wait_ge(s_x2T, p - 3)
                    if t == 0:
                        pe.wait_ge(s_Vs, 1)
                    transpose_xn(p + 1, par)
                if has(t, 0):
                    scores(i, u, 1, t)

                def transpose_probabilities():
                    if has(t, 1):
                        if t == B:
                            pe.wait_ge(s_Pn_last, 1)
                        else:
                            pe.wait_ge(s_Pn, i)
                        if t is None or t >= 2:
                            pe.wait_ge(s_PT, i - 1)
                        for h in range(H):
                            ins = pe.transpose(psT[0:L, h // HG, h % HG * L:(h % HG + 1) * L], P[0:L, (u + 1) % 2, h, :],
                                               ident[0:L, 0:L])
                        ins.then_inc(s_T, 1)

                if t == B:
                    transpose_probabilities()
                if has(t, 3):
                    pe.wait_ge(s_oT, i - 2)
                    if t is None or t >= 4:
                        pe.wait_ge(s_h1, i - 3)
                    pe.matmul(psU[0:L, 0:128], oT[:, :], owT[:, :], start=True, stop=True).then_inc(s_P, 1)
                if even and (t is None or 0 <= p - 4 < NP):
                    pe.wait_ge(s_x2T, p - 3)
                    pe.wait_ge(s_Vs, p + 1 if t is None else min(p + 1, NP))
                    for k in range(2):
                        ins = pe.matmul(psB[0:L, 1 - par, k * E:(k + 1) * E], x2T[:, k * L:(k + 1) * L],
                                        Wr_sb[:, :], start=True, stop=True)
                    ins.then_inc(s_R2, 1)
                if even and (t is None or p + 1 < NP):
                    project(p + 1, 1 - par, par, kwT, s_k)
                if not even and (t is None or 0 <= p - 3 < NP):
                    pe.wait_ge(s_x2, 2 * p - 4)
                    pe.wait_ge(s_h0k, p + 3 if t is None else min(p + 3, NP))
                    if t is None or p >= 4:
                        pe.wait_ge(s_lg, p - 3)
                    for k in range(2):
                        ins = pe.transpose(psB[:, 1 - par, k * L:(k + 1) * L], x2[0:L, 1 - par, k, :], ident[0:L, 0:L])
                    ins.then_inc(s_R1, 1)
                if t != B:
                    transpose_probabilities()
                if even and (t is None or p + 2 < NP):
                    pe.wait_ge(s_Vs, p + 1)
                    if t is None or p >= 4:
                        pe.wait_ge(s_lg, p - 3)
                    transpose_h0(p + 2, psB[:, 1 - par, :])
                if not even and (t is None or p + 1 < NP):
                    pe.wait_ge(s_qs, 2 * p + 4)
                    values(p + 1, 1 - par, par)
                if has(t, 2):
                    pe.wait_ge(s_PT, i - 1)
                    if t is None or t >= 3:
                        pe.wait_ge(s_oT, i - 2)
                    pe.wait_ge(s_Vs, p)
                    for h in range(H):
                        j = h % HG
                        ins = pe.matmul(psO[j * HB:(j + 1) * HB, 0:L],
                                        V[0:L, (par + 1) % 2, u % 2, h * HB:(h + 1) * HB],
                                        PT[0:L, u % 2, h // HG, j * L:(j + 1) * L], start=(h < HG), stop=(h >= HG))
                    ins.then_inc(s_PV, 1)
                if even and (t is None or p + 1 < NP):
                    pe.wait_ge(s_kT, p + 2)
                    project(p + 1, 1 - par, par, qwT, s_q)

            pe.wait_ge(l_rows, 16 * N_ROWS)
            attention_steps(pe, step)

            pe.wait_ge(r_oh, NP)
            pe.matmul(psS[0:L, 0, 0:E * B], before[0:L, 0:L], oh_bf[0:L, :, :].rearrange("p e b -> p (e b)"),
                      start=True, stop=True)
            pe.matmul(psS[0:L, 1, 0:E * B], ones_bf[0:L, 0:L], oh_bf[0:L, :, :].rearrange("p e b -> p (e b)"),
                      start=True, stop=True).then_inc(r_cnt, 1)
            pe.wait_ge(l_ffn, 48)
            pe.wait_ge(s_PT, B)
            pe.transpose(psT[:, 0, 0:E * FC], b1_in[:, :], ident[0:E * FC, 0:E * FC]).then_inc(f_b1, 1)
            pe.wait_ge(r_seq, 1)
            groups = [(*g, r_1h, n + 1) for n, g in enumerate(SLOT_GROUPS)]
            groups.insert(-1, (ACT_SEQ, B, r_1ha, B - ACT_SEQ + 2))
            for g, (b0, b1, made, count) in enumerate(groups):
                pe.wait_ge(made, count)
                if b0 >= B // 2:
                    pe.wait_ge(r_seq, 2)
                for b in range(b0, b1):
                    ins = pe.matmul(psO[:, 0:2 * NT], slot1h[0:L, b, :], tok1h[0:L, b, :, :].rearrange("p a t -> p (a t)"),
                                    start=(b == 0), stop=(g == len(groups) - 1 and b == b1 - 1))
            ins.then_inc(r_ids, 1)

            def transpose_rows(s, r, u, t):
                pe.wait_ge(f_gat[u], 16 * (r + 1))
                if t is None or t >= 2:
                    pe.wait_ge(f_xT, s - 1)
                pe.transpose(psB[:, u % 2, 0:128], xg[:, u, 0:D], ident[:, :]).then_inc(f_Xt, 1)

            pe.wait_ge(r_idx, 1)
            pe.wait_ge(r_eid, 1)
            pe.wait_ge(l_ffn, 48)
            transpose_rows(0, 0, 0, 0)

            def load_expert(s):
                return pe.value_load(eid[0:1, bass.ds(s, 1)], min_val=0, max_val=E - 1)

            def step(s, r, u, t):
                if t is None or t < NT:
                    if t is None or t + 1 < NT:
                        transpose_rows(s + 1, r + (u + 1) // RING, (u + 1) % RING, None if t is None else t + 1)
                    pe.wait_ge(f_xT, s + 1)
                    pe.wait_ge(f_w1, s + 1)
                    if t is None or t >= 2:
                        pe.wait_ge(f_hp, s - 1)
                    for c in range(FC):
                        ins = pe.matmul(psS[:, u % 2, c * 128:(c + 1) * 128],
                                        W1_tile[:, u % 2, c * 128:(c + 1) * 128], xgT[:, u % 2, :],
                                        start=True, stop=True)
                    ins.then_inc(f_L1, 1)
                if has(t, 1, NT):
                    e = load_expert(s - 1)
                    pe.wait_ge(f_hT, s)
                    if t is None or t >= 3:
                        pe.wait_ge(f_y, s - 2)
                    for c in range(FC):
                        ins = pe.matmul((psU if u % 2 == 0 else psO)[:, 0:D], hT[:, (u + 1) % 2, c * 128:(c + 1) * 128],
                                        W2_sb[:, bass.ds(e * F + c * D, D)], start=(c == 0), stop=(c == FC - 1))
                    ins.then_inc(f_L2, 1)

            ffn_steps(pe, step, NT + 1)


_INS = ['x', 'L0_tok_W', 'L0_tok_b', 'L0_tok_gamma', 'L0_tok_beta', 'L0_attn_edge_index', 'L0_attn_edge_attr',
        'L0_attn_q_w', 'L0_attn_q_b', 'L0_attn_k_w', 'L0_attn_k_b', 'L0_attn_v_w', 'L0_attn_v_b', 'L0_attn_o_w',
        'L0_attn_o_b', 'L0_attn_eb_w', 'L0_attn_eb_b', 'L0_ffn_Wr', 'L0_ffn_br', 'L0_ffn_W1', 'L0_ffn_b1',
        'L0_ffn_W2', 'L0_ffn_b2']


def kernel(**inputs):
    import concourse.bacc as bacc
    from concourse.bass_utils import run_bass_kernel_spmd

    nc = bacc.Bacc("TRN2", target_bir_lowering=False, num_devices=1)
    arrays, args = {}, []
    for name in _INS:
        a = np.ascontiguousarray(inputs[name])
        arrays[f"in_{name}"] = a
        args.append(nc.dram_tensor(f"in_{name}", a.shape, mybir.dt.from_np(a.dtype), kind="ExternalInput").ap())
    out = nc.dram_tensor("out_0", (N, D), F32, kind="ExternalOutput").ap()
    build(nc, *args, out)
    r = run_bass_kernel_spmd(nc, [arrays], core_ids=[0])
    return r.results[0]["out_0"].reshape(B, L, D)
```
